# Optimizing a Trainium2 kernel written in Bass

```python
import numpy as np
import jax
import jax.numpy as jnp

def _softmax(x, axis=-1):
    return jax.nn.softmax(x, axis=axis)

def _gelu(x):
    return jax.nn.gelu(x, approximate=True)

def _silu(x):
    return jax.nn.silu(x)

def _sigmoid(x):
    return jax.nn.sigmoid(x)

def _layernorm(x, axis=-1, eps=1e-05):
    m = jnp.mean(x, axis=axis, keepdims=True)
    v = jnp.var(x, axis=axis, keepdims=True)
    return (x - m) / jnp.sqrt(v + eps)

def _scatter_add(tgt, idx, src, axis=0):
    return tgt.at[idx].add(src)

def _segment_sum(src, seg, n):
    return jax.ops.segment_sum(src, seg, n)
kernel_name = 'mk_sandwich_d4_jaxref_r8_ea86f2'

def setup_inputs(seed: int=0):
    np.random.seed(seed)
    _w = jnp.asarray

    def _L0_attn_setup():
        import jax, jax.numpy as jnp
        import numpy as np
        DIM = 128
        NUM_HEADS = 16
        HEAD_DIM = DIM // NUM_HEADS
        WINDOW = 32
        B, L = (2, 256)
        EPS = 1e-05
        INIT_STD = 0.01

        def rmsnorm(x, w):
            x = jnp.clip(x, -10000.0, 10000.0)
            rms = jnp.sqrt(jnp.maximum(jnp.mean(x * x, axis=-1, keepdims=True), EPS) + EPS)
            out = x / rms * w
            return jnp.where(jnp.isfinite(out), out, jnp.zeros_like(out))
        key = jax.random.key(seed)
        ks = jax.random.split(key, 6)
        return {'x': jax.random.normal(ks[0], (B, L, DIM), dtype=jnp.float32), 'wq_w': jax.random.normal(ks[1], (DIM, DIM), dtype=jnp.float32) * INIT_STD, 'wq_b': jnp.zeros((DIM,), jnp.float32), 'wk_w': jax.random.normal(ks[2], (DIM, DIM), dtype=jnp.float32) * INIT_STD, 'wk_b': jnp.zeros((DIM,), jnp.float32), 'wv_w': jax.random.normal(ks[3], (DIM, DIM), dtype=jnp.float32) * INIT_STD, 'wv_b': jnp.zeros((DIM,), jnp.float32), 'wo_w': jax.random.normal(ks[4], (DIM, DIM), dtype=jnp.float32) * INIT_STD, 'wo_b': jnp.zeros((DIM,), jnp.float32), 'qn_w': jnp.ones((HEAD_DIM,), jnp.float32), 'kn_w': jnp.ones((HEAD_DIM,), jnp.float32)}
    _L0_attn_in = _L0_attn_setup()

    def _L0_ffn_setup():
        import jax, jax.numpy as jnp
        import numpy as np
        D_IN, D_HID = (128, 512)

        def _ternary(key, shape):
            return jax.random.randint(key, shape, -1, 2).astype(jnp.float32)

        def _tlin(x, w, s):
            return jnp.einsum('bsi,oi->bso', x, w) * s
        key = jax.random.key(seed)
        ks = jax.random.split(key, 12)
        inv = lambda fan: 1.0 / np.sqrt(fan).astype(np.float32)
        return {'x': jax.random.normal(ks[0], (4, 256, D_IN), dtype=jnp.float32), 'w1_w': _ternary(ks[1], (D_HID, D_IN)), 'w1_s': jax.random.uniform(ks[2], (D_HID,), dtype=jnp.float32) * inv(D_IN), 'w2_w': _ternary(ks[3], (D_HID, D_IN)), 'w2_s': jax.random.uniform(ks[4], (D_HID,), dtype=jnp.float32) * inv(D_IN), 'h1_w': _ternary(ks[5], (D_HID, D_HID)), 'h1_s': jax.random.uniform(ks[6], (D_HID,), dtype=jnp.float32) * inv(D_HID), 'h2_w': _ternary(ks[7], (D_HID, D_HID)), 'h2_s': jax.random.uniform(ks[8], (D_HID,), dtype=jnp.float32) * inv(D_HID), 'w3_w': _ternary(ks[9], (D_IN, D_HID)), 'w3_s': jax.random.uniform(ks[10], (D_IN,), dtype=jnp.float32) * inv(D_HID)}
    _L0_ffn_in = _L0_ffn_setup()

    def _L1_attn_setup():
        import jax, jax.numpy as jnp
        import numpy as np
        import math
        DIM = 128
        ATTN_DIM = 128
        B, S = (2, 512)
        key = jax.random.key(seed)
        k1, k2, k3 = jax.random.split(key, 3)
        x = jax.random.normal(k1, (B, S, DIM), dtype=jnp.float32)
        W_qkv = jax.random.normal(k2, (3 * ATTN_DIM, DIM), dtype=jnp.float32) * (1.0 / math.sqrt(DIM))
        b_qkv = jax.random.normal(k3, (3 * ATTN_DIM,), dtype=jnp.float32) * 0.01
        return {'x': x, 'W_qkv': W_qkv, 'b_qkv': b_qkv}
    _L1_attn_in = _L1_attn_setup()

    def _L1_ffn_setup():
        import jax, jax.numpy as jnp
        import numpy as np
        E = 32
        K = 4
        H = 128
        F = 128
        LIMIT = 7.0
        ALPHA = 1.702
        EPS = 1e-05

        def _rmsnorm(x, scale):
            t = x * jax.lax.rsqrt(jnp.mean(x * x, axis=-1, keepdims=True) + EPS)
            return t * scale

        def _swiglu(h):
            glu = jnp.minimum(h[..., ::2], LIMIT)
            lin = jnp.clip(h[..., 1::2], -LIMIT, LIMIT)
            return glu * jax.nn.sigmoid(ALPHA * glu) * (lin + 1.0)
        key = jax.random.key(seed)
        ks = jax.random.split(key, 8)
        B, S = (1, 128)
        x = jax.random.normal(ks[0], (B, S, H), dtype=jnp.float32)
        norm_scale = jnp.ones((H,), dtype=jnp.float32)
        gate_w = jax.random.normal(ks[1], (E, H), dtype=jnp.float32) * 0.02
        gate_b = jnp.zeros((E,), dtype=jnp.float32)
        w1 = jax.random.normal(ks[2], (E, 2 * F, H), dtype=jnp.float32) * 0.02
        b1 = jnp.zeros((E, 2 * F), dtype=jnp.float32)
        w2 = jax.random.normal(ks[3], (E, H, F), dtype=jnp.float32) * 0.02
        b2 = jnp.zeros((E, H), dtype=jnp.float32)
        return {'x': x, 'norm_scale': norm_scale, 'gate_w': gate_w, 'gate_b': gate_b, 'w1': w1, 'b1': b1, 'w2': w2, 'b2': b2}
    _L1_ffn_in = _L1_ffn_setup()

    def _L2_attn_setup():
        import jax, jax.numpy as jnp
        import numpy as np
        D, H, DK, DV, F, R = (128, 16, 64, 64, 512, 64)
        B, T = (4, 256)
        KCONV = 4
        EPS = 1e-06

        def rmsnorm(x, w):
            return x * jax.lax.rsqrt(jnp.mean(x * x, axis=-1, keepdims=True) + EPS) * w

        def _reference_tuple_inner(x, norm_in_w, conv_w, conv_b, q_w, k_w, v_w, out_w, alpha_w, alpha_b, beta_w, beta_b, head_norm_w, u1_w, u1_b, u2_w, u2_b, ff_norm_w, ff_w1, ff_w3, ff_w2):
            bsz, seq, _ = x.shape
            h = rmsnorm(x, norm_in_w)
            hc = jax.lax.conv_general_dilated(h.transpose(0, 2, 1), conv_w, (1,), [(KCONV - 1, 0)], dimension_numbers=('NCH', 'OIH', 'NCH'), feature_group_count=D)
            h = jax.nn.silu((hc + conv_b[None, :, None]).transpose(0, 2, 1))
            q = (h @ q_w).reshape(bsz, seq, H, DK)
            k = (h @ k_w).reshape(bsz, seq, H, DK)
            v = (h @ v_w).reshape(bsz, seq, H, DV)
            q = q / (jnp.linalg.norm(q, axis=-1, keepdims=True) + EPS)
            k = k / (jnp.linalg.norm(k, axis=-1, keepdims=True) + EPS)
            alpha = jax.nn.sigmoid(h @ alpha_w + alpha_b).reshape(bsz, seq, H, DK)
            beta = jax.nn.sigmoid(h @ beta_w + beta_b)

            def step(s, inp):
                qt, kt, vt, at, bt = inp
                s = s * at[..., None]
                u = jnp.einsum('bhd,bhdv->bhv', kt, s)
                s = s + bt[..., None, None] * (kt[..., None] * (vt - u)[..., None, :])
                out = jnp.einsum('bhdv,bhd->bhv', s, qt)
                return (s, out)
            tm = lambda a: jnp.swapaxes(a, 0, 1)
            s0 = jnp.zeros((bsz, H, DK, DV), x.dtype)
            s_final, outs = jax.lax.scan(step, s0, (tm(q), tm(k), tm(v), tm(alpha), tm(beta)))
            y = tm(outs)
            y = y * jax.lax.rsqrt(jnp.mean(y * y, axis=-1, keepdims=True) + EPS) * head_norm_w
            y = y.reshape(bsz, seq, H * DV)
            gate = jax.nn.sigmoid(jax.nn.silu(x @ u1_w + u1_b) @ u2_w + u2_b)
            y = x + y @ out_w * gate
            y2 = rmsnorm(y, ff_norm_w)
            y = y + jax.nn.silu(y2 @ ff_w1) * (y2 @ ff_w3) @ ff_w2
            return (y, s_final)
        key = jax.random.key(seed)
        ks = jax.random.split(key, 16)
        n = lambda k, shape: jax.random.normal(k, shape, jnp.float32) * 0.02
        return dict(x=jax.random.normal(ks[0], (B, T, D), jnp.float32), norm_in_w=jnp.ones((D,), jnp.float32), conv_w=n(ks[1], (D, 1, KCONV)), conv_b=jnp.zeros((D,), jnp.float32), q_w=n(ks[2], (D, H * DK)), k_w=n(ks[3], (D, H * DK)), v_w=n(ks[4], (D, H * DV)), out_w=n(ks[5], (H * DV, D)), alpha_w=n(ks[6], (D, H * DK)), alpha_b=jnp.zeros((H * DK,), jnp.float32), beta_w=n(ks[7], (D, H)), beta_b=jnp.zeros((H,), jnp.float32), head_norm_w=jnp.ones((H, DV), jnp.float32), u1_w=n(ks[8], (D, R)), u1_b=jnp.zeros((R,), jnp.float32), u2_w=n(ks[9], (R, D)), u2_b=jnp.zeros((D,), jnp.float32), ff_norm_w=jnp.ones((D,), jnp.float32), ff_w1=n(ks[10], (D, F)), ff_w3=n(ks[11], (D, F)), ff_w2=n(ks[12], (F, D)))
    _L2_attn_in = _L2_attn_setup()

    def _L2_ffn_setup():
        import jax, jax.numpy as jnp
        import numpy as np
        E = 8
        K = 2
        key = jax.random.key(seed)
        ks = jax.random.split(key, 6)
        B, S, D, F = (4, 256, 128, 512)
        s_d = 1.0 / np.sqrt(D).astype(np.float32)
        s_f = 1.0 / np.sqrt(F).astype(np.float32)
        return {'x': jax.random.normal(ks[0], (B, S, D), jnp.float32), 'ln_w': jnp.ones((D,), jnp.float32), 'Wg': jax.random.normal(ks[1], (D, E), jnp.float32) * s_d, 'bg': jnp.zeros((E,), jnp.float32), 'W1a': jax.random.normal(ks[2], (E, D, F), jnp.float32) * s_d, 'b1a': jnp.zeros((E, F), jnp.float32), 'W1b': jax.random.normal(ks[3], (E, D, F), jnp.float32) * s_d, 'b1b': jnp.zeros((E, F), jnp.float32), 'W2': jax.random.normal(ks[4], (E, F, D), jnp.float32) * s_f, 'b2': jnp.zeros((E, D), jnp.float32)}
    _L2_ffn_in = _L2_ffn_setup()

    def _L3_attn_setup():
        import jax, jax.numpy as jnp
        import numpy as np
        D_MODEL = 128
        N_HEADS = 16
        D_LATENT = 32
        HEAD_DIM = D_MODEL // N_HEADS

        def apply_rope(x):
            B, T, H, D = x.shape
            inv_freq = 1.0 / 10000.0 ** (jnp.arange(0, D, 2, dtype=jnp.float32) / D)
            t = jnp.arange(T, dtype=jnp.float32)
            freqs = t[:, None] * inv_freq[None, :]
            sin_f = jnp.sin(freqs)[None, :, None, :]
            cos_f = jnp.cos(freqs)[None, :, None, :]
            x1, x2 = jnp.split(x, 2, axis=-1)
            return jnp.concatenate([x1 * cos_f - x2 * sin_f, x1 * sin_f + x2 * cos_f], axis=-1)
        key = jax.random.key(seed)
        ks = jax.random.split(key, 10)
        B, T = (4, 512)
        s = lambda fan_in: 1.0 / np.sqrt(fan_in)
        return {'x': jax.random.normal(ks[0], (B, T, D_MODEL), dtype=jnp.float32), 'Wq': jax.random.normal(ks[1], (D_MODEL, D_MODEL), dtype=jnp.float32) * s(D_MODEL), 'bq': jnp.zeros((D_MODEL,), jnp.float32), 'Wdown': jax.random.normal(ks[2], (D_MODEL, D_LATENT), dtype=jnp.float32) * s(D_MODEL), 'bdown': jnp.zeros((D_LATENT,), jnp.float32), 'Wup': jax.random.normal(ks[3], (D_LATENT, 2 * D_MODEL), dtype=jnp.float32) * s(D_LATENT), 'bup': jnp.zeros((2 * D_MODEL,), jnp.float32), 'Wout': jax.random.normal(ks[4], (D_MODEL, D_MODEL), dtype=jnp.float32) * s(D_MODEL), 'bout': jnp.zeros((D_MODEL,), jnp.float32)}
    _L3_attn_in = _L3_attn_setup()

    def _L3_ffn_setup():
        import jax, jax.numpy as jnp
        import numpy as np
        E, K, D, F = (8, 2, 128, 512)
        EPS = 1e-06
        B, S = (2, 128)
        key = jax.random.key(seed)
        ks = jax.random.split(key, 6)
        s_in = 1.0 / np.sqrt(D)
        s_mid = 1.0 / np.sqrt(F)
        return {'x': jax.random.normal(ks[0], (B, S, D), dtype=jnp.float32), 'Wg': jax.random.normal(ks[1], (D, E), dtype=jnp.float32) * s_in, 'gamma': jnp.ones((E, D), dtype=jnp.float32), 'beta': jnp.zeros((E, D), dtype=jnp.float32), 'W1': jax.random.normal(ks[2], (E, D, F), dtype=jnp.float32) * s_in, 'b1': jnp.zeros((E, F), dtype=jnp.float32), 'W2': jax.random.normal(ks[3], (E, F, D), dtype=jnp.float32) * s_mid, 'b2': jnp.zeros((E, D), dtype=jnp.float32)}
    _L3_ffn_in = _L3_ffn_setup()
    _d = {'L0_attn_x': _L0_attn_in['x'], 'L0_attn_wq_w': _L0_attn_in['wq_w'], 'L0_attn_wq_b': _L0_attn_in['wq_b'], 'L0_attn_wk_w': _L0_attn_in['wk_w'], 'L0_attn_wk_b': _L0_attn_in['wk_b'], 'L0_attn_wv_w': _L0_attn_in['wv_w'], 'L0_attn_wv_b': _L0_attn_in['wv_b'], 'L0_attn_wo_w': _L0_attn_in['wo_w'], 'L0_attn_wo_b': _L0_attn_in['wo_b'], 'L0_attn_qn_w': _L0_attn_in['qn_w'], 'L0_attn_kn_w': _L0_attn_in['kn_w'], 'L0_ffn_w1_w': _L0_ffn_in['w1_w'], 'L0_ffn_w1_s': _L0_ffn_in['w1_s'], 'L0_ffn_w2_w': _L0_ffn_in['w2_w'], 'L0_ffn_w2_s': _L0_ffn_in['w2_s'], 'L0_ffn_h1_w': _L0_ffn_in['h1_w'], 'L0_ffn_h1_s': _L0_ffn_in['h1_s'], 'L0_ffn_h2_w': _L0_ffn_in['h2_w'], 'L0_ffn_h2_s': _L0_ffn_in['h2_s'], 'L0_ffn_w3_w': _L0_ffn_in['w3_w'], 'L0_ffn_w3_s': _L0_ffn_in['w3_s'], 'L1_attn_W_qkv': _L1_attn_in['W_qkv'], 'L1_attn_b_qkv': _L1_attn_in['b_qkv'], 'L1_ffn_norm_scale': _L1_ffn_in['norm_scale'], 'L1_ffn_gate_w': _L1_ffn_in['gate_w'], 'L1_ffn_gate_b': _L1_ffn_in['gate_b'], 'L1_ffn_w1': _L1_ffn_in['w1'], 'L1_ffn_b1': _L1_ffn_in['b1'], 'L1_ffn_w2': _L1_ffn_in['w2'], 'L1_ffn_b2': _L1_ffn_in['b2'], 'L2_attn_norm_in_w': _L2_attn_in['norm_in_w'], 'L2_attn_conv_w': _L2_attn_in['conv_w'], 'L2_attn_conv_b': _L2_attn_in['conv_b'], 'L2_attn_q_w': _L2_attn_in['q_w'], 'L2_attn_k_w': _L2_attn_in['k_w'], 'L2_attn_v_w': _L2_attn_in['v_w'], 'L2_attn_out_w': _L2_attn_in['out_w'], 'L2_attn_alpha_w': _L2_attn_in['alpha_w'], 'L2_attn_alpha_b': _L2_attn_in['alpha_b'], 'L2_attn_beta_w': _L2_attn_in['beta_w'], 'L2_attn_beta_b': _L2_attn_in['beta_b'], 'L2_attn_head_norm_w': _L2_attn_in['head_norm_w'], 'L2_attn_u1_w': _L2_attn_in['u1_w'], 'L2_attn_u1_b': _L2_attn_in['u1_b'], 'L2_attn_u2_w': _L2_attn_in['u2_w'], 'L2_attn_u2_b': _L2_attn_in['u2_b'], 'L2_attn_ff_norm_w': _L2_attn_in['ff_norm_w'], 'L2_attn_ff_w1': _L2_attn_in['ff_w1'], 'L2_attn_ff_w3': _L2_attn_in['ff_w3'], 'L2_attn_ff_w2': _L2_attn_in['ff_w2'], 'L2_ffn_ln_w': _L2_ffn_in['ln_w'], 'L2_ffn_Wg': _L2_ffn_in['Wg'], 'L2_ffn_bg': _L2_ffn_in['bg'], 'L2_ffn_W1a': _L2_ffn_in['W1a'], 'L2_ffn_b1a': _L2_ffn_in['b1a'], 'L2_ffn_W1b': _L2_ffn_in['W1b'], 'L2_ffn_b1b': _L2_ffn_in['b1b'], 'L2_ffn_W2': _L2_ffn_in['W2'], 'L2_ffn_b2': _L2_ffn_in['b2'], 'L3_attn_Wq': _L3_attn_in['Wq'], 'L3_attn_bq': _L3_attn_in['bq'], 'L3_attn_Wdown': _L3_attn_in['Wdown'], 'L3_attn_bdown': _L3_attn_in['bdown'], 'L3_attn_Wup': _L3_attn_in['Wup'], 'L3_attn_bup': _L3_attn_in['bup'], 'L3_attn_Wout': _L3_attn_in['Wout'], 'L3_attn_bout': _L3_attn_in['bout'], 'L3_ffn_Wg': _L3_ffn_in['Wg'], 'L3_ffn_gamma': _L3_ffn_in['gamma'], 'L3_ffn_beta': _L3_ffn_in['beta'], 'L3_ffn_W1': _L3_ffn_in['W1'], 'L3_ffn_b1': _L3_ffn_in['b1'], 'L3_ffn_W2': _L3_ffn_in['W2'], 'L3_ffn_b2': _L3_ffn_in['b2']}
    _x0 = _d['L0_attn_x']
    _d['L0_attn_x'] = jax.random.normal(jax.random.fold_in(jax.random.key(seed), 1), (8, 512, 128), dtype=_x0.dtype)
    del _x0
    return _d

def reference(L0_attn_x, L0_attn_wq_w, L0_attn_wq_b, L0_attn_wk_w, L0_attn_wk_b, L0_attn_wv_w, L0_attn_wv_b, L0_attn_wo_w, L0_attn_wo_b, L0_attn_qn_w, L0_attn_kn_w, L0_ffn_w1_w, L0_ffn_w1_s, L0_ffn_w2_w, L0_ffn_w2_s, L0_ffn_h1_w, L0_ffn_h1_s, L0_ffn_h2_w, L0_ffn_h2_s, L0_ffn_w3_w, L0_ffn_w3_s, L1_attn_W_qkv, L1_attn_b_qkv, L1_ffn_norm_scale, L1_ffn_gate_w, L1_ffn_gate_b, L1_ffn_w1, L1_ffn_b1, L1_ffn_w2, L1_ffn_b2, L2_attn_norm_in_w, L2_attn_conv_w, L2_attn_conv_b, L2_attn_q_w, L2_attn_k_w, L2_attn_v_w, L2_attn_out_w, L2_attn_alpha_w, L2_attn_alpha_b, L2_attn_beta_w, L2_attn_beta_b, L2_attn_head_norm_w, L2_attn_u1_w, L2_attn_u1_b, L2_attn_u2_w, L2_attn_u2_b, L2_attn_ff_norm_w, L2_attn_ff_w1, L2_attn_ff_w3, L2_attn_ff_w2, L2_ffn_ln_w, L2_ffn_Wg, L2_ffn_bg, L2_ffn_W1a, L2_ffn_b1a, L2_ffn_W1b, L2_ffn_b1b, L2_ffn_W2, L2_ffn_b2, L3_attn_Wq, L3_attn_bq, L3_attn_Wdown, L3_attn_bdown, L3_attn_Wup, L3_attn_bup, L3_attn_Wout, L3_attn_bout, L3_ffn_Wg, L3_ffn_gamma, L3_ffn_beta, L3_ffn_W1, L3_ffn_b1, L3_ffn_W2, L3_ffn_b2):

    def _L0_attn_ref(x, wq_w, wq_b, wk_w, wk_b, wv_w, wv_b, wo_w, wo_b, qn_w, kn_w):
        import jax, jax.numpy as jnp
        import numpy as np
        DIM = 128
        NUM_HEADS = 16
        HEAD_DIM = DIM // NUM_HEADS
        WINDOW = 32
        B, L = (2, 256)
        EPS = 1e-05
        INIT_STD = 0.01

        def rmsnorm(x, w):
            x = jnp.clip(x, -10000.0, 10000.0)
            rms = jnp.sqrt(jnp.maximum(jnp.mean(x * x, axis=-1, keepdims=True), EPS) + EPS)
            out = x / rms * w
            return jnp.where(jnp.isfinite(out), out, jnp.zeros_like(out))
        b, l, d = x.shape
        x = x.astype(jnp.float32)

        def proj(w, bias):
            return (x @ w.T + bias).reshape(b, l, NUM_HEADS, HEAD_DIM).transpose(0, 2, 1, 3)
        q = rmsnorm(proj(wq_w, wq_b), qn_w)
        k = rmsnorm(proj(wk_w, wk_b), kn_w)
        v = proj(wv_w, wv_b)
        scale = HEAD_DIM ** (-0.5)
        i = jnp.arange(l)
        allowed = (i[None, :] <= i[:, None]) & (i[:, None] - i[None, :] < WINDOW)
        scores = jnp.einsum('bhqd,bhkd->bhqk', q, k) * scale
        scores = jnp.where(allowed[None, None], scores, -jnp.inf)
        attn = jax.nn.softmax(scores, axis=-1)
        out = jnp.einsum('bhqk,bhkd->bhqd', attn, v)
        out = jnp.where(jnp.isfinite(out), out, jnp.zeros_like(out))
        out = out.transpose(0, 2, 1, 3).reshape(b, l, d)
        return out @ wo_w.T + wo_b

    def _L0_ffn_ref(x, w1_w, w1_s, w2_w, w2_s, h1_w, h1_s, h2_w, h2_s, w3_w, w3_s):
        import jax, jax.numpy as jnp
        import numpy as np
        D_IN, D_HID = (128, 512)

        def _ternary(key, shape):
            return jax.random.randint(key, shape, -1, 2).astype(jnp.float32)

        def _tlin(x, w, s):
            return jnp.einsum('bsi,oi->bso', x, w) * s
        h = jax.nn.silu(_tlin(x, w1_w, w1_s)) * _tlin(x, w2_w, w2_s)
        h = jax.nn.gelu(_tlin(h, h1_w, h1_s), approximate=False)
        h = jax.nn.gelu(_tlin(h, h2_w, h2_s), approximate=False)
        return _tlin(h, w3_w, w3_s)

    def _L1_attn_ref(x, W_qkv, b_qkv):
        import jax, jax.numpy as jnp
        import numpy as np
        import math
        DIM = 128
        ATTN_DIM = 128
        B, S = (2, 512)
        b, s, d = x.shape
        qkv = jnp.einsum('bsd,ed->bse', x, W_qkv) + b_qkv
        q, k, v = jnp.split(qkv, 3, axis=-1)
        score = jnp.einsum('bqd,bkd->bqk', q, k)
        causal = jnp.tril(jnp.ones((s, s), dtype=bool))
        score = jnp.where(causal, score, -jnp.inf)
        attn = jax.nn.softmax(score / math.sqrt(ATTN_DIM), axis=-1)
        y = jnp.einsum('bqk,bkd->bqd', attn, v)
        return y

    def _L1_ffn_ref(x, norm_scale, gate_w, gate_b, w1, b1, w2, b2):
        import jax, jax.numpy as jnp
        import numpy as np
        E = 32
        K = 4
        H = 128
        F = 128
        LIMIT = 7.0
        ALPHA = 1.702
        EPS = 1e-05

        def _rmsnorm(x, scale):
            t = x * jax.lax.rsqrt(jnp.mean(x * x, axis=-1, keepdims=True) + EPS)
            return t * scale

        def _swiglu(h):
            glu = jnp.minimum(h[..., ::2], LIMIT)
            lin = jnp.clip(h[..., 1::2], -LIMIT, LIMIT)
            return glu * jax.nn.sigmoid(ALPHA * glu) * (lin + 1.0)
        B, S, _ = x.shape
        t = _rmsnorm(x, norm_scale)
        g = t @ gate_w.T + gate_b
        tf = t.reshape(-1, H)
        gf = g.reshape(-1, E)
        T = tf.shape[0]
        vals, idx = jax.lax.top_k(gf, K)
        w = jax.nn.softmax(vals, axis=-1)
        combine = jnp.zeros((T, E), dtype=tf.dtype).at[jnp.arange(T)[:, None], idx].add(w)
        h1 = jnp.einsum('th,efh->tef', tf, w1) + b1
        h = _swiglu(h1)
        hw = h * combine[:, :, None]
        out = jnp.einsum('tef,ehf->th', hw, w2) + combine @ b2
        return x + out.reshape(B, S, H)

    def _L2_attn_ref(x, norm_in_w, conv_w, conv_b, q_w, k_w, v_w, out_w, alpha_w, alpha_b, beta_w, beta_b, head_norm_w, u1_w, u1_b, u2_w, u2_b, ff_norm_w, ff_w1, ff_w3, ff_w2):
        import jax, jax.numpy as jnp
        import numpy as np
        D, H, DK, DV, F, R = (128, 16, 64, 64, 512, 64)
        B, T = (4, 256)
        KCONV = 4
        EPS = 1e-06

        def rmsnorm(x, w):
            return x * jax.lax.rsqrt(jnp.mean(x * x, axis=-1, keepdims=True) + EPS) * w

        def _reference_tuple_inner(x, norm_in_w, conv_w, conv_b, q_w, k_w, v_w, out_w, alpha_w, alpha_b, beta_w, beta_b, head_norm_w, u1_w, u1_b, u2_w, u2_b, ff_norm_w, ff_w1, ff_w3, ff_w2):
            bsz, seq, _ = x.shape
            h = rmsnorm(x, norm_in_w)
            hc = jax.lax.conv_general_dilated(h.transpose(0, 2, 1), conv_w, (1,), [(KCONV - 1, 0)], dimension_numbers=('NCH', 'OIH', 'NCH'), feature_group_count=D)
            h = jax.nn.silu((hc + conv_b[None, :, None]).transpose(0, 2, 1))
            q = (h @ q_w).reshape(bsz, seq, H, DK)
            k = (h @ k_w).reshape(bsz, seq, H, DK)
            v = (h @ v_w).reshape(bsz, seq, H, DV)
            q = q / (jnp.linalg.norm(q, axis=-1, keepdims=True) + EPS)
            k = k / (jnp.linalg.norm(k, axis=-1, keepdims=True) + EPS)
            alpha = jax.nn.sigmoid(h @ alpha_w + alpha_b).reshape(bsz, seq, H, DK)
            beta = jax.nn.sigmoid(h @ beta_w + beta_b)

            def step(s, inp):
                qt, kt, vt, at, bt = inp
                s = s * at[..., None]
                u = jnp.einsum('bhd,bhdv->bhv', kt, s)
                s = s + bt[..., None, None] * (kt[..., None] * (vt - u)[..., None, :])
                out = jnp.einsum('bhdv,bhd->bhv', s, qt)
                return (s, out)
            tm = lambda a: jnp.swapaxes(a, 0, 1)
            s0 = jnp.zeros((bsz, H, DK, DV), x.dtype)
            s_final, outs = jax.lax.scan(step, s0, (tm(q), tm(k), tm(v), tm(alpha), tm(beta)))
            y = tm(outs)
            y = y * jax.lax.rsqrt(jnp.mean(y * y, axis=-1, keepdims=True) + EPS) * head_norm_w
            y = y.reshape(bsz, seq, H * DV)
            gate = jax.nn.sigmoid(jax.nn.silu(x @ u1_w + u1_b) @ u2_w + u2_b)
            y = x + y @ out_w * gate
            y2 = rmsnorm(y, ff_norm_w)
            y = y + jax.nn.silu(y2 @ ff_w1) * (y2 @ ff_w3) @ ff_w2
            return (y, s_final)
        return _reference_tuple_inner(x, norm_in_w, conv_w, conv_b, q_w, k_w, v_w, out_w, alpha_w, alpha_b, beta_w, beta_b, head_norm_w, u1_w, u1_b, u2_w, u2_b, ff_norm_w, ff_w1, ff_w3, ff_w2)[0]

    def _L2_ffn_ref(x, ln_w, Wg, bg, W1a, b1a, W1b, b1b, W2, b2):
        import jax, jax.numpy as jnp
        import numpy as np
        E = 8
        K = 2
        B, S, D = x.shape
        eps = jnp.finfo(x.dtype).eps
        xn = x * jax.lax.rsqrt(jnp.mean(x * x, axis=-1, keepdims=True) + eps) * ln_w
        logits = xn @ Wg + bg
        vals, idx = jax.lax.top_k(logits, K)
        topk_w = jax.nn.softmax(vals, axis=-1)
        we = jnp.sum(jax.nn.one_hot(idx, E, dtype=x.dtype) * topk_w[..., None], axis=-2)
        T = B * S
        xf = xn.reshape(T, D)
        wef = we.reshape(T, E).T

        def step(acc, params):
            W1a_e, b1a_e, W1b_e, b1b_e, W2_e, b2_e, w_e = params
            a = xf @ W1a_e + b1a_e
            b = xf @ W1b_e + b1b_e
            y = jax.nn.silu(a) * b @ W2_e + b2_e
            return (acc + w_e[:, None] * y, None)
        out0 = jnp.zeros_like(xf)
        out, _ = jax.lax.scan(step, out0, (W1a, b1a, W1b, b1b, W2, b2, wef))
        return out.reshape(B, S, D)

    def _L3_attn_ref(x, Wq, bq, Wdown, bdown, Wup, bup, Wout, bout):
        import jax, jax.numpy as jnp
        import numpy as np
        D_MODEL = 128
        N_HEADS = 16
        D_LATENT = 32
        HEAD_DIM = D_MODEL // N_HEADS

        def apply_rope(x):
            B, T, H, D = x.shape
            inv_freq = 1.0 / 10000.0 ** (jnp.arange(0, D, 2, dtype=jnp.float32) / D)
            t = jnp.arange(T, dtype=jnp.float32)
            freqs = t[:, None] * inv_freq[None, :]
            sin_f = jnp.sin(freqs)[None, :, None, :]
            cos_f = jnp.cos(freqs)[None, :, None, :]
            x1, x2 = jnp.split(x, 2, axis=-1)
            return jnp.concatenate([x1 * cos_f - x2 * sin_f, x1 * sin_f + x2 * cos_f], axis=-1)
        B, T, D = x.shape
        H, Dh = (N_HEADS, HEAD_DIM)
        q = x @ Wq + bq
        kv_latent = x @ Wdown + bdown
        kv = kv_latent @ Wup + bup
        q = q.reshape(B, T, H, Dh)
        kv = kv.reshape(B, T, H, 2 * Dh)
        k, v = jnp.split(kv, 2, axis=-1)
        q = apply_rope(q)
        k = apply_rope(k)
        att = jnp.einsum('bthd,btgd->bthg', q, k) / jnp.sqrt(jnp.float32(Dh))
        att = jax.nn.softmax(att, axis=-1)
        out = jnp.einsum('bthg,btgd->bthd', att, v)
        out = out.reshape(B, T, D)
        return out @ Wout + bout

    def _L3_ffn_ref(x, Wg, gamma, beta, W1, b1, W2, b2):
        import jax, jax.numpy as jnp
        import numpy as np
        E, K, D, F = (8, 2, 128, 512)
        EPS = 1e-06
        B, S = (2, 128)
        orig_shape = x.shape
        xf = x.reshape(-1, orig_shape[-1])
        scores = xf @ Wg
        w, idx = jax.lax.top_k(scores, K)
        w = jax.nn.softmax(w, axis=-1)
        mu = jnp.mean(xf, axis=-1, keepdims=True)
        var = jnp.var(xf, axis=-1, keepdims=True)
        xhat = (xf - mu) * jax.lax.rsqrt(var + EPS)
        normed = xhat[None, :, :] * gamma[:, None, :] + beta[:, None, :]
        h = jax.nn.relu(jnp.einsum('end,edf->enf', normed, W1) + b1[:, None, :])
        out = jnp.einsum('enf,efd->end', h, W2) + b2[:, None, :] + xf[None, :, :]
        cw = jnp.sum(w[..., None] * jax.nn.one_hot(idx, E, dtype=w.dtype), axis=1)
        y = jnp.einsum('ne,end->nd', cw, out)
        return y.reshape(orig_shape)
    x = L0_attn_x
    x = x + _layernorm(_L0_attn_ref(_layernorm(x, axis=-1), L0_attn_wq_w, L0_attn_wq_b, L0_attn_wk_w, L0_attn_wk_b, L0_attn_wv_w, L0_attn_wv_b, L0_attn_wo_w, L0_attn_wo_b, L0_attn_qn_w, L0_attn_kn_w), axis=-1)
    x = x + _layernorm(_L0_ffn_ref(_layernorm(x, axis=-1), L0_ffn_w1_w, L0_ffn_w1_s, L0_ffn_w2_w, L0_ffn_w2_s, L0_ffn_h1_w, L0_ffn_h1_s, L0_ffn_h2_w, L0_ffn_h2_s, L0_ffn_w3_w, L0_ffn_w3_s), axis=-1)
    x = x + _layernorm(_L1_attn_ref(_layernorm(x, axis=-1), L1_attn_W_qkv, L1_attn_b_qkv), axis=-1)
    x = x + _layernorm(_L1_ffn_ref(_layernorm(x, axis=-1), L1_ffn_norm_scale, L1_ffn_gate_w, L1_ffn_gate_b, L1_ffn_w1, L1_ffn_b1, L1_ffn_w2, L1_ffn_b2), axis=-1)
    x = x + _layernorm(_L2_attn_ref(_layernorm(x, axis=-1), L2_attn_norm_in_w, L2_attn_conv_w, L2_attn_conv_b, L2_attn_q_w, L2_attn_k_w, L2_attn_v_w, L2_attn_out_w, L2_attn_alpha_w, L2_attn_alpha_b, L2_attn_beta_w, L2_attn_beta_b, L2_attn_head_norm_w, L2_attn_u1_w, L2_attn_u1_b, L2_attn_u2_w, L2_attn_u2_b, L2_attn_ff_norm_w, L2_attn_ff_w1, L2_attn_ff_w3, L2_attn_ff_w2), axis=-1)
    x = x + _layernorm(_L2_ffn_ref(_layernorm(x, axis=-1), L2_ffn_ln_w, L2_ffn_Wg, L2_ffn_bg, L2_ffn_W1a, L2_ffn_b1a, L2_ffn_W1b, L2_ffn_b1b, L2_ffn_W2, L2_ffn_b2), axis=-1)
    x = x + _layernorm(_L3_attn_ref(_layernorm(x, axis=-1), L3_attn_Wq, L3_attn_bq, L3_attn_Wdown, L3_attn_bdown, L3_attn_Wup, L3_attn_bup, L3_attn_Wout, L3_attn_bout), axis=-1)
    x = x + _layernorm(_L3_ffn_ref(_layernorm(x, axis=-1), L3_ffn_Wg, L3_ffn_gamma, L3_ffn_beta, L3_ffn_W1, L3_ffn_b1, L3_ffn_W2, L3_ffn_b2), axis=-1)
    return x

_drawn_inputs = setup_inputs


def setup_inputs(seed=0):
    import zlib

    import numpy as np

    out = dict(_drawn_inputs(seed))
    spreads = {'L0_attn_wq_b': (0.0, 0.29),
     'L0_attn_wk_b': (0.0, 0.484),
     'L0_attn_wv_b': (0.0, 0.1),
     'L0_attn_wo_b': (0.0, 0.1),
     'L0_attn_qn_w': (1.0, 0.6),
     'L0_attn_kn_w': (1.0, 0.6),
     'L1_ffn_norm_scale': (1.0, 0.6),
     'L1_ffn_gate_b': (0.0, 0.33),
     'L1_ffn_b1': (0.0, 0.798),
     'L1_ffn_b2': (0.0, 0.1),
     'L2_attn_norm_in_w': (1.0, 0.6),
     'L2_attn_conv_b': (0.0, 0.1),
     'L2_attn_alpha_b': (0.0, 0.593),
     'L2_attn_beta_b': (0.0, 0.8),
     'L2_attn_head_norm_w': (1.0, 0.6),
     'L2_attn_u1_b': (0.0, 0.8),
     'L2_attn_u2_b': (0.0, 0.772),
     'L2_attn_ff_norm_w': (1.0, 0.6),
     'L2_ffn_ln_w': (1.0, 0.2),
     'L2_ffn_bg': (0.0, 0.1),
     'L2_ffn_b1a': (0.0, 0.309),
     'L2_ffn_b1b': (0.0, 0.298),
     'L2_ffn_b2': (0.0, 0.1),
     'L3_attn_bq': (0.0, 0.325),
     'L3_attn_bdown': (0.0, 0.1),
     'L3_attn_bup': (0.0, 0.1),
     'L3_attn_bout': (0.0, 0.1),
     'L3_ffn_gamma': (1.0, 0.6),
     'L3_ffn_beta': (0.0, 0.8),
     'L3_ffn_b1': (0.0, 0.8),
     'L3_ffn_b2': (0.0, 0.626)}
    factors = {'L1_attn_b_qkv': 2.899,
     'L1_ffn_w1': 3.998,
     'L1_ffn_w2': 3.74,
     'L2_attn_alpha_w': 23.727,
     'L2_attn_beta_w': 32.651,
     'L2_attn_u1_w': 8.0,
     'L2_attn_u2_w': 8.0,
     'L2_attn_ff_w1': 5.515,
     'L2_attn_ff_w3': 5.679,
     'L2_attn_ff_w2': 4.91,
     'L0_attn_wq_w': 3.113}
    for name, (base, spread) in spreads.items():
        noise = np.random.default_rng([zlib.crc32(name.encode()), seed]).standard_normal(out[name].shape)
        drawn = base * np.exp(spread * noise) if base else spread * noise
        out[name] = jnp.asarray(drawn.astype(out[name].dtype))
    for name, factor in factors.items():
        out[name] = (out[name] * factor).astype(out[name].dtype)
    return out
```

```python
from contextlib import ExitStack

import numpy as np
import concourse.bass as bass
from concourse import mybir

F32 = mybir.dt.float32
I32 = mybir.dt.int32
ALU = mybir.AluOpType
ACT = mybir.ActivationFunctionType
AX = mybir.AxisListType

STAGES = (0, 1, 2, 3, 4, 5, 6, 7)

B, L, D = 8, 512, 128
P = 128
TB = L // P
NT = B * TB
NEG = -1.0e30
LN_EPS = 1e-5




class Chain:

    def __init__(self, eng, sem):
        self.eng, self.sem, self.n = eng, sem, 0

    def reset(self):
        self.eng.sem_clear(self.sem)
        self.n = 0

    def link(self, ins):
        ins.then_inc(self.sem, 1)
        self.n += 1
        self.eng.wait_ge(self.sem, self.n)


class Core:

    def __init__(self, nc, ctx, A):
        self.nc, self.A = nc, A
        sb = lambda n, s: ctx.enter_context(nc.sbuf_tensor(n, s, F32))
        self.x = sb("x", [P, NT + TB, D])
        self.xn = sb("xn", [P, NT + TB, D])
        self.xT = sb("xT", [P, (B + 1) * L])
        self.ident = sb("ident", [P, P])
        self.beta = sb("beta", [P, B, NT, 2])
        self.mhalf = sb("mhalf", [P, 64])
        self.sems = {}
        self.load_counts = {}
        self.ctx = ctx
        self.psum = ctx.enter_context(nc.psum_tensor("psum", [P, 8, L], F32))
        self.ps = [self.psum[:, i, :] for i in range(8)]

    def lasting_sem(self, name):
        if name not in self.sems:
            self.sems[name] = self.ctx.enter_context(self.nc.semaphore(name))
        return self.sems[name]

    def sem(self, name):
        if name not in self.tokens:
            self.tokens[name] = self.stage_ctx.enter_context(self.nc.semaphore(f"{self.stage_tag}_{name}"))
        return self.tokens[name]


class Stage:

    def __init__(self, core, tag):
        self.c, self.tag, self.ctx = core, tag, ExitStack()
        self.loads = []
        self.due = {}
        core.stage_ctx, core.stage_tag, core.tokens = self.ctx, tag, {}

    def sb(self, name, shape, dt=F32):
        return self.ctx.enter_context(self.c.nc.sbuf_tensor(f"{self.tag}_{name}", shape, dt))

    def load(self, name, shape, group=0):
        t = self.sb(name, shape)
        self.loads.append((t, self.c.A[f"{self.tag}_{name}"], group))
        self.due[group] = self.c.load_counts[group] = self.c.load_counts.get(group, 0) + 16
        return t

    def issue_loads(self, sp):
        for t, src, group in self.loads:
            sp.dma_start(t[:], src).then_inc(self.c.lasting_sem(f"loaded{group}"), 16)

    def wait_loads(self, eng, group=0):
        eng.wait_ge(self.c.lasting_sem(f"loaded{group}"), self.due[group])


def flat(ap):
    return ap.rearrange("p a b -> p (a b)")



class Norm:

    def __init__(self, st, name, eps, rms=False):
        self.st, self.eps, self.rms = st, eps, rms
        self.stats = st.sb(f"{name}_stats", [P, TB, 6])
        self.mv = st.sb(f"{name}_mv", [P, TB, 2])
        self.rstd = st.sb(f"{name}_rstd", [P, TB, 1])
        self.tmp = st.sb(f"{name}_tmp", [P, TB, 1])
        s = st.c.sem
        self.var_ready = s(f"{name}_var_ready")
        self.rstd_ready = s(f"{name}_rstd_ready")

    def dve_stats(self, v, ch, tiles):
        for t in range(TB):
            r = v.bn_stats(self.stats[:, t, :], tiles(t))
        ch.link(r)
        for t in range(TB):
            r = v.bn_aggr(self.mv[:, t, :], self.stats[:, t, :])
        if self.rms:
            ch.link(r)
            ch.link(v.tensor_tensor(self.tmp[:], self.mv[:, :, 0:1], self.mv[:, :, 0:1], ALU.mult))
            r = v.tensor_tensor(self.mv[:, :, 1:2], self.mv[:, :, 1:2], self.tmp[:], ALU.add)
        r.then_inc(self.var_ready, 1)

    def pool_rstd(self, g, ch):
        g.wait_ge(self.var_ready, 1)
        g.sem_clear(self.var_ready)
        ch.link(g.tensor_scalar(self.rstd[:, :, 0], self.mv[:, :, 1], self.eps, None, ALU.add))
        g.tensor_tensor(self.rstd[:, :, 0], self.rstd[:, :, 0], self.st.c.mhalf[:, 0:TB],
                        ALU.pow).then_inc(self.rstd_ready, 1)

    def dve_apply(self, v, outs, ins):
        v.wait_ge(self.rstd_ready, 1)
        v.sem_clear(self.rstd_ready)
        for t in range(TB):
            if self.rms:
                r = v.tensor_scalar(outs(t), ins(t), self.rstd[:, t, 0:1], None, ALU.mult)
            else:
                r = v.tensor_scalar(outs(t), ins(t), self.mv[:, t, 0:1], self.rstd[:, t, 0:1],
                                    ALU.subtract, ALU.mult)
        return r




class Pre:

    def __init__(self, st, inner=None, eps=0.0, gamma=None, both=False, static=False):
        self.st, self.inner, self.gamma, self.both = st, inner, gamma, both
        self.static = static or both
        self.n1 = Norm(st, "pre", LN_EPS)
        self.n2 = Norm(st, "inner", eps, rms=(inner == "rms")) if inner else None
        self.y1 = st.sb("pre_y1", [P, TB, D])
        self.y2 = st.sb("pre_y2", [P, TB, D]) if inner else self.y1
        self.xTs = st.sb("pre_xTs", [P, L]) if self.static else None
        s = st.c.sem
        self.y_ready = s("pre_y_ready")
        self.y_free = s("pre_y_free")
        self.t_ready = s("pre_t_ready")
        self.t_free = s("pre_t_free")
        self.xT_ready = s("pre_xT_ready")
        self.xTs_ready = s("pre_xTs_ready")
        self.xTs_free = s("pre_xTs_free")

    def seed_pe(self, pe):
        pe.sem_inc(self.y_free, 1)
        if self.static:
            pe.sem_inc(self.xTs_free, 1)

    def seed_act(self, a):
        a.sem_inc(self.t_free, 1)

    def drain_dve(self, v):
        v.wait_ge(self.y_free, 1)
        v.sem_clear(self.y_free)

    def drain_pe(self, pe):
        pe.wait_ge(self.t_free, 1)
        pe.sem_clear(self.t_free)
        pe.wait_ge(self.xT_ready, 1)
        pe.sem_clear(self.xT_ready)
        if self.both:
            pe.wait_ge(self.xTs_ready, 1)
            pe.sem_clear(self.xTs_ready)

    def drain_act(self, a):
        if self.static:
            a.wait_ge(self.xTs_free, 1)
            a.sem_clear(self.xTs_free)

    def dve(self, v, ch, b):
        c = self.st.c
        self.n1.dve_stats(v, ch, lambda t: c.x[:, b * TB + t, :])
        v.wait_ge(self.y_free, 1)
        v.sem_clear(self.y_free)
        r = self.n1.dve_apply(v, lambda t: self.y1[:, t, :], lambda t: c.x[:, b * TB + t, :])
        if self.inner:
            ch.link(r)
            self.n2.dve_stats(v, ch, lambda t: self.y1[:, t, :])
            r = self.n2.dve_apply(v, lambda t: self.y2[:, t, :], lambda t: self.y1[:, t, :])
        ch.link(r)
        v.sem_inc(self.y_ready, 1)

    def pool(self, g, ch, b):
        self.n1.pool_rstd(g, ch)
        if self.inner:
            self.n2.pool_rstd(g, ch)

    def pe(self, pe, b):
        c = self.st.c
        pe.wait_ge(self.y_ready, 1)
        pe.sem_clear(self.y_ready)
        srcs = [self.y1, self.y2] if self.both else [self.y2]
        for n, src in enumerate(srcs):
            pe.wait_ge(self.t_free, 1)
            pe.sem_clear(self.t_free)
            for t in range(TB):
                r = pe.transpose(c.ps[7][:, t * P:(t + 1) * P], src[:, t, :], c.ident[:])
            r.then_inc(self.t_ready, 1)
            if n == len(srcs) - 1:
                pe.drain().then_inc(self.y_free, 1)

    def act(self, a, b):
        c = self.st.c
        scale = self.gamma[:, 0:1] if self.gamma is not None else 1.0
        a.wait_ge(self.t_ready, 1)
        a.sem_clear(self.t_ready)
        if self.static:
            a.wait_ge(self.xTs_free, 1)
            a.sem_clear(self.xTs_free)
            r = a.activation(self.xTs[:], c.ps[7][:], ACT.Identity, scale=scale)
            r.then_inc(self.xTs_ready, 1)
        if self.both:
            a.drain().then_inc(self.t_free, 1)
            a.wait_ge(self.t_ready, 1)
            a.sem_clear(self.t_ready)
        a.activation(c.xT[:, bass.ds(b * L, L)], c.ps[7][:], ACT.Identity, scale=scale).then_inc(self.xT_ready, 1)
        a.drain().then_inc(self.t_free, 1)



class Post:
    def __init__(self, st):
        self.st = st
        self.norm = Norm(st, "post", LN_EPS)
        self.z = st.sb("post_z", [P, TB, D])

    def dve_stats(self, v, ch, tiles):
        self.norm.dve_stats(v, ch, tiles)

    def dve_add(self, v, ch, b, tiles):
        c = self.st.c
        ch.link(self.norm.dve_apply(v, lambda t: self.z[:, t, :], tiles))
        xb = c.x[:, bass.ds(b * TB, TB), :]
        ch.link(v.tensor_tensor(xb, xb, self.z[:], ALU.add))

    def pool(self, g, ch):
        self.norm.pool_rstd(g, ch)



HID = 512
HC = HID // P


def stage_ffn0(core):
    st = Stage(core, "f0")
    c, nc, s = core, core.nc, core.sem
    w1, w2 = st.load("w1", [P, HID]), st.load("w2", [P, HID])
    s1, s2, g1, g2 = (st.load(n, [P, HC]) for n in ("s1", "s2", "g1", "g2"))
    h1, h2 = st.load("h1", [P, HC, HID]), st.load("h2", [P, HC, HID])
    w3, s3 = st.load("w3", [P, HC, D]), st.load("s3", [P, D])
    pre, post = Pre(st), Post(st)
    t_s = st.sb("silu", [P, 2, L])
    hid = [st.sb(f"hid{i}", [P, HC, L]) for i in range(3)]
    y = st.sb("y", [P, TB, D])
    ready = [s(f"bank{i}_ready") for i in range(4)]
    free = [s(f"bank{i}_free") for i in range(4)]
    t_ready = [s(f"silu{i}_ready") for i in range(2)]
    t_free = [s(f"silu{i}_free") for i in range(2)]
    h_ready = [s(f"hid{i}_ready") for i in range(3)]
    h_free = [s(f"hid{i}_free") for i in range(3)]
    y_ready, y_free = s("y_ready"), s("y_free")
    with nc.Block() as block:
        @block.sync
        def _(sp):
            st.issue_loads(sp)

        @block.gpsimd
        def _(g):
            ch = Chain(g, core.lasting_sem("pool_chain"))
            ch.reset()
            pre.pool(g, ch, 0)
            with g.Fori(0, B) as b:
                ch.reset()
                pre.pool(g, ch, b + 1)
                post.pool(g, ch)

        @block.tensor
        def _(pe):
            st.wait_loads(pe)
            pre.seed_pe(pe)
            for i in range(3):
                pe.sem_inc(h_free[i], 1)
            pre.pe(pe, 0)
            with pe.Fori(0, B) as b:
                pe.wait_ge(pre.xT_ready, 1)
                pe.sem_clear(pre.xT_ready)
                xb = c.xT[:, bass.ds(b * L, L)]
                for m in range(HC):
                    for k, w in enumerate((w1, w2)):
                        i = (2 * m + k) % 4
                        pe.wait_ge(free[i], 1)
                        pe.sem_clear(free[i])
                        pe.matmul(c.ps[i][:], w[:, m * P:(m + 1) * P], xb, start=True,
                                  stop=True).then_inc(ready[i], 1)
                for n, w in enumerate((h1, h2)):
                    for m in range(HC):
                        pe.wait_ge(free[m], 1)
                        pe.sem_clear(free[m])
                        for k in range(HC):
                            if m == 0:
                                pe.wait_ge(h_ready[n], k + 1)
                            r = pe.matmul(c.ps[m][:], w[:, k, m * P:(m + 1) * P], hid[n][:, k, :],
                                          start=(k == 0), stop=(k == HC - 1))
                        r.then_inc(ready[m], 1)
                    pe.sem_clear(h_ready[n])
                    pe.drain().then_inc(h_free[n], 1)
                    if n == 0:
                        pre.pe(pe, b + 1)
                pe.wait_ge(h_ready[2], HC)
                pe.sem_clear(h_ready[2])
                pe.wait_ge(y_free, 1)
                pe.sem_clear(y_free)
                for t in range(TB):
                    for k in range(HC):
                        r = pe.matmul(c.ps[4][:, t * P:(t + 1) * P], hid[2][:, k, t * P:(t + 1) * P],
                                      w3[:, k, :], start=(k == 0), stop=(k == HC - 1))
                r.then_inc(y_ready, 1)
                pe.drain().then_inc(h_free[2], 1)
            for i in range(4):
                pe.wait_ge(free[i], 1)
                pe.sem_clear(free[i])
            pe.wait_ge(y_free, 1)
            pe.sem_clear(y_free)
            pre.drain_pe(pe)

        @block.scalar
        def _(a):
            st.wait_loads(a)
            pre.seed_act(a)
            a.sem_inc(free[0], 1)
            a.sem_inc(free[2], 1)
            pre.act(a, 0)
            with a.Fori(0, B) as b:
                for m in range(HC):
                    i = 2 * m % 4
                    a.wait_ge(ready[i], 1)
                    a.sem_clear(ready[i])
                    a.wait_ge(t_free[m % 2], 1)
                    a.sem_clear(t_free[m % 2])
                    a.activation(t_s[:, m % 2, :], c.ps[i][:], ACT.Silu, scale=s1[:, m:m + 1]).then_inc(t_ready[m % 2], 1)
                    a.drain().then_inc(free[i], 1)
                for n, sc in enumerate((g1, g2)):
                    a.wait_ge(h_free[n + 1], 1)
                    a.sem_clear(h_free[n + 1])
                    for m in range(HC):
                        a.wait_ge(ready[m], 1)
                        a.sem_clear(ready[m])
                        a.activation(hid[n + 1][:, m, :], c.ps[m][:], ACT.Gelu,
                                     scale=sc[:, m:m + 1]).then_inc(h_ready[n + 1], 1)
                        a.drain().then_inc(free[m], 1)
                    if n == 0:
                        pre.act(a, b + 1)
            pre.drain_act(a)
            for i in range(1, 3):
                a.wait_ge(h_free[i], 1)
                a.sem_clear(h_free[i])
            for i in range(2):
                a.wait_ge(t_free[i], 1)
                a.sem_clear(t_free[i])

        @block.vector
        def _(v):
            ch = Chain(v, core.lasting_sem("dve_chain"))
            ch.reset()
            st.wait_loads(v)
            v.sem_inc(free[1], 1)
            v.sem_inc(free[3], 1)
            v.sem_inc(y_free, 1)
            for i in range(2):
                v.sem_inc(t_free[i], 1)
            pre.dve(v, ch, 0)
            with v.Fori(0, B) as b:
                ch.reset()
                v.wait_ge(h_free[0], 1)
                v.sem_clear(h_free[0])
                for m in range(HC):
                    i = (2 * m + 1) % 4
                    v.wait_ge(ready[i], 1)
                    v.sem_clear(ready[i])
                    v.wait_ge(t_ready[m % 2], 1)
                    v.sem_clear(t_ready[m % 2])
                    v.scalar_tensor_tensor(hid[0][:, m, :], c.ps[i][:], s2[:, m:m + 1], t_s[:, m % 2, :],
                                           ALU.mult, ALU.mult).then_inc(h_ready[0], 1)
                    d = v.drain()
                    d.then_inc(free[i], 1)
                    v.sem_inc(t_free[m % 2], 1)
                pre.dve(v, ch, b + 1)
                v.wait_ge(y_ready, 1)
                v.sem_clear(y_ready)
                ch.link(v.tensor_tensor(y[:], c.ps[4][:].rearrange("p (a b) -> p a b", a=TB),
                                        s3[:].unsqueeze(1).broadcast_to((P, TB, D)), ALU.mult))
                v.sem_inc(y_free, 1)
                post.dve_stats(v, ch, lambda t: y[:, t, :])
                post.dve_add(v, ch, b, lambda t: y[:, t, :])
            pre.drain_dve(v)
            v.wait_ge(h_free[0], 1)
            v.sem_clear(h_free[0])
    st.ctx.close()



SENTINEL = -3.0e38
TAKEN = 3.0e38
UNITS = 32
QUARTERS = 4
UQ = UNITS // QUARTERS
AT_LN, AT_TRANSPOSE, AT_LOGITS, AT_TOPK, AT_EXP, AT_WEIGH, AT_COMBINE_T, AT_COMBINE_B2, AT_SUM = \
    2, 6, 9, 11, 13, 14, 17, 20, 22


def stage_moe(core, tag, E, topk, inner, eps, residual, kind):
    st = Stage(core, tag)
    c, nc, s = core, core.nc, core.sem
    FC = UNITS // E
    relu, silu, glu7 = kind == "relu", kind == "silu", kind == "glu7"
    gate, gate_b = st.load("gate", [P, E]), st.load("gate_b", [P, E])
    b2 = st.load("b2", [E, D])
    ba = st.load("ba", [P, UNITS])
    if relu:
        gamma = None
        eg, eb = st.load("eg", [P, E]), st.load("eb", [P, E])
    else:
        gamma, bb = st.load("gamma", [P, 1]), st.load("bb", [P, UNITS])
    wa, wb, wd = [], [], []
    for q in range(QUARTERS):
        wa.append(st.load(f"wa{q}", [P, UQ, P], q + 1))
        if not relu:
            wb.append(st.load(f"wb{q}", [P, UQ, P], q + 1))
        wd.append(st.load(f"wd{q}", [P, UQ, D], q + 1))
    pre = Pre(st, inner=inner, eps=eps, gamma=gamma, both=relu, static=True)
    post = Post(st)
    lg = st.sb("logits", [P, TB, E + 8])
    taken = st.sb("taken", [P, TB, E + 8])
    top, mark = st.sb("top", [P, TB, 8]), st.sb("mark", [P, TB, 8])
    ex, den = st.sb("ex", [P, TB, E]), st.sb("den", [P, TB, 1])
    comb_next, comb = st.sb("combine_next", [P, TB, E]), st.sb("combine", [P, TB, E])
    combT = st.sb("combineT", [E, L])
    acc_next, acc = st.sb("acc_next", [P, TB, D]), st.sb("acc", [P, TB, D])
    h, ta = st.sb("h", [P, 2, L]), st.sb("ta", [P, 2, L])
    if glu7:
        tb, tc, td = st.sb("tb", [P, 2, L]), st.sb("tc", [P, 2, L]), st.sb("td", [P, 2, L])
        c1 = st.sb("c1", [P, 1])
    if relu:
        nrm = st.sb("normed", [P, 2, L])
    a_ready = [s(f"bank{i}_ready") for i in range(4)]
    a_free = [s(f"bank{i}_free") for i in range(4)]
    t_ready = [s(f"ta{i}_ready") for i in range(2)]
    t_free = [s(f"ta{i}_free") for i in range(2)]
    h_ready = [s(f"h{i}_ready") for i in range(2)]
    y_ready = [s(f"y{i}_ready") for i in range(2)]
    y_free = [s(f"y{i}_free") for i in range(2)]
    n_ready = [s(f"normed{i}_ready") for i in range(2)]
    logits_ready, ex_ready, ex_done = s("logits_ready"), s("ex_ready"), s("ex_done")
    comb_ready, combT_ps, combT_ready = s("combine_ready"), s("combineT_ps"), s("combineT_ready")
    cb_ready, r_free, consts_ready = s("combine_b2_ready"), s("router_bank_free"), s("consts_ready")
    bank_r = c.ps[6]

    with nc.Block() as block:
        @block.sync
        def _(sp):
            st.issue_loads(sp)

        @block.gpsimd
        def _(g):
            ch = Chain(g, core.lasting_sem("pool_chain"))
            ch.reset()
            pre.pool(g, ch, 0)
            with g.Fori(0, B) as b:
                ch.reset()
                pre.pool(g, ch, b + 1)
                post.pool(g, ch)

        @block.tensor
        def _(pe):
            def logits():
                pe.wait_ge(pre.xTs_ready, 1)
                pe.sem_clear(pre.xTs_ready)
                pe.wait_ge(r_free, 1)
                pe.sem_clear(r_free)
                for t in range(TB):
                    r = pe.matmul(bank_r[:, t * E:(t + 1) * E], pre.xTs[:, t * P:(t + 1) * P], gate[:],
                                  start=True, stop=True)
                r.then_inc(logits_ready, 1)
                pe.drain().then_inc(pre.xTs_free, 1)

            def combine_t():
                pe.wait_ge(comb_ready, 1)
                pe.sem_clear(comb_ready)
                for t in range(TB):
                    r = pe.transpose(bank_r[0:E, t * P:(t + 1) * P], comb_next[:, t, :], c.ident[:])
                r.then_inc(combT_ps, 1)

            def combine_b2():
                pe.wait_ge(combT_ready, 1)
                pe.sem_clear(combT_ready)
                for t in range(TB):
                    r = pe.matmul(bank_r[:, t * P:(t + 1) * P], combT[:, t * P:(t + 1) * P], b2[:],
                                  start=True, stop=True)
                r.then_inc(cb_ready, 1)

            def up(u, xb):
                e, q, j = u // FC, u // UQ, u % UQ
                if j == 0:
                    st.wait_loads(pe, q + 1)
                if relu:
                    if u % FC == 0:
                        pe.wait_ge(n_ready[e % 2], 1)
                        pe.sem_clear(n_ready[e % 2])
                    pe.wait_ge(a_free[u % 4], 1)
                    pe.sem_clear(a_free[u % 4])
                    pe.matmul(c.ps[u % 4][:], wa[q][:, j, :], nrm[:, e % 2, :], start=True,
                              stop=True).then_inc(a_ready[u % 4], 1)
                else:
                    for k, w in enumerate((wa, wb)):
                        i = 2 * (u % 2) + k
                        pe.wait_ge(a_free[i], 1)
                        pe.sem_clear(a_free[i])
                        pe.matmul(c.ps[i][:], w[q][:, j, :], xb, start=True, stop=True).then_inc(a_ready[i], 1)

            def down(u):
                e, m = u // FC, u % FC
                if m == 0:
                    pe.wait_ge(y_free[e % 2], 1)
                    pe.sem_clear(y_free[e % 2])
                pe.wait_ge(h_ready[u % 2], 1)
                pe.sem_clear(h_ready[u % 2])
                for t in range(TB):
                    r = pe.matmul(c.ps[4 + e % 2][:, t * P:(t + 1) * P], h[:, u % 2, t * P:(t + 1) * P],
                                  wd[u // UQ][:, u % UQ, :], start=(m == 0 and t == 0), stop=(m == FC - 1),
                                  skip_group_check=True)
                if m == FC - 1:
                    r.then_inc(y_ready[e % 2], 1)

            st.wait_loads(pe)
            pre.seed_pe(pe)
            pre.pe(pe, 0)
            logits()
            combine_t()
            combine_b2()
            with pe.Fori(0, B) as b:
                if not relu:
                    pe.wait_ge(pre.xT_ready, 1)
                    pe.sem_clear(pre.xT_ready)
                xb = c.xT[:, bass.ds(b * L, L)]
                for u in range(UNITS):
                    if u == AT_TRANSPOSE:
                        pre.pe(pe, b + 1)
                    if u == AT_LOGITS:
                        logits()
                    if u == AT_COMBINE_T:
                        combine_t()
                    if u == AT_COMBINE_B2:
                        combine_b2()
                    up(u, xb)
                    if u >= 1:
                        down(u - 1)
                down(UNITS - 1)
            for i in range(4):
                pe.wait_ge(a_free[i], 1)
                pe.sem_clear(a_free[i])
            pe.wait_ge(y_free[0], 1)
            pe.sem_clear(y_free[0])
            pe.wait_ge(y_free[1], 1)
            pe.sem_clear(y_free[1])
            pe.wait_ge(r_free, 1)
            pe.sem_clear(r_free)
            pe.wait_ge(pre.t_free, 1)
            pe.sem_clear(pre.t_free)
            if not relu:
                pe.wait_ge(pre.xT_ready, 1)
                pe.sem_clear(pre.xT_ready)

        @block.scalar
        def _(a):
            ch = Chain(a, core.lasting_sem("act_chain"))
            ch.reset()
            st.wait_loads(a)
            pre.seed_act(a)
            for i in ((0, 2) if silu else (0, 1, 2, 3)):
                a.sem_inc(a_free[i], 1)

            def exps():
                a.wait_ge(ex_ready, 1)
                a.sem_clear(ex_ready)
                a.activation(ex[:], ex[:], ACT.Exp).then_inc(ex_done, 1)

            def combine_t():
                a.wait_ge(combT_ps, 1)
                a.sem_clear(combT_ps)
                a.activation(combT[:], bank_r[0:E, :], ACT.Copy).then_inc(combT_ready, 1)

            pre.act(a, 0)
            exps()
            combine_t()
            a.wait_ge(consts_ready, 1)
            a.sem_clear(consts_ready)
            with a.Fori(0, B) as b:
                ch.reset()
                for u in range(UNITS):
                    if u == AT_TRANSPOSE:
                        pre.act(a, b + 1)
                    if u == AT_EXP:
                        exps()
                    if u == AT_COMBINE_T:
                        combine_t()
                    j = u % 2
                    if relu:
                        a.wait_ge(a_ready[u % 4], 1)
                        a.sem_clear(a_ready[u % 4])
                        a.activation(h[:, j, :], c.ps[u % 4][:], ACT.Relu, bias=ba[:, u:u + 1]).then_inc(h_ready[j], 1)
                        a.drain().then_inc(a_free[u % 4], 1)
                    elif silu:
                        a.wait_ge(a_ready[2 * j], 1)
                        a.sem_clear(a_ready[2 * j])
                        a.wait_ge(t_free[j], 1)
                        a.sem_clear(t_free[j])
                        a.activation(ta[:, j, :], c.ps[2 * j][:], ACT.Silu, bias=ba[:, u:u + 1]).then_inc(t_ready[j], 1)
                        a.drain().then_inc(a_free[2 * j], 1)
                    else:
                        a.wait_ge(a_ready[2 * j], 1)
                        a.sem_clear(a_ready[2 * j])
                        a.wait_ge(t_free[j], 1)
                        a.sem_clear(t_free[j])
                        ch.link(a.activation(ta[:, j, :], c.ps[2 * j][:], ACT.Relu, bias=ba[:, u:u + 1], scale=-1.0))
                        a.sem_inc(a_free[2 * j], 1)
                        a.activation(tc[:, j, :], ta[:, j, :], ACT.Sigmoid, scale=-1.702, bias=c1[:])
                        a.wait_ge(a_ready[2 * j + 1], 1)
                        a.sem_clear(a_ready[2 * j + 1])
                        a.activation(tb[:, j, :], c.ps[2 * j + 1][:], ACT.Relu, bias=bb[:, u:u + 1],
                                     scale=-1.0).then_inc(t_ready[j], 1)
                        a.drain().then_inc(a_free[2 * j + 1], 1)
            pre.drain_act(a)
            if not relu:
                a.wait_ge(t_free[0], 1)
                a.sem_clear(t_free[0])
                a.wait_ge(t_free[1], 1)
                a.sem_clear(t_free[1])

        @block.vector
        def _(v):
            ch = Chain(v, core.lasting_sem("dve_chain"))
            ch.reset()

            def route():
                v.wait_ge(logits_ready, 1)
                v.sem_clear(logits_ready)
                ch.link(v.tensor_tensor(lg[:, :, 0:E], bank_r[:, 0:TB * E].rearrange("p (t e) -> p t e", t=TB),
                                        gate_b[:].unsqueeze(1).broadcast_to((P, TB, E)), ALU.add))
                for t in range(TB):
                    r = v.max(top[:, t, :], lg[:, t, 0:E])
                ch.link(r)
                ch.link(v.tensor_copy(mark[:, :, 0:topk], top[:, :, 0:topk]))
                v.tensor_tensor(ex[:], lg[:, :, 0:E], top[:, :, 0:1].broadcast_to((P, TB, E)),
                                ALU.subtract).then_inc(ex_ready, 1)
                for t in range(TB):
                    r = v.match_replace(taken[:, t, :], mark[:, t, :], lg[:, t, :], TAKEN)
                ch.link(r)
                ch.link(v.tensor_scalar(taken[:, :, 0:E], taken[:, :, 0:E], TAKEN, None, ALU.is_equal))

            def weigh():
                v.wait_ge(ex_done, 1)
                v.sem_clear(ex_done)
                ch.link(v.tensor_tensor(ex[:], ex[:], taken[:, :, 0:E], ALU.mult))
                ch.link(v.tensor_reduce(den[:], ex[:], AX.X, ALU.add))
                ch.link(v.reciprocal(den[:], den[:]))
                ch.link(v.tensor_tensor(comb_next[:], ex[:], den[:].broadcast_to((P, TB, E)), ALU.mult))
                v.sem_inc(comb_ready, 1)

            def start_sum():
                v.wait_ge(cb_ready, 1)
                v.sem_clear(cb_ready)
                src = bank_r[:].rearrange("p (t d) -> p t d", t=TB)
                if residual:
                    ch.link(v.tensor_tensor(acc_next[:], src, pre.y1[:], ALU.add))
                else:
                    ch.link(v.tensor_copy(acc_next[:], src))
                v.sem_inc(r_free, 1)

            def make_normed(e, b):
                if e < E:
                    v.tensor_scalar(nrm[:, e % 2, :], c.xT[:, bass.ds(b * L, L)], eg[:, e:e + 1], eb[:, e:e + 1],
                                    ALU.mult, ALU.add).then_inc(n_ready[e % 2], 1)

            def collect(e, b):
                v.wait_ge(y_ready[e % 2], 1)
                v.sem_clear(y_ready[e % 2])
                for t in range(TB):
                    r = v.scalar_tensor_tensor(acc[:, t, :], c.ps[4 + e % 2][:, t * P:(t + 1) * P],
                                               comb[:, t, e:e + 1], acc[:, t, :], ALU.mult, ALU.add)
                ch.link(r)
                v.sem_inc(y_free[e % 2], 1)
                if relu:
                    make_normed(e + 2, b)

            st.wait_loads(v)
            v.memset(lg[:], SENTINEL)
            ch.link(v.memset(mark[:], SENTINEL))
            if glu7:
                v.memset(c1[:], 7.0 * 1.702)
                v.tensor_scalar(ba[:], ba[:], -1.0, 7.0, ALU.mult, ALU.add)
                ch.link(v.tensor_scalar(bb[:], bb[:], -1.0, 7.0, ALU.mult, ALU.add))
            v.sem_inc(consts_ready, 1)
            if silu:
                v.sem_inc(a_free[1], 1)
                v.sem_inc(a_free[3], 1)
            for i in range(2):
                v.sem_inc(y_free[i], 1)
                if not relu:
                    v.sem_inc(t_free[i], 1)
            v.sem_inc(r_free, 1)
            pre.dve(v, ch, 0)
            route()
            weigh()
            start_sum()
            with v.Fori(0, B) as b:
                ch.reset()
                v.tensor_copy(comb[:], comb_next[:])
                if relu:
                    v.wait_ge(pre.xT_ready, 1)
                    v.sem_clear(pre.xT_ready)
                    make_normed(0, b)
                    make_normed(1, b)
                ch.link(v.tensor_copy(acc[:], acc_next[:]))
                for u in range(UNITS):
                    if u == AT_LN:
                        pre.dve(v, ch, b + 1)
                    if u == AT_TOPK:
                        route()
                    if u == AT_WEIGH:
                        weigh()
                    if u == AT_SUM:
                        start_sum()
                    j = u % 2
                    if silu:
                        v.wait_ge(a_ready[2 * j + 1], 1)
                        v.sem_clear(a_ready[2 * j + 1])
                        v.wait_ge(t_ready[j], 1)
                        v.sem_clear(t_ready[j])
                        v.scalar_tensor_tensor(h[:, j, :], c.ps[2 * j + 1][:], bb[:, u:u + 1], ta[:, j, :],
                                               ALU.add, ALU.mult).then_inc(h_ready[j], 1)
                        v.drain().then_inc(a_free[2 * j + 1], 1)
                        v.sem_inc(t_free[j], 1)
                    if glu7:
                        v.wait_ge(t_ready[j], 1)
                        v.sem_clear(t_ready[j])
                        v.scalar_tensor_tensor(td[:, j, :], ta[:, j, :], 7.0, tc[:, j, :], ALU.subtract, ALU.mult)
                        ch.link(v.tensor_scalar(tb[:, j, :], tb[:, j, :], 8.0, 6.0, ALU.subtract, ALU.min))
                        v.tensor_tensor(h[:, j, :], td[:, j, :], tb[:, j, :], ALU.mult).then_inc(h_ready[j], 1)
                        v.drain().then_inc(t_free[j], 1)
                    if u >= FC + 1 and (u - FC - 1) % FC == 0:
                        collect((u - FC - 1) // FC, b)
                for e in range((UNITS - 1 - FC - 1) // FC + 1, E):
                    collect(e, b)
                post.dve_stats(v, ch, lambda t: acc[:, t, :])
                post.dve_add(v, ch, b, lambda t: acc[:, t, :])
            pre.drain_dve(v)
            if relu:
                v.wait_ge(pre.xT_ready, 1)
                v.sem_clear(pre.xT_ready)
    st.ctx.close()


def stage_moe1(core):
    stage_moe(core, "m1", 32, 4, "rms", 1e-5, True, "glu7")


def stage_moe2(core):
    stage_moe(core, "m2", 8, 2, "rms", float(np.finfo(np.float32).eps), False, "silu")


def stage_moe3(core):
    stage_moe(core, "m3", 8, 2, "ln", 1e-6, True, "relu")



H, HD = 16, 8
WIN = 32
G, HG = 4, 4
VW = HD + 1
CLIP, QK_EPS = 10000.0, 1e-5
SPAN = WIN + P
UN0 = G * TB
PRE0 = 10


def stage_attn0(core):
    st = Stage(core, "a0")
    c, nc, s = core, core.nc, core.sem
    wqk, wv = st.load("wqk", [P, 2 * D]), st.load("wv", [P, D])
    bqk, bv = st.load("bqk", [P, 2 * D]), st.load("bv", [P, D])
    nw = st.load("nw", [P, 2, HD])
    window = st.load("window", [P, SPAN])
    hm = st.load("headmask", [P, H])
    wo, bo = st.load("wo", [P, D]), st.load("bo", [P, D])
    pre, post = Pre(st, static=True), Post(st)
    NH = 2 * H
    raw = st.sb("raw", [P, TB * NH, HD])
    sq = st.sb("sq", [P, TB * NH, HD])
    rstd = st.sb("rstd", [P, TB * NH, 1])
    mh = st.sb("mhalf", [P, TB * NH])
    nwf = st.sb("nwf", [P, NH, HD])
    qk = st.sb("qk", [P, TB, 2, D])
    qT, kT = st.sb("qT", [P, L]), st.sb("kT", [P, L])
    qz = st.sb("qz", [P, H, L])
    va, vh = st.sb("v", [P, TB, H, VW]), st.sb("vh", [WIN, TB, H, VW])
    pr = st.sb("probs", [P, 4, HG, SPAN])
    nm = st.sb("negmax", [P, UN0, HG])
    pT, hT = st.sb("probsT", [P, L]), st.sb("haloT", [WIN, L])
    rec = st.sb("rec", [P, TB, HG, 1])
    o = st.sb("o", [P, TB, H, HD])
    oT, y = st.sb("oT", [P, L]), st.sb("y", [P, TB, D])
    qk_ps, v_ps = s("q_ps"), s("v_ps")
    ms_ready, rs_ready = s("head_ms_ready"), s("head_rstd_ready")
    qk_ready = s("qk_ready")
    tr_ready = [s(f"proj{i}_ready") for i in range(2)]
    qT_dve, qT_pool = s("qT_to_dve"), s("qT_to_pool")
    kT_ready = s("kT_ready")
    qz_ready = [s("qz_dve_ready"), s("qz_pool_ready")]
    v_ready = s("v_ready")
    s_ready = [s(f"scores{i}_ready") for i in range(2)]
    s_free = [s(f"scores{i}_free") for i in range(2)]
    m_ready = [s(f"max{i}_ready") for i in range(4)]
    p_ready = [s(f"probs{i}_ready") for i in range(4)]
    pt_ps, pt_ready = s("probsT0_ps"), s("probsT0_ready")
    ht_ps, ht_ready = s("probsT1_ps"), s("probsT1_ready")
    o_ready = [s(f"out{i}_ready") for i in range(2)]
    o_free = [s(f"out{i}_free") for i in range(2)]
    on_ready, oT_ps, oT_ready, y_ready = s("on_ready"), s("oT_ps"), s("oT_ready"), s("y_ready")
    y_free = s("y_free")

    def width(qb):
        return P if qb == 0 else SPAN

    def score_slot(i, w):
        return c.psum[:, 2 * i:2 * i + 2, :].rearrange("p a (c n) -> p (a c) n", c=2)[:, :, 0:w]

    with nc.Block() as block:
        @block.sync
        def _(sp):
            st.issue_loads(sp)

        @block.gpsimd
        def _(g):
            ch = Chain(g, core.lasting_sem("pool_chain"))
            ch.reset()
            ch.link(g.memset(mh[:], -0.5))
            pre.pool(g, ch, 0)
            with g.Fori(0, B) as b:
                ch.reset()
                g.wait_ge(ms_ready, 1)
                g.sem_clear(ms_ready)
                ch.link(g.tensor_scalar(rstd[:, :, 0], rstd[:, :, 0], QK_EPS, None, ALU.add))
                g.tensor_tensor(rstd[:, :, 0], rstd[:, :, 0], mh[:], ALU.pow).then_inc(rs_ready, 1)
                g.wait_ge(qT_pool, 1)
                g.sem_clear(qT_pool)
                for h in range(H // 2, H):
                    r = g.tensor_scalar(qz[:, h, :], qT[:], hm[:, h:h + 1], None, ALU.mult)
                    if h % HG == HG - 1:
                        r.then_inc(qz_ready[1], 1)
                pre.pool(g, ch, b + 1)
                post.pool(g, ch)

        @block.tensor
        def _(pe):
            def scores(u):
                g, qb = u // TB, u % TB
                w = width(qb)
                k0 = (qb + 1) * P - w
                pe.wait_ge(s_free[u % 2], 1)
                pe.sem_clear(s_free[u % 2])
                if qb == 0:
                    ready, n = qz_ready[g // 2], g % 2 + 1
                    if n == 1:
                        pe.wait_ge(ready, n)
                    else:
                        pe.wait_ge(ready, n)
                        pe.sem_clear(ready)
                for j in range(HG):
                    r = pe.matmul(score_slot(u % 2, w)[:, j, :], qz[:, g * HG + j, qb * P:(qb + 1) * P],
                                  kT[:, k0:k0 + w], start=True, stop=True)
                r.then_inc(s_ready[u % 2], 1)

            def transposes(u):
                qb = u % TB
                w = width(qb)
                pe.wait_ge(p_ready[u % 4], 1)
                pe.sem_clear(p_ready[u % 4])
                if qb:
                    for j in range(HG):
                        r = pe.transpose(c.ps[7][0:WIN, j * P:(j + 1) * P], pr[:, u % 4, j, 0:WIN], c.ident[:])
                    r.then_inc(ht_ps, 1)
                for j in range(HG):
                    r = pe.transpose(c.ps[4][:, j * P:(j + 1) * P], pr[:, u % 4, j, w - P:w], c.ident[:])
                r.then_inc(pt_ps, 1)

            def values(u):
                g, qb = u // TB, u % TB
                if qb == 0:
                    pe.wait_ge(o_free[g % 2], 1)
                    pe.sem_clear(o_free[g % 2])
                pe.wait_ge(pt_ready, 1)
                pe.sem_clear(pt_ready)
                if qb:
                    pe.wait_ge(ht_ready, 1)
                    pe.sem_clear(ht_ready)
                for j in range(HG):
                    h = g * HG + j
                    at, bank = (qb * HG + j) * VW, c.ps[6 - g % 2]
                    r = pe.matmul(bank[:, at:at + VW], pT[:, j * P:(j + 1) * P], va[:, qb, h, :],
                                  start=True, stop=(qb == 0))
                    if qb:
                        r = pe.matmul(bank[:, at:at + VW], hT[:, j * P:(j + 1) * P], vh[:, qb, h, :],
                                      start=False, stop=True)
                if qb == TB - 1:
                    r.then_inc(o_ready[g % 2], 1)

            st.wait_loads(pe)
            pre.seed_pe(pe)
            pre.pe(pe, 0)
            with pe.Fori(0, B) as b:
                pe.wait_ge(pre.xT_ready, 1)
                pe.sem_clear(pre.xT_ready)
                pe.wait_ge(pre.xTs_ready, 1)
                pe.sem_clear(pre.xTs_ready)
                pe.wait_ge(s_free[0], 1)
                pe.sem_clear(s_free[0])
                pe.wait_ge(s_free[1], 1)
                pe.sem_clear(s_free[1])
                for t in range(TB):
                    r = pe.matmul(c.ps[t // 2][:, (t % 2) * 2 * D:(t % 2 + 1) * 2 * D],
                                  pre.xTs[:, t * P:(t + 1) * P], wqk[:], start=True, stop=True)
                r.then_inc(qk_ps, 1)
                for t in range(TB):
                    pe.matmul(c.ps[2][:, t * P:(t + 1) * P], pre.xTs[:, t * P:(t + 1) * P], wv[:],
                              start=True, stop=True)
                for t in range(1, TB):
                    r = pe.matmul(c.ps[3][0:WIN, t * P:(t + 1) * P], pre.xTs[:, t * P - WIN:t * P], wv[:],
                                  start=True, stop=True)
                r.then_inc(v_ps, 1)
                pe.drain().then_inc(pre.xTs_free, 1)
                pe.wait_ge(qk_ready, 1)
                pe.sem_clear(qk_ready)
                for i in range(2):
                    for t in range(TB):
                        r = pe.transpose(c.ps[4 + i][:, t * P:(t + 1) * P], qk[:, t, i, :], c.ident[:])
                    r.then_inc(tr_ready[i], 1)
                pe.wait_ge(v_ready, 1)
                pe.sem_clear(v_ready)
                pe.wait_ge(kT_ready, 1)
                pe.sem_clear(kT_ready)
                for u in range(UN0 + 3):
                    if u < UN0:
                        scores(u)
                    if u >= 3:
                        values(u - 3)
                    if u == PRE0:
                        pre.pe(pe, b + 1)
                    if u == PRE0 + 1:
                        pe.wait_ge(pre.t_free, 1)
                    if 2 <= u < UN0 + 2:
                        transposes(u - 2)
                pe.wait_ge(on_ready, 1)
                pe.sem_clear(on_ready)
                for t in range(TB):
                    r = pe.transpose(c.ps[4][:, t * P:(t + 1) * P], o[:, t, :, :].rearrange("p h d -> p (h d)"),
                                     c.ident[:])
                r.then_inc(oT_ps, 1)
                pe.wait_ge(oT_ready, 1)
                pe.sem_clear(oT_ready)
                pe.wait_ge(y_free, 1)
                pe.sem_clear(y_free)
                pe.wait_ge(pre.t_free, 1)
                pe.sem_clear(pre.t_free)
                for t in range(TB):
                    r = pe.matmul(c.ps[7][:, t * P:(t + 1) * P], oT[:, t * P:(t + 1) * P], wo[:],
                                  start=True, stop=True)
                r.then_inc(y_ready, 1)
            for i in range(2):
                pe.wait_ge(o_free[i], 1)
                pe.sem_clear(o_free[i])
                pe.wait_ge(s_free[i], 1)
                pe.sem_clear(s_free[i])
            pe.wait_ge(y_free, 1)
            pe.sem_clear(y_free)
            pe.wait_ge(pre.t_free, 1)
            pe.sem_clear(pre.t_free)
            pe.wait_ge(pre.xT_ready, 1)
            pe.sem_clear(pre.xT_ready)
            pe.wait_ge(pre.xTs_ready, 1)
            pe.sem_clear(pre.xTs_ready)

        @block.scalar
        def _(a):
            st.wait_loads(a)
            pre.seed_act(a)
            pre.act(a, 0)
            with a.Fori(0, B) as b:
                a.wait_ge(tr_ready[0], 1)
                a.sem_clear(tr_ready[0])
                a.activation(qT[:], c.ps[4], ACT.Copy).then_inc(qT_dve, 1)
                a.drain().then_inc(qT_pool, 1)
                for u in range(UN0 + 2):
                    if u == PRE0:
                        pre.act(a, b + 1)
                    if u < UN0:
                        w = width(u % TB)
                        a.wait_ge(m_ready[u % 4], 1)
                        a.sem_clear(m_ready[u % 4])
                        for j in range(HG):
                            e = pr[:, u % 4, j, 0:w]
                            r = a.activation(e, e, ACT.Exp, bias=nm[:, u, j:j + 1])
                        r.then_inc(p_ready[u % 4], 1)
                    if u >= 2 and (u - 2) % TB:
                        a.wait_ge(ht_ps, 1)
                        a.sem_clear(ht_ps)
                        a.activation(hT[:], c.ps[7][0:WIN, :], ACT.Copy).then_inc(ht_ready, 1)
                a.wait_ge(oT_ps, 1)
                a.sem_clear(oT_ps)
                a.activation(oT[:], c.ps[4][:], ACT.Copy).then_inc(oT_ready, 1)

        @block.vector
        def _(v):
            ch = Chain(v, core.lasting_sem("dve_chain"))
            ch.reset()
            st.wait_loads(v)
            v.memset(vh[:], 1.0)
            ch.link(v.memset(va[:], 1.0))
            ch.link(v.tensor_scalar(nw[:, 0, :], nw[:, 0, :], float(HD) ** -0.5, None, ALU.mult))
            ch.link(v.tensor_copy(nwf[:].rearrange("p (a h) d -> p a h d", a=2),
                                  nw[:].unsqueeze(2).broadcast_to((P, 2, H, HD))))
            for i in range(2):
                v.sem_inc(o_free[i], 1)
                v.sem_inc(s_free[i], 1)
            v.sem_inc(y_free, 1)

            def normalise():
                v.wait_ge(qk_ps, 1)
                v.sem_clear(qk_ps)
                ch.link(v.tensor_tensor(raw[:].rearrange("p (t h) d -> p t (h d)", t=TB),
                                        c.psum[:, 0:2, :].rearrange("p a (t n) -> p (a t) n", t=2),
                                        bqk[:].unsqueeze(1).broadcast_to((P, TB, 2 * D)), ALU.add))
                v.sem_inc(s_free[0], 1)
                ch.link(v.tensor_scalar(raw[:], raw[:], CLIP, -CLIP, ALU.min, ALU.max))
                ch.link(v.tensor_tensor(sq[:], raw[:], raw[:], ALU.mult))
                ch.link(v.tensor_reduce(rstd[:, :, 0], sq[:], AX.X, ALU.add))
                v.tensor_scalar(rstd[:], rstd[:], 1.0 / HD, QK_EPS, ALU.mult, ALU.max).then_inc(ms_ready, 1)
                v.wait_ge(v_ps, 1)
                v.sem_clear(v_ps)
                bh = bv[:].rearrange("p (h d) -> p h d", h=H)
                v.tensor_tensor(va[:, :, :, 0:HD], c.ps[2].rearrange("p (t h d) -> p t h d", t=TB, h=H),
                                bh.unsqueeze(1).broadcast_to((P, TB, H, HD)), ALU.add)
                ch.link(v.tensor_tensor(vh[:, 1:TB, :, 0:HD],
                                        c.ps[3][0:WIN, P:].rearrange("p (t h d) -> p t h d", t=TB - 1, h=H),
                                        bh[0:WIN].unsqueeze(1).broadcast_to((WIN, TB - 1, H, HD)), ALU.add))
                v.sem_inc(s_free[1], 1)
                v.sem_inc(v_ready, 1)
                v.wait_ge(rs_ready, 1)
                v.sem_clear(rs_ready)
                ch.link(v.tensor_tensor(raw[:], raw[:], rstd[:].broadcast_to((P, TB * NH, HD)), ALU.mult))
                v.tensor_tensor(qk[:].rearrange("p t a n -> p t (a n)"), raw[:].rearrange("p (t h) d -> p t (h d)", t=TB),
                                nwf[:].rearrange("p h d -> p (h d)").unsqueeze(1).broadcast_to((P, TB, 2 * D)),
                                ALU.mult).then_inc(qk_ready, 1)

            def norm(g):
                i = g % 2
                v.wait_ge(o_ready[i], 1)
                v.sem_clear(o_ready[i])
                ov = c.ps[6 - i][:, 0:UN0 * VW].rearrange("p (t j w) -> p t j w", t=TB, w=VW)
                ch.link(v.reciprocal(rec[:], ov[:, :, :, HD:VW]))
                ch.link(v.tensor_tensor(o[:, :, g * HG:(g + 1) * HG, :], ov[:, :, :, 0:HD],
                                        rec[:].broadcast_to((P, TB, HG, HD)), ALU.mult))
                v.sem_inc(o_free[i], 1)

            pre.dve(v, ch, 0)
            with v.Fori(0, B) as b:
                ch.reset()
                normalise()
                v.wait_ge(tr_ready[1], 1)
                v.sem_clear(tr_ready[1])
                v.tensor_copy(kT[:], c.ps[5]).then_inc(kT_ready, 1)
                v.wait_ge(qT_dve, 1)
                v.sem_clear(qT_dve)
                for h in range(H // 2):
                    r = v.tensor_scalar(qz[:, h, :], qT[:], hm[:, h:h + 1], None, ALU.mult)
                    if h % HG == HG - 1:
                        r.then_inc(qz_ready[0], 1)
                for u in range(UN0 + 3):
                    if u == 4:
                        pre.dve(v, ch, b + 1)
                    if u < UN0:
                        w = width(u % TB)
                        e = pr[:, u % 4, :, 0:w]
                        v.wait_ge(s_ready[u % 2], 1)
                        v.sem_clear(s_ready[u % 2])
                        ch.link(v.tensor_tensor(e, score_slot(u % 2, w),
                                                window[:, SPAN - w:].unsqueeze(1).broadcast_to((P, HG, w)), ALU.add))
                        v.sem_inc(s_free[u % 2], 1)
                        v.tensor_reduce(nm[:, u, :], e, AX.X, ALU.max, negate=True).then_inc(m_ready[u % 4], 1)
                    if 2 <= u < UN0 + 2:
                        v.wait_ge(pt_ps, 1)
                        v.sem_clear(pt_ps)
                        v.tensor_copy(pT[:], c.ps[4][:]).then_inc(pt_ready, 1)
                    if u >= TB + 3 and (u - 3) % TB == 0 and u < UN0 + 3:
                        norm((u - 3) // TB - 1)
                norm(G - 1)
                v.sem_inc(on_ready, 1)
                v.wait_ge(y_ready, 1)
                v.sem_clear(y_ready)
                ch.link(v.tensor_tensor(y[:], c.ps[7].rearrange("p (a b) -> p a b", a=TB),
                                        bo[:].unsqueeze(1).broadcast_to((P, TB, D)), ALU.add))
                v.sem_inc(y_free, 1)
                v.sem_inc(pre.t_free, 1)
                post.dve_stats(v, ch, lambda t: y[:, t, :])
                post.dve_add(v, ch, b, lambda t: y[:, t, :])
            pre.drain_dve(v)
    st.ctx.close()



def stage_attn1(core):
    st = Stage(core, "a1")
    c, nc, s = core, core.nc, core.sem
    wq, wk, wv = (st.load(n, [P, D]) for n in ("wq", "wk", "wv"))
    bq, bk, bv = st.load("bq", [P, 1]), st.load("bk", [P, 1]), st.load("bv", [P, D])
    causal = st.load("causal", [P, P])
    scale = float(D) ** -0.5
    pre, post = Pre(st, static=True), Post(st)
    q, k = st.sb("q", [P, L]), st.sb("k", [P, L])
    vv = st.sb("v", [P, TB, D])
    pr = st.sb("probs", [P, TB, L])
    prT = st.sb("probsT", [P, 2, L])
    nm, den = st.sb("negmax", [P, TB]), st.sb("den", [P, TB])
    y = st.sb("y", [P, TB, D])
    q_ps, k_ps, v_ps = s("q_ps"), s("k_ps"), s("v_ps")
    qk_ready, v_ready = s("qk_ready"), s("v_ready")
    s_ready = [s(f"scores{i}_ready") for i in range(4)]
    m_ready = [s(f"max{i}_ready") for i in range(4)]
    p_ready = [s(f"probs{i}_ready") for i in range(4)]
    pt_ready = [s(f"probsT{i}_ps") for i in range(4)]
    pts_ready = [s(f"probsT{i}_ready") for i in range(4)]
    o_ready, y_free = s("out_ready"), s("out_free")
    with nc.Block() as block:
        @block.sync
        def _(sp):
            st.issue_loads(sp)

        @block.gpsimd
        def _(g):
            ch = Chain(g, core.lasting_sem("pool_chain"))
            ch.reset()
            pre.pool(g, ch, 0)
            with g.Fori(0, B) as b:
                ch.reset()
                pre.pool(g, ch, b + 1)
                post.pool(g, ch)

        @block.tensor
        def _(pe):
            def av(qb):
                pe.wait_ge(pts_ready[qb], 1)
                pe.sem_clear(pts_ready[qb])
                for kb in range(qb + 1):
                    r = pe.matmul(c.ps[6][:, qb * P:(qb + 1) * P], prT[:, qb % 2, kb * P:(kb + 1) * P],
                                  vv[:, kb, :], start=(kb == 0), stop=(kb == qb))
                return r

            st.wait_loads(pe)
            pre.seed_pe(pe)
            pre.pe(pe, 0)
            with pe.Fori(0, B) as b:
                pe.wait_ge(pre.xT_ready, 1)
                pe.sem_clear(pre.xT_ready)
                pe.wait_ge(pre.xTs_ready, 1)
                pe.sem_clear(pre.xTs_ready)
                xb = c.xT[:, bass.ds(b * L, L)]
                pe.matmul(c.ps[0][:], wq[:], xb, start=True, stop=True).then_inc(q_ps, 1)
                pe.matmul(c.ps[1][:], wk[:], xb, start=True, stop=True).then_inc(k_ps, 1)
                for t in range(TB):
                    r = pe.matmul(c.ps[2][:, t * P:(t + 1) * P], pre.xTs[:, t * P:(t + 1) * P], wv[:],
                                  start=True, stop=True)
                r.then_inc(v_ps, 1)
                pe.drain().then_inc(pre.xTs_free, 1)
                pe.wait_ge(qk_ready, 1)
                pe.sem_clear(qk_ready)
                pe.wait_ge(v_ready, 1)
                pe.sem_clear(v_ready)
                for qb in (3, 2, 1, 0):
                    n = (qb + 1) * P
                    pe.matmul(c.ps[qb][:, 0:n], q[:, qb * P:n], k[:, 0:n], start=True,
                              stop=True).then_inc(s_ready[qb], 1)
                pre.pe(pe, b + 1)
                pe.wait_ge(y_free, 1)
                pe.sem_clear(y_free)
                for qb in (3, 2, 1, 0):
                    pe.wait_ge(p_ready[qb], 1)
                    pe.sem_clear(p_ready[qb])
                    for kb in range(qb + 1):
                        r = pe.transpose(c.ps[4 + qb % 2][:, kb * P:(kb + 1) * P],
                                         pr[:, qb, kb * P:(kb + 1) * P], c.ident[:])
                    r.then_inc(pt_ready[qb], 1)
                    if qb < 3:
                        av(qb + 1)
                av(0).then_inc(o_ready, 1)
            pe.wait_ge(y_free, 1)
            pe.sem_clear(y_free)
            pe.wait_ge(pre.t_free, 1)
            pe.sem_clear(pre.t_free)
            pe.wait_ge(pre.xT_ready, 1)
            pe.sem_clear(pre.xT_ready)
            pe.wait_ge(pre.xTs_ready, 1)
            pe.sem_clear(pre.xTs_ready)

        @block.scalar
        def _(a):
            ch = Chain(a, core.lasting_sem("act_chain"))
            ch.reset()
            st.wait_loads(a)
            pre.seed_act(a)
            pre.act(a, 0)
            with a.Fori(0, B) as b:
                ch.reset()
                a.wait_ge(q_ps, 1)
                a.sem_clear(q_ps)
                a.activation(q[:], c.ps[0][:], ACT.Identity, bias=bq[:])
                a.wait_ge(k_ps, 1)
                a.sem_clear(k_ps)
                a.activation(k[:], c.ps[1][:], ACT.Identity, bias=bk[:]).then_inc(qk_ready, 1)
                pre.act(a, b + 1)
                for qb in (3, 2, 1, 0):
                    n = (qb + 1) * P
                    a.wait_ge(m_ready[qb], 1)
                    a.sem_clear(m_ready[qb])
                    a.activation(pr[:, qb, 0:n], c.ps[qb][:, 0:n], ACT.Exp, bias=nm[:, qb:qb + 1], scale=scale,
                                 accum_out=den[:, qb:qb + 1]).then_inc(p_ready[qb], 1)
                    if qb == 2:
                        a.wait_ge(pt_ready[3], 1)
                        a.sem_clear(pt_ready[3])
                        a.activation(prT[:, 1, :], c.ps[5][:], ACT.Copy).then_inc(pts_ready[3], 1)

        @block.vector
        def _(v):
            ch = Chain(v, core.lasting_sem("dve_chain"))
            ch.reset()
            st.wait_loads(v)
            v.sem_inc(y_free, 1)
            pre.dve(v, ch, 0)
            with v.Fori(0, B) as b:
                ch.reset()
                v.wait_ge(v_ps, 1)
                v.sem_clear(v_ps)
                v.tensor_tensor(vv[:], c.ps[2][:].rearrange("p (a b) -> p a b", a=TB),
                                bv[:].unsqueeze(1).broadcast_to((P, TB, D)), ALU.add).then_inc(v_ready, 1)
                pre.dve(v, ch, b + 1)
                for qb in (3, 2, 1, 0):
                    n = (qb + 1) * P
                    v.wait_ge(s_ready[qb], 1)
                    v.sem_clear(s_ready[qb])
                    dg = c.ps[qb][:, qb * P:n]
                    ch.link(v.tensor_tensor(dg, dg, causal[:], ALU.add))
                    ch.link(v.tensor_reduce(nm[:, qb:qb + 1], c.ps[qb][:, 0:n], AX.X, ALU.max, negate=True))
                    v.tensor_scalar(nm[:, qb:qb + 1], nm[:, qb:qb + 1], scale, None, ALU.mult).then_inc(m_ready[qb], 1)
                for qb in (2, 1, 0):
                    n = (qb + 1) * P
                    v.wait_ge(pt_ready[qb], 1)
                    v.sem_clear(pt_ready[qb])
                    v.tensor_copy(prT[:, qb % 2, 0:n], c.ps[4 + qb % 2][:, 0:n]).then_inc(pts_ready[qb], 1)
                v.wait_ge(o_ready, 1)
                v.sem_clear(o_ready)
                ch.link(v.reciprocal(den[:], den[:]))
                for t in range(TB):
                    r = v.tensor_scalar(y[:, t, :], c.ps[6][:, t * P:(t + 1) * P], den[:, t:t + 1], None, ALU.mult)
                ch.link(r)
                v.sem_inc(y_free, 1)
                post.dve_stats(v, ch, lambda t: y[:, t, :])
                post.dve_add(v, ch, b, lambda t: y[:, t, :])
            pre.drain_dve(v)
    st.ctx.close()



LAT = 32


def stage_attn3(core):
    st = Stage(core, "a3")
    c, nc, s = core, core.nc, core.sem
    wq, bqk = st.load("wq", [P, D]), st.load("bqk", [P, 2, D])
    wd, bd = st.load("wd", [P, LAT]), st.load("bd", [LAT, 1])
    wkv, bv = st.load("wkv", [LAT, 2 * D]), st.load("bv", [P, D])
    cos, sin = st.load("cos", [P, TB, HD]), st.load("sin", [P, TB, HD])
    wo, bo = st.load("wo", [P, D]), st.load("bo", [P, D])
    scale = float(HD) ** -0.5
    pre, post = Pre(st, static=True), Post(st)
    lat = st.sb("lat", [LAT, L])
    raw = st.sb("raw", [P, TB, 2, D])
    rot, rot2 = st.sb("rot", [P, TB, 2, D]), st.sb("rot2", [P, TB, 2, D])
    vv = st.sb("v", [P, TB, D])
    prod = st.sb("prod", [P, 2, H * H, HD])
    pv = st.sb("pv", [P, 2, H * HD, H])
    sc = st.sb("scores", [P, 2, H, H])
    nm = st.sb("max", [P, 2, H, 1])
    den = st.sb("den", [P, 2, H, 1])
    o = st.sb("o", [P, TB, H, HD])
    oT, y = st.sb("oT", [P, L]), st.sb("y", [P, TB, D])
    lat_ps, lat_ready = s("lat_ps"), s("lat_ready")
    q_ps, kv_ps = s("q_ps"), s("kv_ps")
    bank_free = s("proj_free")
    rot_ready = s("rot_ready")
    prod_ready = [s(f"prod{i}_ready") for i in range(2)]
    prod_free = [s(f"prod{i}_free") for i in range(2)]
    s_ready = [s(f"scores{i}_ready") for i in range(2)]
    p_ready = [s(f"probs{i}_ready") for i in range(2)]
    p_sum = [s(f"probs{i}_sum") for i in range(2)]
    pv_ready = [s(f"pv{i}_ready") for i in range(2)]
    pv_free = [s(f"pv{i}_free") for i in range(2)]
    on_ready, oT_ps, oT_ready, y_ready = s("on_ready"), s("oT_ps"), s("oT_ready"), s("y_ready")
    y_free = s("y_free")

    with nc.Block() as block:
        @block.sync
        def _(sp):
            st.issue_loads(sp)

        @block.gpsimd
        def _(g):
            ch = Chain(g, core.lasting_sem("pool_chain"))
            ch.reset()

            def scores(t):
                i = t % 2
                g.wait_ge(prod_free[i], 1)
                g.sem_clear(prod_free[i])
                for h in range(0, H, 4):
                    qh = rot[:, t, 0, h * HD:(h + 4) * HD].rearrange("p (h d) -> p h d", d=HD)
                    kk = rot[:, t, 1, :].rearrange("p (g d) -> p g d", d=HD)
                    r = g.tensor_tensor(prod[:, i, h * H:(h + 4) * H, :].rearrange("p (h g) d -> p h g d", h=4),
                                        qh.unsqueeze(2).broadcast_to((P, 4, H, HD)),
                                        kk.unsqueeze(1).broadcast_to((P, 4, H, HD)), ALU.mult)
                r.then_inc(prod_ready[i], 1)

            def values(t):
                i = t % 2
                g.wait_ge(p_ready[i], 1)
                g.sem_clear(p_ready[i])
                g.wait_ge(pv_free[i], 1)
                g.sem_clear(pv_free[i])
                for h in range(0, H, 4):
                    ph = sc[:, i, h:h + 4, :]
                    vt = vv[:, t, :].rearrange("p (g d) -> p d g", d=HD)
                    r = g.tensor_tensor(pv[:, i, h * HD:(h + 4) * HD, :].rearrange("p (h d) g -> p h d g", h=4),
                                        ph.unsqueeze(2).broadcast_to((P, 4, HD, H)),
                                        vt.unsqueeze(1).broadcast_to((P, 4, HD, H)), ALU.mult)
                r.then_inc(pv_ready[i], 1)

            pre.pool(g, ch, 0)
            with g.Fori(0, B) as b:
                ch.reset()
                g.wait_ge(rot_ready, 1)
                g.sem_clear(rot_ready)
                for t in range(TB + 1):
                    if t < TB:
                        scores(t)
                    if t >= 1:
                        values(t - 1)
                    if t == 1:
                        pre.pool(g, ch, b + 1)
                post.pool(g, ch)
            for i in range(2):
                g.wait_ge(prod_free[i], 1)
                g.sem_clear(prod_free[i])
                g.wait_ge(pv_free[i], 1)
                g.sem_clear(pv_free[i])

        @block.tensor
        def _(pe):
            st.wait_loads(pe)
            pre.seed_pe(pe)
            pre.pe(pe, 0)
            with pe.Fori(0, B) as b:
                pe.wait_ge(pre.xT_ready, 1)
                pe.sem_clear(pre.xT_ready)
                pe.wait_ge(pre.xTs_ready, 1)
                pe.sem_clear(pre.xTs_ready)
                pe.wait_ge(bank_free, 1)
                pe.sem_clear(bank_free)
                pe.matmul(c.ps[3][0:LAT, :], wd[:], pre.xTs[:], start=True, stop=True).then_inc(lat_ps, 1)
                for t in range(TB):
                    r = pe.matmul(c.ps[0][:, t * P:(t + 1) * P], pre.xTs[:, t * P:(t + 1) * P], wq[:],
                                  start=True, stop=True)
                r.then_inc(q_ps, 1)
                pe.drain().then_inc(pre.xTs_free, 1)
                pe.wait_ge(lat_ready, 1)
                pe.sem_clear(lat_ready)
                for t in range(TB):
                    r = pe.matmul(c.ps[1 + t // 2][:, (t % 2) * 2 * D:(t % 2 + 1) * 2 * D],
                                  lat[:, t * P:(t + 1) * P], wkv[:], start=True, stop=True)
                r.then_inc(kv_ps, 1)
                pre.pe(pe, b + 1)
                pe.wait_ge(on_ready, 1)
                pe.sem_clear(on_ready)
                for t in range(TB):
                    r = pe.transpose(c.ps[4][:, t * P:(t + 1) * P], o[:, t, :, :].rearrange("p h d -> p (h d)"),
                                     c.ident[:])
                r.then_inc(oT_ps, 1)
                pe.wait_ge(oT_ready, 1)
                pe.sem_clear(oT_ready)
                pe.wait_ge(y_free, 1)
                pe.sem_clear(y_free)
                for t in range(TB):
                    r = pe.matmul(c.ps[5][:, t * P:(t + 1) * P], oT[:, t * P:(t + 1) * P], wo[:],
                                  start=True, stop=True)
                r.then_inc(y_ready, 1)
            pe.wait_ge(bank_free, 1)
            pe.sem_clear(bank_free)
            pe.wait_ge(y_free, 1)
            pe.sem_clear(y_free)
            pe.wait_ge(pre.t_free, 1)
            pe.sem_clear(pre.t_free)
            pe.wait_ge(pre.xT_ready, 1)
            pe.sem_clear(pre.xT_ready)
            pe.wait_ge(pre.xTs_ready, 1)
            pe.sem_clear(pre.xTs_ready)

        @block.scalar
        def _(a):
            st.wait_loads(a)
            pre.seed_act(a)
            pre.act(a, 0)
            with a.Fori(0, B) as b:
                a.wait_ge(lat_ps, 1)
                a.sem_clear(lat_ps)
                a.activation(lat[:], c.ps[3][0:LAT, :], ACT.Identity, bias=bd[:]).then_inc(lat_ready, 1)
                for t in range(TB):
                    if t == 2:
                        pre.act(a, b + 1)
                    i = t % 2
                    a.wait_ge(s_ready[i], 1)
                    a.sem_clear(s_ready[i])
                    a.activation(sc[:, i, :, :], sc[:, i, :, :], ACT.Exp, scale=scale).then_inc(p_ready[i], 1)
                    a.drain().then_inc(p_sum[i], 1)
                a.wait_ge(oT_ps, 1)
                a.sem_clear(oT_ps)
                a.activation(oT[:], c.ps[4][:], ACT.Copy).then_inc(oT_ready, 1)

        @block.vector
        def _(v):
            ch = Chain(v, core.lasting_sem("dve_chain"))
            ch.reset()
            st.wait_loads(v)
            for i in range(2):
                v.sem_inc(prod_free[i], 1)
                v.sem_inc(pv_free[i], 1)
            v.sem_inc(bank_free, 1)
            v.sem_inc(y_free, 1)

            def rotate():
                v.wait_ge(q_ps, 1)
                v.sem_clear(q_ps)
                v.tensor_tensor(raw[:, :, 0, :], c.ps[0].rearrange("p (t n) -> p t n", t=TB),
                                bqk[:, 0, :].unsqueeze(1).broadcast_to((P, TB, D)), ALU.add)
                v.wait_ge(kv_ps, 1)
                v.sem_clear(kv_ps)
                kv = c.psum[:, 1:3, :].rearrange("p a (t n) -> p (a t) n", t=2)
                v.tensor_tensor(vv[:], kv[:, :, D:], bv[:].unsqueeze(1).broadcast_to((P, TB, D)), ALU.add)
                ch.link(v.tensor_tensor(raw[:, :, 1, :], kv[:, :, 0:D],
                                        bqk[:, 1, :].unsqueeze(1).broadcast_to((P, TB, D)), ALU.add))
                v.sem_inc(bank_free, 1)
                half = HD // 2
                for t in range(TB):
                    x = raw[:, t, :, :].rearrange("p a (h d) -> p (a h) d", d=HD)
                    x1 = rot[:, t, :, :].rearrange("p a (h d) -> p (a h) d", d=HD)
                    x2 = rot2[:, t, :, :].rearrange("p a (h d) -> p (a h) d", d=HD)
                    v.tensor_tensor(x1, x, cos[:, t, :].unsqueeze(1).broadcast_to((P, 2 * H, HD)), ALU.mult)
                    v.tensor_tensor(x2[:, :, 0:half], x[:, :, half:HD],
                                    sin[:, t, 0:half].unsqueeze(1).broadcast_to((P, 2 * H, half)), ALU.mult)
                    r = v.tensor_tensor(x2[:, :, half:HD], x[:, :, 0:half],
                                        sin[:, t, half:HD].unsqueeze(1).broadcast_to((P, 2 * H, half)), ALU.mult)
                ch.link(r)
                ch.link(v.tensor_tensor(rot[:], rot[:], rot2[:], ALU.add))
                v.sem_inc(rot_ready, 1)

            def scores(t):
                i = t % 2
                v.wait_ge(prod_ready[i], 1)
                v.sem_clear(prod_ready[i])
                ch.link(v.tensor_reduce(sc[:, i, :, :].rearrange("p h g -> p (h g)"), prod[:, i, :, :], AX.X, ALU.add))
                v.sem_inc(prod_free[i], 1)
                ch.link(v.tensor_reduce(nm[:, i, :, 0], sc[:, i, :, :], AX.X, ALU.max))
                v.tensor_tensor(sc[:, i, :, :], sc[:, i, :, :], nm[:, i, :, :].broadcast_to((P, H, H)),
                                ALU.subtract).then_inc(s_ready[i], 1)

            def values(t):
                i = t % 2
                v.wait_ge(p_sum[i], 1)
                v.sem_clear(p_sum[i])
                ch.link(v.tensor_reduce(den[:, i, :, 0], sc[:, i, :, :], AX.X, ALU.add))
                ch.link(v.reciprocal(den[:, i, :, :], den[:, i, :, :]))
                v.wait_ge(pv_ready[i], 1)
                v.sem_clear(pv_ready[i])
                ch.link(v.tensor_reduce(o[:, t, :, :].rearrange("p h d -> p (h d)"), pv[:, i, :, :], AX.X, ALU.add))
                v.sem_inc(pv_free[i], 1)
                ch.link(v.tensor_tensor(o[:, t, :, :], o[:, t, :, :], den[:, i, :, :].broadcast_to((P, H, HD)),
                                        ALU.mult))

            pre.dve(v, ch, 0)
            with v.Fori(0, B) as b:
                ch.reset()
                rotate()
                for t in range(TB + 1):
                    if t < TB:
                        scores(t)
                    if t == 1:
                        pre.dve(v, ch, b + 1)
                    if t >= 1:
                        values(t - 1)
                v.sem_inc(on_ready, 1)
                v.wait_ge(y_ready, 1)
                v.sem_clear(y_ready)
                ch.link(v.tensor_tensor(y[:], c.ps[5].rearrange("p (a b) -> p a b", a=TB),
                                        bo[:].unsqueeze(1).broadcast_to((P, TB, D)), ALU.add))
                v.sem_inc(y_free, 1)
                post.dve_stats(v, ch, lambda t: y[:, t, :])
                post.dve_add(v, ch, b, lambda t: y[:, t, :])
            pre.drain_dve(v)
    st.ctx.close()



DH, NPAIR = 64, 8
NU = 2 * TB
LEVELS = 7
KCONV = 4
TURNS = B * NPAIR
DELTA_EPS = 1e-6
RANK = 64
WCOLS = 5 * P + 3


def stage_delta_in(core):
    st = Stage(core, "d")
    c, nc, s = core, core.nc, core.sem
    gamma, cw, cb = st.load("gamma", [P, 1]), st.load("cw", [P, KCONV]), st.load("cb", [P, 1])
    bw, bb = st.load("betaw", [P, 2 * NPAIR]), st.load("betab", [P, 2 * NPAIR])
    pre = Pre(st, inner="rms", eps=DELTA_EPS)
    pad = KCONV - 1
    hp = st.sb("hp", [P, pad + L])
    cv = st.sb("cv", [P, 2, L])
    hs = st.sb("hs", [P, L])
    bt = st.sb("bt", [P, TB, 2 * NPAIR])
    t_ready, t_free = s("pre_t_ready"), s("pre_t_free")
    hp_ready, cv_ready, hs_ready, hs_free = s("conv_in_ready"), s("conv_ready"), s("hs_ready"), s("hs_free")
    b_ps, b_ready, b_done, bank_free = s("beta_ps"), s("beta_ready"), s("beta_done"), s("beta_bank_free")
    with nc.Block() as block:
        @block.sync
        def _(sp):
            st.issue_loads(sp)

        @block.gpsimd
        def _(g):
            ch = Chain(g, core.lasting_sem("pool_chain"))
            with g.Fori(0, B) as b:
                ch.reset()
                pre.pool(g, ch, b)

        @block.tensor
        def _(pe):
            st.wait_loads(pe)
            pe.sem_inc(pre.y_free, 1)
            pe.sem_inc(hs_free, 1)
            with pe.Fori(0, B) as b:
                pe.wait_ge(pre.y_ready, 1)
                pe.sem_clear(pre.y_ready)
                pe.wait_ge(t_free, 1)
                pe.sem_clear(t_free)
                for t in range(TB):
                    r = pe.transpose(c.ps[7][:, t * P:(t + 1) * P], pre.y2[:, t, :], c.ident[:])
                r.then_inc(t_ready, 1)
                pe.drain().then_inc(pre.y_free, 1)
                pe.wait_ge(hs_ready, 1)
                pe.sem_clear(hs_ready)
                pe.wait_ge(bank_free, 1)
                pe.sem_clear(bank_free)
                for t in range(TB):
                    r = pe.matmul(c.ps[6][:, t * 2 * NPAIR:(t + 1) * 2 * NPAIR], hs[:, t * P:(t + 1) * P], bw[:],
                                  start=True, stop=True)
                r.then_inc(b_ps, 1)
                pe.drain().then_inc(hs_free, 1)
            pe.wait_ge(t_free, 1)
            pe.sem_clear(t_free)
            pe.wait_ge(bank_free, 1)
            pe.sem_clear(bank_free)

        @block.scalar
        def _(a):
            ch = Chain(a, core.lasting_sem("act_chain"))
            st.wait_loads(a)
            a.sem_inc(t_free, 1)
            with a.Fori(0, B) as b:
                ch.reset()
                a.wait_ge(t_ready, 1)
                a.sem_clear(t_ready)
                a.activation(hp[:, pad:], c.ps[7], ACT.Identity, scale=gamma[:]).then_inc(hp_ready, 1)
                a.drain().then_inc(t_free, 1)
                a.wait_ge(cv_ready, 1)
                a.sem_clear(cv_ready)
                a.wait_ge(hs_free, 1)
                a.sem_clear(hs_free)
                a.activation(c.xT[:, bass.ds(b * L, L)], cv[:, 1, :], ACT.Silu, bias=cb[:])
                a.activation(hs[:], cv[:, 1, :], ACT.Silu, bias=cb[:]).then_inc(hs_ready, 1)
                a.wait_ge(b_ready, 1)
                a.sem_clear(b_ready)
                ch.link(a.activation(c.beta[:, :, bass.ds(b * TB, TB), :],
                                     bt[:].rearrange("p t (a h) -> p a t h", h=2), ACT.Sigmoid))
                a.sem_inc(b_done, 1)
            a.wait_ge(hs_free, 1)
            a.sem_clear(hs_free)

        @block.vector
        def _(v):
            ch = Chain(v, core.lasting_sem("dve_chain"))
            ch.reset()
            st.wait_loads(v)
            ch.link(v.memset(hp[:], 0.0))
            v.sem_inc(bank_free, 1)
            with v.Fori(0, B) as b:
                ch.reset()
                pre.dve(v, ch, b)
                v.wait_ge(hp_ready, 1)
                v.sem_clear(hp_ready)
                ch.link(v.tensor_scalar(cv[:, 0, :], hp[:, 0:L], cw[:, 0:1], None, ALU.mult))
                for k in range(1, KCONV):
                    r = v.scalar_tensor_tensor(cv[:, k % 2, :], hp[:, k:k + L], cw[:, k:k + 1],
                                               cv[:, (k + 1) % 2, :], ALU.mult, ALU.add)
                    ch.link(r)
                v.sem_inc(cv_ready, 1)
                v.wait_ge(b_ps, 1)
                v.sem_clear(b_ps)
                ch.link(v.tensor_tensor(bt[:], c.ps[6][:, 0:TB * 2 * NPAIR].rearrange("p (t h) -> p t h", t=TB),
                                        bb[:].unsqueeze(1).broadcast_to((P, TB, 2 * NPAIR)), ALU.add))
                v.sem_inc(bank_free, 1)
                v.sem_inc(b_ready, 1)
                v.wait_ge(b_done, 1)
                v.sem_clear(b_done)
            v.wait_ge(pre.y_free, 1)
            v.sem_clear(pre.y_free)
            v.memset(c.xn[:], 0.0)
    st.ctx.close()


def stage_delta(core):
    st = Stage(core, "e")
    c, nc, s = core, core.nc, core.sem
    sb, load = st.sb, st.load
    low = load("low", [P, LEVELS, DH])
    lowi = sb("lowi", [P, LEVELS, DH], I32)
    heads2 = load("heads2", [P, P])
    ow = load("ow", [P, NPAIR, D])
    W = sb("w", [P, WCOLS])
    hn = sb("hn", [P, 1])
    hs = sb("hs", [P, L])
    sq, rn = sb("sq", [P, 2, L]), sb("rn", [P, 2, L])
    k, kq = sb("k", [P, L]), sb("kq", [P, 2, L])
    be = sb("be", [P, L])
    pr, su = sb("pre", [P, L]), sb("suf", [P, L])
    ks, kp = sb("ks", [P, 2, L]), sb("kp", [P, 2, TB, 2, DH])
    N = sb("N", [P, LEVELS, NU * P])
    Z = sb("Z", [P, LEVELS, NU * P])
    T, TT, AT = sb("T", [P, NU * P]), sb("TT", [P, NU * P]), sb("AT", [P, NU * P])
    kqb, ke, ket = sb("kqb", [P, 2, L]), sb("ke", [P, L]), sb("ket", [P, TB, P])
    bv, tot = sb("bv", [P, TB, P]), sb("tot", [P, TB])
    S, R, U = sb("S", [P, P]), sb("R", [P, P]), sb("U", [P, P])
    ysb, ysq = sb("ysb", [P, TB, P]), sb("ysq", [P, TB, P])
    ms = sb("ms", [P, NU])
    yT = sb("yT", [P, L])
    w_ready, w_free = s("w_ready"), s("w_free")
    hs_ready, hs_free = s("hs_ready"), s("hs_free")
    qk_ps, a_ps, be_ps, v_ps = s("qk_ps"), s("alpha_ps"), s("beta_ps"), s("v_ps")
    sq_ready, ss_ps, rn_ready = s("sq_ready"), s("ss_ps"), s("root_ready")
    al_ready = s("alpha_ready")
    kq_ready, kq_pe = s("kq_ready"), s("kq_to_pe")
    lv_ready = [s(f"scaled{i}_ready") for i in range(2)]
    lv_free = [s(f"scaled{i}_free") for i in range(2)]
    gr_ps, gr_free = s("gram_ps"), s("gram_free")
    n_ready = [s(f"N{i}_ready") for i in range(2)]
    z_ps, z_ready = s("Z_ps"), s("Z_ready")
    t_ps, t_ready = s("T_ps"), s("T_ready")
    chain_in, ke_ps, ket_ready = s("chain_in"), s("ke_ps"), s("ket_ready")
    p_ps, r_ready, u_ps, u_ready = s("P_ps"), s("R_ready"), s("U_ps"), s("U_ready")
    s_ps, s_ready, o_ps = s("S_ps"), s("S_ready"), s("O_ps")
    ysq_ready, ms_ready, rs_ready = s("ysq_ready"), s("head_ms_ready"), s("head_rstd_ready")
    ys_ready, yT_ps, yT_ready = s("ys_ready"), s("yT_ps"), s("yT_ready")
    out_ps, out_free = s("out_ps"), s("out_free")

    def odd(ap, m):
        return ap.rearrange("p (b c) -> p b c", c=2 * m)[:, :, m:2 * m]

    def even(ap, m):
        return ap.rearrange("p (b c) -> p b c", c=2 * m)[:, :, 0:m]

    def packed(ap, m):
        return ap.rearrange("p (b c) -> p b c", c=m)

    def unit(ap, u):
        return ap[:, u * P:(u + 1) * P]

    def rows_of(hd):
        return slice(hd * DH, (hd + 1) * DH)

    with nc.Block() as block:
        @block.sync
        def _(sp):
            st.issue_loads(sp)
            with sp.Fori(0, TURNS) as i:
                sp.wait_ge(w_free, 2)
                sp.sem_clear(w_free)
                sp.dma_start(W[:], c.A["e_w"][bass.ds((i // B) * P, P), :]).then_inc(w_ready, 16)
            sp.wait_ge(w_free, 2)
            sp.sem_clear(w_free)

        @block.gpsimd
        def _(g):
            ch = Chain(g, core.lasting_sem("pool_chain"))
            g.memset(N[:], 0.0)
            g.memset(ks[:], 0.0)
            with g.Fori(0, TURNS) as i:
                ch.reset()
                g.wait_ge(hs_free, 1)
                g.sem_clear(hs_free)
                g.tensor_copy(hs[:], c.xT[:, bass.ds((i % B) * L, L)]).then_inc(hs_ready, 1)
                g.wait_ge(al_ready, 1)
                g.sem_clear(al_ready)
                g.wait_ge(kq_ready, 1)
                g.sem_clear(kq_ready)
                for l in range(LEVELS):
                    m = 1 << l
                    if l >= 2:
                        g.wait_ge(lv_free[l % 2], 1)
                        g.sem_clear(lv_free[l % 2])
                    if l == 0:
                        g.tensor_copy(even(ks[:, 0, :], m), even(k[:], m))
                    else:
                        g.tensor_tensor(even(ks[:, l % 2, :], m), even(k[:], m), even(su[:], m), ALU.mult)
                    for n in range(2):
                        four = lambda ap: ap.rearrange("p (t b c) -> p t b c", t=TB, c=2 * m)[:, :, :, m:2 * m]
                        r = g.tensor_tensor(kp[:, l % 2, :, n, :].rearrange("p t (b c) -> p t b c", c=m),
                                            four(kq[:, n, :]), four(pr[:]), ALU.mult)
                    ch.link(r)
                    g.sem_inc(lv_ready[l % 2], 1)
                    nb = L // (2 * m)
                    tail_odd = odd(pr[:], m)[:, :, m - 1:m].broadcast_to((P, nb, m))
                    tail_even = even(pr[:], m)[:, :, m - 1:m].broadcast_to((P, nb, m))
                    if l == 0:
                        ch.link(g.memset(su[:], 1.0))
                        ch.link(g.tensor_copy(even(su[:], m), tail_odd))
                    else:
                        ch.link(g.tensor_tensor(even(su[:], m), even(su[:], m), tail_odd, ALU.mult))
                    ch.link(g.tensor_tensor(odd(pr[:], m), odd(pr[:], m), tail_even, ALU.mult))
                for n in range(2):
                    g.tensor_tensor(kqb[:, n, :], kq[:, n, :], pr[:], ALU.mult)
                g.tensor_copy(tot[:], pr[:].rearrange("p (t n) -> p t n", t=TB)[:, :, P - 1])
                g.tensor_tensor(ke[:], k[:], su[:], ALU.mult).then_inc(chain_in, 1)
                g.wait_ge(lv_free[0], 1)
                g.sem_clear(lv_free[0])
                g.wait_ge(lv_free[1], 1)
                g.sem_clear(lv_free[1])
                g.wait_ge(ms_ready, 1)
                g.sem_clear(ms_ready)
                ch.link(g.tensor_scalar(ms[:], ms[:], 1.0 / DH, DELTA_EPS, ALU.mult, ALU.add))
                g.tensor_tensor(ms[:], ms[:], c.mhalf[:, 0:NU], ALU.pow).then_inc(rs_ready, 1)
            g.wait_ge(hs_free, 1)
            g.sem_clear(hs_free)

        @block.tensor
        def _(pe):
            st.wait_loads(pe)
            pe.sem_inc(hs_free, 1)
            pe.sem_inc(w_free, 1)

            def gram(l):
                pe.wait_ge(gr_free, 1)
                pe.sem_clear(gr_free)
                pe.wait_ge(lv_ready[l % 2], 1)
                pe.sem_clear(lv_ready[l % 2])
                for hd in range(2):
                    for t in range(TB):
                        r = pe.matmul(c.ps[hd][:, t * P:(t + 1) * P], ks[rows_of(hd), l % 2, t * P:(t + 1) * P],
                                      kp[rows_of(hd), l % 2, t, :, :].rearrange("p n j -> p (n j)"),
                                      start=True, stop=True)
                r.then_inc(gr_ps, 1)
                pe.drain().then_inc(lv_free[l % 2], 1)

            with pe.Fori(0, TURNS) as i:
                pe.wait_ge(hs_ready, 1)
                pe.sem_clear(hs_ready)
                pe.wait_ge(w_ready, 16)
                pe.sem_clear(w_ready)
                pe.wait_ge(out_free, 1)
                pe.sem_clear(out_free)
                for n in range(4):
                    r = pe.matmul(c.ps[n][:], W[:, n * P:(n + 1) * P], hs[:], start=True, stop=True)
                    if n:
                        r.then_inc((None, qk_ps, a_ps, be_ps)[n], 1)
                for t in range(TB):
                    r = pe.matmul(c.ps[4][:, t * P:(t + 1) * P], hs[:, t * P:(t + 1) * P], W[:, 4 * P:5 * P],
                                  start=True, stop=True)
                r.then_inc(v_ps, 1)
                pe.drain().then_inc(w_free, 1)
                pe.sem_inc(hs_free, 1)
                pe.wait_ge(sq_ready, 1)
                pe.sem_clear(sq_ready)
                for n in range(2):
                    r = pe.matmul(c.ps[5 + n][:], heads2[:], sq[:, n, :], start=True, stop=True)
                r.then_inc(ss_ps, 1)
                pe.wait_ge(kq_pe, 1)
                pe.sem_clear(kq_pe)
                for hd in range(2):
                    for t in range(TB):
                        cols = slice(t * P, (t + 1) * P)
                        r = pe.matmul(c.ps[hd][:, cols], k[rows_of(hd), cols], kq[rows_of(hd), 1, cols],
                                      start=True, stop=True)
                r.then_inc(gr_ps, 1)
                gram(0)
                for l in range(LEVELS):
                    m = 1 << l
                    if l + 1 < LEVELS:
                        gram(l + 1)
                    pe.wait_ge(n_ready[l % 2], 1)
                    pe.sem_clear(n_ready[l % 2])
                    if l:
                        pe.wait_ge(t_ready, 1)
                        pe.sem_clear(t_ready)
                    for u in range(NU):
                        r = pe.matmul(packed(c.ps[2][:, u * DH:(u + 1) * DH], m), unit(N[:, l, :], u), even(unit(T, u), m),
                                      start=True, stop=True)
                    r.then_inc(z_ps, 1)
                    pe.wait_ge(z_ready, 1)
                    pe.sem_clear(z_ready)
                    if l + 1 < LEVELS:
                        for u in range(NU):
                            pe.matmul(packed(c.ps[3][:, u * DH:(u + 1) * DH], m), unit(TT, u), even(unit(Z[:, l, :], u), m),
                                      start=True, stop=True)
                    for u in range(NU):
                        r = pe.matmul(packed(c.ps[4][:, u * DH:(u + 1) * DH], m), unit(Z[:, l, :], u), odd(unit(TT, u), m),
                                      start=True, stop=True)
                    r.then_inc(t_ps, 1)
                pe.wait_ge(chain_in, 1)
                pe.sem_clear(chain_in)
                for t in range(TB):
                    r = pe.transpose(c.ps[7][:, t * P:(t + 1) * P], ke[:, t * P:(t + 1) * P], c.ident[:])
                r.then_inc(ke_ps, 1)
                pe.wait_ge(t_ready, 1)
                pe.sem_clear(t_ready)
                pe.wait_ge(gr_free, 1)
                pe.sem_clear(gr_free)
                pe.wait_ge(ket_ready, 1)
                pe.sem_clear(ket_ready)
                for t in range(TB):
                    cols = slice(t * P, (t + 1) * P)
                    if t:
                        pe.wait_ge(s_ready, 1)
                        pe.sem_clear(s_ready)
                        pe.matmul(c.ps[5][:, 0:P], kqb[:, 0, cols], S[:], start=True, stop=True).then_inc(p_ps, 1)
                        pe.matmul(c.ps[6][:, cols], kqb[:, 1, cols], S[:], start=True, stop=False,
                                  skip_group_check=True)
                        pe.wait_ge(r_ready, 1)
                        pe.sem_clear(r_ready)
                    for hd in range(2):
                        r = pe.matmul(c.ps[5][:, P + hd * DH:P + (hd + 1) * DH], unit(TT, hd * TB + t),
                                      (R if t else bv[:, 0, :])[:, rows_of(hd)], start=True, stop=True)
                    r.then_inc(u_ps, 1)
                    pe.wait_ge(u_ready, 1)
                    pe.sem_clear(u_ready)
                    if t + 1 < TB:
                        pe.matmul(c.ps[7][:, 0:P], ket[:, t, :], U[:], start=True, stop=True).then_inc(s_ps, 1)
                    for hd in range(2):
                        r = pe.matmul(c.ps[6][:, t * P + hd * DH:t * P + (hd + 1) * DH], unit(AT, hd * TB + t),
                                      U[:, rows_of(hd)], start=(t == 0), stop=(t == 0 or hd == 1), skip_group_check=True)
                r.then_inc(o_ps, 1)
                pe.wait_ge(ys_ready, 1)
                pe.sem_clear(ys_ready)
                for t in range(TB):
                    r = pe.transpose(c.ps[1][:, t * P:(t + 1) * P], ysb[:, t, :], c.ident[:])
                r.then_inc(yT_ps, 1)
                pe.wait_ge(yT_ready, 1)
                pe.sem_clear(yT_ready)
                for t in range(TB):
                    r = pe.matmul(c.ps[0][:, t * P:(t + 1) * P], yT[:, t * P:(t + 1) * P],
                                  ow[:, bass.ds(i // B, 1), :].rearrange("p o d -> p (o d)"), start=True, stop=True)
                r.then_inc(out_ps, 1)
            pe.wait_ge(out_free, 1)
            pe.sem_clear(out_free)

        @block.scalar
        def _(a):
            ch = Chain(a, core.lasting_sem("act_chain"))
            a.sem_inc(w_free, 1)
            with a.Fori(0, TURNS) as i:
                ch.reset()
                a.wait_ge(qk_ps, 1)
                a.sem_clear(qk_ps)
                a.activation(sq[:], c.psum[:, 0:2, :], ACT.Square).then_inc(sq_ready, 1)
                a.wait_ge(a_ps, 1)
                a.sem_clear(a_ps)
                a.activation(pr[:], c.ps[2][:], ACT.Sigmoid, bias=W[:, 5 * P:5 * P + 1]).then_inc(al_ready, 1)
                a.wait_ge(be_ps, 1)
                a.sem_clear(be_ps)
                a.activation(be[:], c.ps[3][:], ACT.Sigmoid, bias=W[:, 5 * P + 1:5 * P + 2])
                a.activation(hn[:], W[:, 5 * P + 2:5 * P + 3], ACT.Copy)
                a.drain().then_inc(w_free, 1)
                a.wait_ge(ss_ps, 1)
                a.sem_clear(ss_ps)
                a.activation(rn[:], c.psum[:, 5:7, :], ACT.Sqrt).then_inc(rn_ready, 1)
                for l in range(LEVELS):
                    m = 1 << l
                    a.wait_ge(z_ps, 1)
                    a.sem_clear(z_ps)
                    a.activation(even(Z[:, l, :], m), packed(c.ps[2][:], m), ACT.Copy).then_inc(z_ready, 1)
                a.wait_ge(ke_ps, 1)
                a.sem_clear(ke_ps)
                a.activation(flat(ket), c.ps[7][:], ACT.Copy).then_inc(ket_ready, 1)
                for t in range(TB):
                    a.wait_ge(u_ps, 1)
                    a.sem_clear(u_ps)
                    a.activation(U[:], c.ps[5][:, P:2 * P], ACT.Copy).then_inc(u_ready, 1)
                a.wait_ge(o_ps, 1)
                a.sem_clear(o_ps)
                a.activation(flat(ysq), c.ps[6][:], ACT.Square).then_inc(ysq_ready, 1)
                a.wait_ge(yT_ps, 1)
                a.sem_clear(yT_ps)
                a.activation(yT[:], c.ps[1][:], ACT.Copy, scale=hn[:]).then_inc(yT_ready, 1)

        @block.vector
        def _(v):
            ch = Chain(v, core.lasting_sem("dve_chain"))
            ch.reset()
            v.sem_inc(out_free, 1)
            v.memset(Z[:], 0.0)
            v.memset(S[:], 0.0)
            st.wait_loads(v)
            ch.link(v.tensor_copy(lowi[:], low[:]))

            def level_in(l):
                m = 1 << l
                nb = DH // m
                v.wait_ge(gr_ps, 1)
                v.sem_clear(gr_ps)
                gr = c.psum[:, 0:2, :].rearrange("p a (t n b c) -> p (a t) n b c", n=2, t=TB, c=m)
                wide = lambda ap: ap.rearrange("p (b c) -> p b c", c=m).unsqueeze(1).broadcast_to((P, NU, nb, m))
                cols = lambda ap: ap.rearrange("p (u b c) -> p u b c", u=NU, c=2 * m)[:, :, :, m:2 * m]
                v.tensor_tensor(cols(N[:, l, :]), gr[:, :, 0], wide(low[:, l, :]), ALU.mult).then_inc(n_ready[l % 2], 1)
                ch.link(v.copy_predicated(cols(AT[:]), wide(lowi[:, l, :]), gr[:, :, 1]))
                v.sem_inc(gr_free, 1)

            with v.Fori(0, TURNS) as i:
                ch.reset()
                v.wait_ge(v_ps, 1)
                v.sem_clear(v_ps)
                beta = flat(c.beta[:, :, :, :].rearrange("p a t h -> p a (t h)"))[:, bass.ds((i // B) * 2 * NT + (i % B) * 2 * TB, 2 * TB)]
                v.tensor_tensor(bv[:].rearrange("p t (h d) -> p (t h) d", h=2),
                                c.ps[4].rearrange("p (u d) -> p u d", d=DH),
                                beta.unsqueeze(2).broadcast_to((P, NU, DH)), ALU.mult)
                v.tensor_copy(T[:].rearrange("p (u n) -> p u n", u=NU), c.ident[:].unsqueeze(1).broadcast_to((P, NU, P)))
                ch.link(v.tensor_copy(TT[:].rearrange("p (u n) -> p u n", u=NU), c.ident[:].unsqueeze(1).broadcast_to((P, NU, P))))
                v.wait_ge(rn_ready, 1)
                v.sem_clear(rn_ready)
                ch.link(v.tensor_scalar(rn[:], rn[:], DELTA_EPS, None, ALU.add))
                ch.link(v.reciprocal(rn[:], rn[:]))
                v.tensor_tensor(kq[:, 1, :], c.ps[0][:], rn[:, 0, :], ALU.mult)
                ch.link(v.tensor_tensor(k[:], c.ps[1][:], rn[:, 1, :], ALU.mult))
                ch.link(v.tensor_tensor(kq[:, 0, :], k[:], be[:], ALU.mult))
                v.sem_inc(kq_ready, 1)
                v.sem_inc(kq_pe, 1)
                v.wait_ge(gr_ps, 1)
                v.sem_clear(gr_ps)
                ch.link(v.tensor_tensor(AT[:].rearrange("p (u n) -> p u n", u=NU),
                                        c.psum[:, 0:2, :].rearrange("p a (t n) -> p (a t) n", t=TB),
                                        c.ident[:].unsqueeze(1).broadcast_to((P, NU, P)), ALU.mult))
                v.sem_inc(gr_free, 1)
                level_in(0)
                for l in range(LEVELS):
                    m = 1 << l
                    if l + 1 < LEVELS:
                        level_in(l + 1)
                    v.wait_ge(t_ps, 1)
                    v.sem_clear(t_ps)
                    if l + 1 < LEVELS:
                        v.tensor_tensor(even(T[:], m), even(T[:], m), packed(c.ps[3][:], m), ALU.subtract)
                    ch.link(v.tensor_tensor(odd(TT[:], m), odd(TT[:], m), packed(c.ps[4][:], m), ALU.subtract))
                    v.sem_inc(t_ready, 1)
                for t in range(TB):
                    if t:
                        v.wait_ge(p_ps, 1)
                        v.sem_clear(p_ps)
                        v.tensor_tensor(R[:], bv[:, t, :], c.ps[5][:, 0:P], ALU.subtract).then_inc(r_ready, 1)
                    if t + 1 < TB:
                        v.wait_ge(s_ps, 1)
                        v.sem_clear(s_ps)
                        for hd in range(2):
                            blk = (rows_of(hd), rows_of(hd))
                            ps = c.psum[rows_of(hd), 7, rows_of(hd)]
                            if t:
                                r = v.scalar_tensor_tensor(S[blk], S[blk], tot[rows_of(hd), t:t + 1], ps, ALU.mult, ALU.add)
                            else:
                                r = v.tensor_copy(S[blk], ps)
                        ch.link(r)
                        v.sem_inc(s_ready, 1)
                v.wait_ge(ysq_ready, 1)
                v.sem_clear(ysq_ready)
                v.tensor_reduce(ms[:], ysq[:].rearrange("p t (h d) -> p (t h) d", h=2), AX.X, ALU.add).then_inc(ms_ready, 1)
                v.wait_ge(rs_ready, 1)
                v.sem_clear(rs_ready)
                v.tensor_tensor(ysb[:].rearrange("p t (h d) -> p (t h) d", h=2),
                                c.ps[6].rearrange("p (u d) -> p u d", d=DH),
                                ms[:].unsqueeze(2).broadcast_to((P, NU, DH)), ALU.mult).then_inc(ys_ready, 1)
                v.wait_ge(out_ps, 1)
                v.sem_clear(out_ps)
                acc = c.xn[:, bass.ds((i % B) * TB, TB), :]
                ch.link(v.tensor_tensor(acc, acc, c.ps[0].rearrange("p (t d) -> p t d", t=TB), ALU.add))
                v.sem_inc(out_free, 1)
    st.ctx.close()


FF = 512


def stage_delta_out(core):
    st = Stage(core, "g")
    c, nc, s = core, core.nc, core.sem
    u1, u1b = st.load("u1", [P, RANK]), st.load("u1b", [RANK, 1])
    u2, u2b = st.load("u2", [RANK, D]), st.load("u2b", [P, D])
    w1, w3, w2 = st.load("w1", [P, FF]), st.load("w3", [P, FF]), st.load("w2", [P, FF // P, D])
    gamma = st.load("gamma", [P, 1])
    pre, post = Pre(st, static=True), Post(st)
    norm = Norm(st, "inner", DELTA_EPS, rms=True)
    yk, y2 = st.sb("y", [P, TB, D]), st.sb("y2", [P, TB, D])
    g1, gs = st.sb("g1", [RANK, L]), st.sb("gate", [P, TB, D])
    y2T, sl, hid = st.sb("y2T", [P, L]), st.sb("silu", [P, 2, L]), st.sb("hid", [P, FF // P, L])
    g1_ps, g1_ready, g2_ps = s("g1_ps"), s("g1_ready"), s("g2_ps")
    gs_ready, gate_ready = s("gs_ready"), s("gate_ready")
    y2_ready, y2_ps, y2T_ready = s("y2_ready"), s("y2T_ps"), s("y2T_ready")
    a_ps = [s(f"bank{i}_ready") for i in range(2)]
    b_ps = [s(f"bank{i + 2}_ready") for i in range(2)]
    sl_ready = [s(f"silu{i}_ready") for i in range(2)]
    h_free = [s(f"bank{i}_free") for i in range(2)]
    hid_ready, y_ready, y_free = s("hid_ready"), s("y_ready"), s("y_free")
    with nc.Block() as block:
        @block.sync
        def _(sp):
            st.issue_loads(sp)

        @block.gpsimd
        def _(g):
            ch = Chain(g, core.lasting_sem("pool_chain"))
            ch.reset()
            pre.pool(g, ch, 0)
            with g.Fori(0, B) as b:
                ch.reset()
                norm.pool_rstd(g, ch)
                pre.pool(g, ch, b + 1)
                post.pool(g, ch)

        @block.tensor
        def _(pe):
            st.wait_loads(pe)
            pre.seed_pe(pe)
            pre.pe(pe, 0)
            with pe.Fori(0, B) as b:
                pe.wait_ge(pre.xT_ready, 1)
                pe.sem_clear(pre.xT_ready)
                pe.wait_ge(pre.xTs_ready, 1)
                pe.sem_clear(pre.xTs_ready)
                pe.matmul(c.ps[0][0:RANK, :], u1[:], pre.xTs[:], start=True, stop=True).then_inc(g1_ps, 1)
                pe.drain().then_inc(pre.xTs_free, 1)
                pe.wait_ge(g1_ready, 1)
                pe.sem_clear(g1_ready)
                for t in range(TB):
                    r = pe.matmul(c.ps[1][:, t * P:(t + 1) * P], g1[:, t * P:(t + 1) * P], u2[:], start=True, stop=True)
                r.then_inc(g2_ps, 1)
                pe.wait_ge(y2_ready, 1)
                pe.sem_clear(y2_ready)
                for t in range(TB):
                    r = pe.transpose(c.ps[2][:, t * P:(t + 1) * P], y2[:, t, :], c.ident[:])
                r.then_inc(y2_ps, 1)
                pe.wait_ge(y2T_ready, 1)
                pe.sem_clear(y2T_ready)
                for m in range(FF // P):
                    i = m % 2
                    pe.wait_ge(h_free[i], 1)
                    pe.sem_clear(h_free[i])
                    pe.matmul(c.ps[3 + i][:], w1[:, m * P:(m + 1) * P], y2T[:], start=True, stop=True).then_inc(a_ps[i], 1)
                    pe.matmul(c.ps[5 + i][:], w3[:, m * P:(m + 1) * P], y2T[:], start=True, stop=True).then_inc(b_ps[i], 1)
                pre.pe(pe, b + 1)
                pe.wait_ge(hid_ready, 1)
                pe.sem_clear(hid_ready)
                pe.wait_ge(y_free, 1)
                pe.sem_clear(y_free)
                for t in range(TB):
                    for m in range(FF // P):
                        r = pe.matmul(c.ps[2][:, t * P:(t + 1) * P], hid[:, m, t * P:(t + 1) * P], w2[:, m, :],
                                      start=(m == 0), stop=(m == FF // P - 1))
                r.then_inc(y_ready, 1)
            for i in range(2):
                pe.wait_ge(h_free[i], 1)
                pe.sem_clear(h_free[i])
            pe.wait_ge(y_free, 1)
            pe.sem_clear(y_free)
            pre.drain_pe(pe)
            pe.wait_ge(pre.xTs_ready, 1)
            pe.sem_clear(pre.xTs_ready)

        @block.scalar
        def _(a):
            st.wait_loads(a)
            pre.seed_act(a)
            pre.act(a, 0)
            with a.Fori(0, B) as b:
                a.wait_ge(g1_ps, 1)
                a.sem_clear(g1_ps)
                a.activation(g1[:], c.ps[0][0:RANK, :], ACT.Silu, bias=u1b[:]).then_inc(g1_ready, 1)
                a.wait_ge(gs_ready, 1)
                a.sem_clear(gs_ready)
                a.activation(gs[:], gs[:], ACT.Sigmoid).then_inc(gate_ready, 1)
                a.wait_ge(y2_ps, 1)
                a.sem_clear(y2_ps)
                a.activation(y2T[:], c.ps[2][:], ACT.Copy, scale=gamma[:]).then_inc(y2T_ready, 1)
                for m in range(FF // P):
                    i = m % 2
                    a.wait_ge(a_ps[i], 1)
                    a.sem_clear(a_ps[i])
                    a.activation(sl[:, i, :], c.ps[3 + i][:], ACT.Silu).then_inc(sl_ready[i], 1)
                pre.act(a, b + 1)

        @block.vector
        def _(v):
            ch = Chain(v, core.lasting_sem("dve_chain"))
            ch.reset()
            st.wait_loads(v)
            for i in range(2):
                v.sem_inc(h_free[i], 1)
            v.sem_inc(y_free, 1)
            pre.dve(v, ch, 0)
            with v.Fori(0, B) as b:
                ch.reset()
                v.wait_ge(g2_ps, 1)
                v.sem_clear(g2_ps)
                v.tensor_tensor(gs[:], c.ps[1].rearrange("p (t d) -> p t d", t=TB),
                                u2b[:].unsqueeze(1).broadcast_to((P, TB, D)), ALU.add).then_inc(gs_ready, 1)
                v.wait_ge(gate_ready, 1)
                v.sem_clear(gate_ready)
                ch.link(v.tensor_tensor(gs[:], gs[:], c.xn[:, bass.ds(b * TB, TB), :], ALU.mult))
                ch.link(v.tensor_tensor(yk[:], pre.y1[:], gs[:], ALU.add))
                norm.dve_stats(v, ch, lambda t: yk[:, t, :])
                ch.link(norm.dve_apply(v, lambda t: y2[:, t, :], lambda t: yk[:, t, :]))
                v.sem_inc(y2_ready, 1)
                pre.dve(v, ch, b + 1)
                for m in range(FF // P):
                    i = m % 2
                    v.wait_ge(b_ps[i], 1)
                    v.sem_clear(b_ps[i])
                    v.wait_ge(sl_ready[i], 1)
                    v.sem_clear(sl_ready[i])
                    ch.link(v.tensor_tensor(hid[:, m, :], c.ps[5 + i][:], sl[:, i, :], ALU.mult))
                    v.sem_inc(h_free[i], 1)
                v.sem_inc(hid_ready, 1)
                v.wait_ge(y_ready, 1)
                v.sem_clear(y_ready)
                ch.link(v.tensor_tensor(yk[:], yk[:], c.ps[2].rearrange("p (t d) -> p t d", t=TB), ALU.add))
                v.sem_inc(y_free, 1)
                post.dve_stats(v, ch, lambda t: yk[:, t, :])
                post.dve_add(v, ch, b, lambda t: yk[:, t, :])
            pre.drain_dve(v)
    st.ctx.close()


def stage_attn2(core):
    stage_delta_in(core)
    stage_delta(core)
    stage_delta_out(core)


RUN = {0: stage_attn0, 4: stage_attn2, 1: stage_ffn0, 2: stage_attn1, 6: stage_attn3, 3: stage_moe1, 5: stage_moe2, 7: stage_moe3}


def network(nc, A, out):
    with ExitStack() as ctx:
        core = Core(nc, ctx, A)
        x_loaded, stored = core.lasting_sem("x_loaded"), core.lasting_sem("stored")
        with nc.Block() as block:
            @block.sync
            def _(sp):
                sp.dma_start(core.x[:, 0:NT, :], A["x"].rearrange("(t p) d -> p t d", p=P)).then_inc(x_loaded, 16)
                sp.dma_start(core.ident[:], A["ident"]).then_inc(x_loaded, 16)
                sp.wait_ge(x_loaded, 32)

            @block.gpsimd
            def _(g):
                g.memset(core.x[:, NT:NT + TB, :], 0.0)
                g.memset(core.xn[:], 0.0)
                g.memset(core.mhalf[:], -0.5)
        for n in STAGES:
            RUN[n](core)
        with nc.Block() as block:
            @block.sync
            def _(sp):
                sp.dma_start(out.rearrange("(t p) d -> p t d", p=P), core.x[:, 0:NT, :]).then_inc(stored, 16)
                sp.wait_ge(stored, 16)



def kmajor(w):
    k, n = w.shape
    return w.reshape(k // P, P, n).transpose(1, 0, 2)


def columns(v):
    return v.reshape(-1, P).T


def rows(v):
    return np.broadcast_to(v.reshape(1, -1), (P, v.size))


def layout(I):
    A = {"x": I["L0_attn_x"].reshape(B * L, D), "ident": np.eye(P, dtype=np.float32)}
    f = lambda n: I["L0_attn_" + n]
    seen = np.arange(P)[:, None] - (np.arange(SPAN)[None, :] - WIN)
    A.update(a0_wqk=np.concatenate([f("wq_w").T, f("wk_w").T], 1), a0_wv=f("wv_w").T,
             a0_bqk=rows(np.concatenate([f("wq_b"), f("wk_b")])), a0_bv=rows(f("wv_b")),
             a0_nw=rows(np.stack([f("qn_w"), f("kn_w")])).reshape(P, 2, HD), a0_wo=f("wo_w").T, a0_bo=rows(f("wo_b")),
             a0_headmask=np.repeat(np.eye(H, dtype=np.float32), HD, axis=0),
             a0_window=np.where((seen >= 0) & (seen < WIN), 0.0, NEG).astype(np.float32))

    f = lambda n: I["L0_ffn_" + n]
    A.update(f0_w1=f("w1_w").T, f0_w2=f("w2_w").T, f0_s1=columns(f("w1_s")), f0_s2=columns(f("w2_s")),
             f0_g1=columns(f("h1_s")), f0_g2=columns(f("h2_s")), f0_h1=kmajor(f("h1_w").T),
             f0_h2=kmajor(f("h2_w").T), f0_w3=kmajor(f("w3_w").T), f0_s3=rows(f("w3_s")))

    def quarters(name, w):
        for q in range(QUARTERS):
            A[f"{name}{q}"] = w[q * UQ:(q + 1) * UQ].transpose(1, 0, 2)

    ups = lambda w: w.reshape(w.shape[0], P, -1, P).transpose(0, 2, 1, 3).reshape(UNITS, P, P)
    downs = lambda w: w.reshape(UNITS, P, P)
    w, bias = I["L1_attn_W_qkv"], I["L1_attn_b_qkv"]
    i = np.arange(P)
    A.update(a1_wq=w[0:D].T, a1_wk=w[D:2 * D].T, a1_wv=w[2 * D:].T, a1_bq=columns(bias[0:D]),
             a1_bk=columns(bias[D:2 * D]), a1_bv=rows(bias[2 * D:]),
             a1_causal=np.where(i[None, :] <= i[:, None], 0.0, NEG).astype(np.float32))

    f = lambda n: I["L2_attn_" + n]
    A.update(d_gamma=columns(f("norm_in_w")), d_cw=f("conv_w").reshape(D, KCONV), d_cb=columns(f("conv_b")),
             d_betaw=f("beta_w"), d_betab=rows(f("beta_b")))
    pair = lambda w: w.reshape(w.shape[0], NPAIR, P).transpose(1, 0, 2)
    each = lambda w: np.repeat(w.reshape(-1, 2 * NPAIR), DH, axis=1)
    perchan = lambda v: v.reshape(NPAIR, P, 1)
    A["e_w"] = np.concatenate([pair(f("q_w")), pair(f("k_w")), pair(f("alpha_w")), pair(each(f("beta_w"))),
                               pair(f("v_w")), perchan(f("alpha_b")), perchan(each(f("beta_b"))),
                               perchan(f("head_norm_w"))], 2).reshape(NPAIR * P, WCOLS)
    slot = np.arange(DH)
    masks = []
    for m in (1 << l for l in range(LEVELS)):
        col = slot // m * 2 * m + m + slot % m
        masks.append(np.arange(P)[:, None] // m == col[None, :] // m - 1)
    A.update(e_low=np.stack(masks, 1).astype(np.float32), e_ow=f("out_w").reshape(NPAIR, P, D).transpose(1, 0, 2),
             e_heads2=np.kron(np.eye(2), np.ones((DH, DH))).astype(np.float32))
    A.update(g_u1=f("u1_w"), g_u1b=f("u1_b").reshape(RANK, 1), g_u2=f("u2_w"), g_u2b=rows(f("u2_b")),
             g_w1=f("ff_w1"), g_w3=f("ff_w3"), g_w2=kmajor(f("ff_w2")), g_gamma=columns(f("ff_norm_w")))

    f = lambda n: I["L3_attn_" + n]
    up, bup = f("Wup").reshape(LAT, H, 2, HD), f("bup").reshape(H, 2, HD)
    A.update(a3_wq=f("Wq"), a3_bqk=rows(np.stack([f("bq"), bup[:, 0].reshape(D)])).reshape(P, 2, D),
             a3_wd=f("Wdown"), a3_bd=f("bdown").reshape(LAT, 1),
             a3_wkv=up.transpose(0, 2, 1, 3).reshape(LAT, 2 * D), a3_bv=rows(bup[:, 1].reshape(D)),
             a3_wo=f("Wout"), a3_bo=rows(f("bout")))
    inv = (1.0 / 10000.0 ** (np.arange(0, HD, 2, dtype=np.float32) / HD)).astype(np.float32)
    ang = (np.arange(L, dtype=np.float32)[:, None] * inv[None, :]).astype(np.float32)
    tiles = lambda a: a.astype(np.float32).reshape(TB, P, HD).transpose(1, 0, 2)
    A.update(a3_cos=tiles(np.concatenate([np.cos(ang), np.cos(ang)], 1)),
             a3_sin=tiles(np.concatenate([-np.sin(ang), np.sin(ang)], 1)))

    f = lambda n: I["L1_ffn_" + n]
    A.update(m1_gate=f("gate_w").T, m1_gate_b=rows(f("gate_b")), m1_b2=f("b2"), m1_gamma=columns(f("norm_scale")),
             m1_ba=f("b1")[:, 0::2].reshape(UNITS, P).T, m1_bb=f("b1")[:, 1::2].reshape(UNITS, P).T)
    quarters("m1_wa", ups(f("w1")[:, 0::2, :].transpose(0, 2, 1)))
    quarters("m1_wb", ups(f("w1")[:, 1::2, :].transpose(0, 2, 1)))
    quarters("m1_wd", downs(f("w2").transpose(0, 2, 1)))
    f = lambda n: I["L2_ffn_" + n]
    A.update(m2_gate=f("Wg"), m2_gate_b=rows(f("bg")), m2_b2=f("b2"), m2_gamma=columns(f("ln_w")),
             m2_ba=f("b1a").reshape(UNITS, P).T, m2_bb=f("b1b").reshape(UNITS, P).T)
    quarters("m2_wa", ups(f("W1a")))
    quarters("m2_wb", ups(f("W1b")))
    quarters("m2_wd", downs(f("W2")))
    f = lambda n: I["L3_ffn_" + n]
    A.update(m3_gate=f("Wg"), m3_gate_b=np.zeros((P, 8), np.float32), m3_b2=f("b2"), m3_eg=f("gamma").T,
             m3_eb=f("beta").T, m3_ba=f("b1").reshape(UNITS, P).T)
    quarters("m3_wa", ups(f("W1")))
    quarters("m3_wd", downs(f("W2")))
    return A


def kernel(**inputs):
    import concourse.bacc as bacc
    from concourse.bass_utils import run_bass_kernel_spmd

    nc = bacc.Bacc("TRN2", target_bir_lowering=False, num_devices=1)
    arrays = {f"in_{k}": np.ascontiguousarray(a) for k, a in layout({k: np.asarray(a) for k, a in inputs.items()}).items()}
    A = {k[3:]: nc.dram_tensor(k, a.shape, F32, kind="ExternalInput").ap() for k, a in arrays.items()}
    out = nc.dram_tensor("out_0", (B * L, D), F32, kind="ExternalOutput").ap()
    network(nc, A, out)
    r = run_bass_kernel_spmd(nc, [arrays], core_ids=[0])
    return r.results[0]["out_0"].reshape(B, L, D)
```

```python
from contextlib import ExitStack

import numpy as np
import concourse.bass as bass
from concourse import mybir

F32 = mybir.dt.float32
I32 = mybir.dt.int32
ALU = mybir.AluOpType
ACT = mybir.ActivationFunctionType
AX = mybir.AxisListType

STAGES = (0, 1, 2, 3, 4, 5, 6, 7)

B, L, D = 8, 512, 128
P = 128
TB = L // P
NT = B * TB
NEG = -1.0e30
LN_EPS = 1e-5




class Chain:

    def __init__(self, eng, sem):
        self.eng, self.sem, self.n = eng, sem, 0

    def reset(self):
        self.eng.sem_clear(self.sem)
        self.n = 0

    def link(self, ins):
        ins.then_inc(self.sem, 1)
        self.n += 1
        self.eng.wait_ge(self.sem, self.n)


class Core:

    def __init__(self, nc, ctx, A):
        self.nc, self.A = nc, A
        sb = lambda n, s: ctx.enter_context(nc.sbuf_tensor(n, s, F32))
        self.x = sb("x", [P, NT + TB, D])
        self.xn = sb("xn", [P, NT, D])
        self.xT = sb("xT", [P, (B + 1) * L])
        self.ident = sb("ident", [P, P])
        self.beta = sb("beta", [P, B, NT, 2])
        self.mhalf = sb("mhalf", [P, 64])
        self.sems = {}
        self.load_counts = {}
        self.ctx = ctx
        self.psum = ctx.enter_context(nc.psum_tensor("psum", [P, 8, L], F32))
        self.ps = [self.psum[:, i, :] for i in range(8)]

    def lasting_sem(self, name):
        if name not in self.sems:
            self.sems[name] = self.ctx.enter_context(self.nc.semaphore(name))
        return self.sems[name]

    def sem(self, name):
        if name not in self.tokens:
            self.tokens[name] = self.stage_ctx.enter_context(self.nc.semaphore(f"{self.stage_tag}_{name}"))
        return self.tokens[name]


class Stage:

    def __init__(self, core, tag):
        self.c, self.tag, self.ctx = core, tag, ExitStack()
        self.loads = []
        self.due = {}
        core.stage_ctx, core.stage_tag, core.tokens = self.ctx, tag, {}

    def sb(self, name, shape, dt=F32):
        return self.ctx.enter_context(self.c.nc.sbuf_tensor(f"{self.tag}_{name}", shape, dt))

    def load(self, name, shape, group=0):
        t = self.sb(name, shape)
        self.loads.append((t, self.c.A[f"{self.tag}_{name}"], group))
        self.due[group] = self.c.load_counts[group] = self.c.load_counts.get(group, 0) + 16
        return t

    def issue_loads(self, sp):
        for t, src, group in self.loads:
            sp.dma_start(t[:], src).then_inc(self.c.lasting_sem(f"loaded{group}"), 16)

    def wait_loads(self, eng, group=0):
        eng.wait_ge(self.c.lasting_sem(f"loaded{group}"), self.due[group])


def flat(ap):
    return ap.rearrange("p a b -> p (a b)")



class Norm:

    def __init__(self, st, name, eps, rms=False):
        self.st, self.eps, self.rms = st, eps, rms
        self.stats = st.sb(f"{name}_stats", [P, TB, 6])
        self.mv = st.sb(f"{name}_mv", [P, TB, 2])
        self.rstd = st.sb(f"{name}_rstd", [P, TB, 1])
        self.tmp = st.sb(f"{name}_tmp", [P, TB, 1])
        s = st.c.sem
        self.var_ready = s(f"{name}_var_ready")
        self.rstd_ready = s(f"{name}_rstd_ready")

    def dve_stats(self, v, ch, tiles):
        for t in range(TB):
            r = v.bn_stats(self.stats[:, t, :], tiles(t))
        ch.link(r)
        for t in range(TB):
            r = v.bn_aggr(self.mv[:, t, :], self.stats[:, t, :])
        if self.rms:
            ch.link(r)
            ch.link(v.tensor_tensor(self.tmp[:], self.mv[:, :, 0:1], self.mv[:, :, 0:1], ALU.mult))
            r = v.tensor_tensor(self.mv[:, :, 1:2], self.mv[:, :, 1:2], self.tmp[:], ALU.add)
        r.then_inc(self.var_ready, 1)

    def pool_rstd(self, g, ch):
        g.wait_ge(self.var_ready, 1)
        g.sem_clear(self.var_ready)
        ch.link(g.tensor_scalar(self.rstd[:, :, 0], self.mv[:, :, 1], self.eps, None, ALU.add))
        g.tensor_tensor(self.rstd[:, :, 0], self.rstd[:, :, 0], self.st.c.mhalf[:, 0:TB],
                        ALU.pow).then_inc(self.rstd_ready, 1)

    def dve_apply(self, v, outs, ins):
        v.wait_ge(self.rstd_ready, 1)
        v.sem_clear(self.rstd_ready)
        for t in range(TB):
            if self.rms:
                r = v.tensor_scalar(outs(t), ins(t), self.rstd[:, t, 0:1], None, ALU.mult)
            else:
                r = v.tensor_scalar(outs(t), ins(t), self.mv[:, t, 0:1], self.rstd[:, t, 0:1],
                                    ALU.subtract, ALU.mult)
        return r




class Pre:

    def __init__(self, st, inner=None, eps=0.0, gamma=None, both=False, static=False):
        self.st, self.inner, self.gamma, self.both = st, inner, gamma, both
        self.static = static or both
        self.n1 = Norm(st, "pre", LN_EPS)
        self.n2 = Norm(st, "inner", eps, rms=(inner == "rms")) if inner else None
        self.y1 = st.sb("pre_y1", [P, TB, D])
        self.y2 = st.sb("pre_y2", [P, TB, D]) if inner else self.y1
        self.xTs = st.sb("pre_xTs", [P, L]) if self.static else None
        s = st.c.sem
        self.y_ready = s("pre_y_ready")
        self.y_free = s("pre_y_free")
        self.t_ready = s("pre_t_ready")
        self.t_free = s("pre_t_free")
        self.xT_ready = s("pre_xT_ready")
        self.xTs_ready = s("pre_xTs_ready")
        self.xTs_free = s("pre_xTs_free")

    def seed_pe(self, pe):
        pe.sem_inc(self.y_free, 1)
        if self.static:
            pe.sem_inc(self.xTs_free, 1)

    def seed_act(self, a):
        a.sem_inc(self.t_free, 1)

    def drain_dve(self, v):
        v.wait_ge(self.y_free, 1)
        v.sem_clear(self.y_free)

    def drain_pe(self, pe):
        pe.wait_ge(self.t_free, 1)
        pe.sem_clear(self.t_free)
        pe.wait_ge(self.xT_ready, 1)
        pe.sem_clear(self.xT_ready)
        if self.both:
            pe.wait_ge(self.xTs_ready, 1)
            pe.sem_clear(self.xTs_ready)

    def drain_act(self, a):
        if self.static:
            a.wait_ge(self.xTs_free, 1)
            a.sem_clear(self.xTs_free)

    def dve(self, v, ch, b):
        c = self.st.c
        self.n1.dve_stats(v, ch, lambda t: c.x[:, b * TB + t, :])
        v.wait_ge(self.y_free, 1)
        v.sem_clear(self.y_free)
        r = self.n1.dve_apply(v, lambda t: self.y1[:, t, :], lambda t: c.x[:, b * TB + t, :])
        if self.inner:
            ch.link(r)
            self.n2.dve_stats(v, ch, lambda t: self.y1[:, t, :])
            r = self.n2.dve_apply(v, lambda t: self.y2[:, t, :], lambda t: self.y1[:, t, :])
        ch.link(r)
        v.sem_inc(self.y_ready, 1)

    def pool(self, g, ch, b):
        self.n1.pool_rstd(g, ch)
        if self.inner:
            self.n2.pool_rstd(g, ch)

    def pe(self, pe, b):
        c = self.st.c
        pe.wait_ge(self.y_ready, 1)
        pe.sem_clear(self.y_ready)
        srcs = [self.y1, self.y2] if self.both else [self.y2]
        for n, src in enumerate(srcs):
            pe.wait_ge(self.t_free, 1)
            pe.sem_clear(self.t_free)
            for t in range(TB):
                r = pe.transpose(c.ps[7][:, t * P:(t + 1) * P], src[:, t, :], c.ident[:])
            r.then_inc(self.t_ready, 1)
            if n == len(srcs) - 1:
                pe.drain().then_inc(self.y_free, 1)

    def act(self, a, b):
        c = self.st.c
        scale = self.gamma[:, 0:1] if self.gamma is not None else 1.0
        a.wait_ge(self.t_ready, 1)
        a.sem_clear(self.t_ready)
        if self.static:
            a.wait_ge(self.xTs_free, 1)
            a.sem_clear(self.xTs_free)
            r = a.activation(self.xTs[:], c.ps[7][:], ACT.Identity, scale=scale)
            r.then_inc(self.xTs_ready, 1)
        if self.both:
            a.drain().then_inc(self.t_free, 1)
            a.wait_ge(self.t_ready, 1)
            a.sem_clear(self.t_ready)
        a.activation(c.xT[:, bass.ds(b * L, L)], c.ps[7][:], ACT.Identity, scale=scale).then_inc(self.xT_ready, 1)
        a.drain().then_inc(self.t_free, 1)



class Post:
    def __init__(self, st):
        self.st = st
        self.norm = Norm(st, "post", LN_EPS)
        self.z = st.sb("post_z", [P, TB, D])

    def dve_stats(self, v, ch, tiles):
        self.norm.dve_stats(v, ch, tiles)

    def dve_add(self, v, ch, b, tiles):
        c = self.st.c
        ch.link(self.norm.dve_apply(v, lambda t: self.z[:, t, :], tiles))
        xb = c.x[:, bass.ds(b * TB, TB), :]
        ch.link(v.tensor_tensor(xb, xb, self.z[:], ALU.add))

    def pool(self, g, ch):
        self.norm.pool_rstd(g, ch)



HID = 512
HC = HID // P


def stage_ffn0(core):
    st = Stage(core, "f0")
    c, nc, s = core, core.nc, core.sem
    w1, w2 = st.load("w1", [P, HID]), st.load("w2", [P, HID])
    s1, s2, g1, g2 = (st.load(n, [P, HC]) for n in ("s1", "s2", "g1", "g2"))
    h1, h2 = st.load("h1", [P, HC, HID]), st.load("h2", [P, HC, HID])
    w3, s3 = st.load("w3", [P, HC, D]), st.load("s3", [P, D])
    pre, post = Pre(st), Post(st)
    t_s = st.sb("silu", [P, 2, L])
    hid = [st.sb(f"hid{i}", [P, HC, L]) for i in range(3)]
    y = st.sb("y", [P, TB, D])
    ready = [s(f"bank{i}_ready") for i in range(4)]
    free = [s(f"bank{i}_free") for i in range(4)]
    t_ready = [s(f"silu{i}_ready") for i in range(2)]
    t_free = [s(f"silu{i}_free") for i in range(2)]
    h_ready = [s(f"hid{i}_ready") for i in range(3)]
    h_free = [s(f"hid{i}_free") for i in range(3)]
    y_ready, y_free = s("y_ready"), s("y_free")
    with nc.Block() as block:
        @block.sync
        def _(sp):
            st.issue_loads(sp)

        @block.gpsimd
        def _(g):
            ch = Chain(g, core.lasting_sem("pool_chain"))
            ch.reset()
            pre.pool(g, ch, 0)
            with g.Fori(0, B) as b:
                ch.reset()
                pre.pool(g, ch, b + 1)
                post.pool(g, ch)

        @block.tensor
        def _(pe):
            st.wait_loads(pe)
            pre.seed_pe(pe)
            for i in range(3):
                pe.sem_inc(h_free[i], 1)
            pre.pe(pe, 0)
            with pe.Fori(0, B) as b:
                pe.wait_ge(pre.xT_ready, 1)
                pe.sem_clear(pre.xT_ready)
                xb = c.xT[:, bass.ds(b * L, L)]
                for m in range(HC):
                    for k, w in enumerate((w1, w2)):
                        i = (2 * m + k) % 4
                        pe.wait_ge(free[i], 1)
                        pe.sem_clear(free[i])
                        pe.matmul(c.ps[i][:], w[:, m * P:(m + 1) * P], xb, start=True,
                                  stop=True).then_inc(ready[i], 1)
                for n, w in enumerate((h1, h2)):
                    for m in range(HC):
                        pe.wait_ge(free[m], 1)
                        pe.sem_clear(free[m])
                        for k in range(HC):
                            if m == 0:
                                pe.wait_ge(h_ready[n], k + 1)
                            r = pe.matmul(c.ps[m][:], w[:, k, m * P:(m + 1) * P], hid[n][:, k, :],
                                          start=(k == 0), stop=(k == HC - 1))
                        r.then_inc(ready[m], 1)
                    pe.sem_clear(h_ready[n])
                    pe.drain().then_inc(h_free[n], 1)
                    if n == 0:
                        pre.pe(pe, b + 1)
                pe.wait_ge(h_ready[2], HC)
                pe.sem_clear(h_ready[2])
                pe.wait_ge(y_free, 1)
                pe.sem_clear(y_free)
                for t in range(TB):
                    for k in range(HC):
                        r = pe.matmul(c.ps[4][:, t * P:(t + 1) * P], hid[2][:, k, t * P:(t + 1) * P],
                                      w3[:, k, :], start=(k == 0), stop=(k == HC - 1))
                r.then_inc(y_ready, 1)
                pe.drain().then_inc(h_free[2], 1)
            for i in range(4):
                pe.wait_ge(free[i], 1)
                pe.sem_clear(free[i])
            pe.wait_ge(y_free, 1)
            pe.sem_clear(y_free)
            pre.drain_pe(pe)

        @block.scalar
        def _(a):
            st.wait_loads(a)
            pre.seed_act(a)
            a.sem_inc(free[0], 1)
            a.sem_inc(free[2], 1)
            pre.act(a, 0)
            with a.Fori(0, B) as b:
                for m in range(HC):
                    i = 2 * m % 4
                    a.wait_ge(ready[i], 1)
                    a.sem_clear(ready[i])
                    a.wait_ge(t_free[m % 2], 1)
                    a.sem_clear(t_free[m % 2])
                    a.activation(t_s[:, m % 2, :], c.ps[i][:], ACT.Silu, scale=s1[:, m:m + 1]).then_inc(t_ready[m % 2], 1)
                    a.drain().then_inc(free[i], 1)
                for n, sc in enumerate((g1, g2)):
                    a.wait_ge(h_free[n + 1], 1)
                    a.sem_clear(h_free[n + 1])
                    for m in range(HC):
                        a.wait_ge(ready[m], 1)
                        a.sem_clear(ready[m])
                        a.activation(hid[n + 1][:, m, :], c.ps[m][:], ACT.Gelu,
                                     scale=sc[:, m:m + 1]).then_inc(h_ready[n + 1], 1)
                        a.drain().then_inc(free[m], 1)
                    if n == 0:
                        pre.act(a, b + 1)
            pre.drain_act(a)
            for i in range(1, 3):
                a.wait_ge(h_free[i], 1)
                a.sem_clear(h_free[i])
            for i in range(2):
                a.wait_ge(t_free[i], 1)
                a.sem_clear(t_free[i])

        @block.vector
        def _(v):
            ch = Chain(v, core.lasting_sem("dve_chain"))
            ch.reset()
            st.wait_loads(v)
            v.sem_inc(free[1], 1)
            v.sem_inc(free[3], 1)
            v.sem_inc(y_free, 1)
            for i in range(2):
                v.sem_inc(t_free[i], 1)
            pre.dve(v, ch, 0)
            with v.Fori(0, B) as b:
                ch.reset()
                v.wait_ge(h_free[0], 1)
                v.sem_clear(h_free[0])
                for m in range(HC):
                    i = (2 * m + 1) % 4
                    v.wait_ge(ready[i], 1)
                    v.sem_clear(ready[i])
                    v.wait_ge(t_ready[m % 2], 1)
                    v.sem_clear(t_ready[m % 2])
                    v.scalar_tensor_tensor(hid[0][:, m, :], c.ps[i][:], s2[:, m:m + 1], t_s[:, m % 2, :],
                                           ALU.mult, ALU.mult).then_inc(h_ready[0], 1)
                    d = v.drain()
                    d.then_inc(free[i], 1)
                    v.sem_inc(t_free[m % 2], 1)
                pre.dve(v, ch, b + 1)
                v.wait_ge(y_ready, 1)
                v.sem_clear(y_ready)
                ch.link(v.tensor_tensor(y[:], c.ps[4][:].rearrange("p (a b) -> p a b", a=TB),
                                        s3[:].unsqueeze(1).broadcast_to((P, TB, D)), ALU.mult))
                v.sem_inc(y_free, 1)
                post.dve_stats(v, ch, lambda t: y[:, t, :])
                post.dve_add(v, ch, b, lambda t: y[:, t, :])
            pre.drain_dve(v)
            v.wait_ge(h_free[0], 1)
            v.sem_clear(h_free[0])
    st.ctx.close()



SENTINEL = -3.0e38
TAKEN = 3.0e38
UNITS = 32
QUARTERS = 4
UQ = UNITS // QUARTERS
AT_LN, AT_TRANSPOSE, AT_LOGITS, AT_TOPK, AT_EXP, AT_WEIGH, AT_COMBINE_T, AT_COMBINE_B2, AT_SUM = \
    2, 6, 9, 11, 13, 14, 17, 20, 22


def stage_moe(core, tag, E, topk, inner, eps, residual, kind):
    st = Stage(core, tag)
    c, nc, s = core, core.nc, core.sem
    FC = UNITS // E
    relu, silu, glu7 = kind == "relu", kind == "silu", kind == "glu7"
    gate, gate_b = st.load("gate", [P, E]), st.load("gate_b", [P, E])
    b2 = st.load("b2", [E, D])
    ba = st.load("ba", [P, UNITS])
    if relu:
        gamma = None
        eg, eb = st.load("eg", [P, E]), st.load("eb", [P, E])
    else:
        gamma, bb = st.load("gamma", [P, 1]), st.load("bb", [P, UNITS])
    wa, wb, wd = [], [], []
    for q in range(QUARTERS):
        wa.append(st.load(f"wa{q}", [P, UQ, P], q + 1))
        if not relu:
            wb.append(st.load(f"wb{q}", [P, UQ, P], q + 1))
        wd.append(st.load(f"wd{q}", [P, UQ, D], q + 1))
    pre = Pre(st, inner=inner, eps=eps, gamma=gamma, both=relu, static=True)
    post = Post(st)
    lg = st.sb("logits", [P, TB, E + 8])
    taken = st.sb("taken", [P, TB, E + 8])
    top, mark = st.sb("top", [P, TB, 8]), st.sb("mark", [P, TB, 8])
    ex, den = st.sb("ex", [P, TB, E]), st.sb("den", [P, TB, 1])
    comb_next, comb = st.sb("combine_next", [P, TB, E]), st.sb("combine", [P, TB, E])
    combT = st.sb("combineT", [E, L])
    acc_next, acc = st.sb("acc_next", [P, TB, D]), st.sb("acc", [P, TB, D])
    h, ta = st.sb("h", [P, 2, L]), st.sb("ta", [P, 2, L])
    if glu7:
        tb, tc, td = st.sb("tb", [P, 2, L]), st.sb("tc", [P, 2, L]), st.sb("td", [P, 2, L])
        c1 = st.sb("c1", [P, 1])
    if relu:
        nrm = st.sb("normed", [P, 2, L])
    a_ready = [s(f"bank{i}_ready") for i in range(4)]
    a_free = [s(f"bank{i}_free") for i in range(4)]
    t_ready = [s(f"ta{i}_ready") for i in range(2)]
    t_free = [s(f"ta{i}_free") for i in range(2)]
    h_ready = [s(f"h{i}_ready") for i in range(2)]
    y_ready = [s(f"y{i}_ready") for i in range(2)]
    y_free = [s(f"y{i}_free") for i in range(2)]
    n_ready = [s(f"normed{i}_ready") for i in range(2)]
    logits_ready, ex_ready, ex_done = s("logits_ready"), s("ex_ready"), s("ex_done")
    comb_ready, combT_ps, combT_ready = s("combine_ready"), s("combineT_ps"), s("combineT_ready")
    cb_ready, r_free, consts_ready = s("combine_b2_ready"), s("router_bank_free"), s("consts_ready")
    bank_r = c.ps[6]

    with nc.Block() as block:
        @block.sync
        def _(sp):
            st.issue_loads(sp)

        @block.gpsimd
        def _(g):
            ch = Chain(g, core.lasting_sem("pool_chain"))
            ch.reset()
            pre.pool(g, ch, 0)
            with g.Fori(0, B) as b:
                ch.reset()
                pre.pool(g, ch, b + 1)
                post.pool(g, ch)

        @block.tensor
        def _(pe):
            def logits():
                pe.wait_ge(pre.xTs_ready, 1)
                pe.sem_clear(pre.xTs_ready)
                pe.wait_ge(r_free, 1)
                pe.sem_clear(r_free)
                for t in range(TB):
                    r = pe.matmul(bank_r[:, t * E:(t + 1) * E], pre.xTs[:, t * P:(t + 1) * P], gate[:],
                                  start=True, stop=True)
                r.then_inc(logits_ready, 1)
                pe.drain().then_inc(pre.xTs_free, 1)

            def combine_t():
                pe.wait_ge(comb_ready, 1)
                pe.sem_clear(comb_ready)
                for t in range(TB):
                    r = pe.transpose(bank_r[0:E, t * P:(t + 1) * P], comb_next[:, t, :], c.ident[:])
                r.then_inc(combT_ps, 1)

            def combine_b2():
                pe.wait_ge(combT_ready, 1)
                pe.sem_clear(combT_ready)
                for t in range(TB):
                    r = pe.matmul(bank_r[:, t * P:(t + 1) * P], combT[:, t * P:(t + 1) * P], b2[:],
                                  start=True, stop=True)
                r.then_inc(cb_ready, 1)

            def up(u, xb):
                e, q, j = u // FC, u // UQ, u % UQ
                if j == 0:
                    st.wait_loads(pe, q + 1)
                if relu:
                    if u % FC == 0:
                        pe.wait_ge(n_ready[e % 2], 1)
                        pe.sem_clear(n_ready[e % 2])
                    pe.wait_ge(a_free[u % 4], 1)
                    pe.sem_clear(a_free[u % 4])
                    pe.matmul(c.ps[u % 4][:], wa[q][:, j, :], nrm[:, e % 2, :], start=True,
                              stop=True).then_inc(a_ready[u % 4], 1)
                else:
                    for k, w in enumerate((wa, wb)):
                        i = 2 * (u % 2) + k
                        pe.wait_ge(a_free[i], 1)
                        pe.sem_clear(a_free[i])
                        pe.matmul(c.ps[i][:], w[q][:, j, :], xb, start=True, stop=True).then_inc(a_ready[i], 1)

            def down(u):
                e, m = u // FC, u % FC
                if m == 0:
                    pe.wait_ge(y_free[e % 2], 1)
                    pe.sem_clear(y_free[e % 2])
                pe.wait_ge(h_ready[u % 2], 1)
                pe.sem_clear(h_ready[u % 2])
                for t in range(TB):
                    r = pe.matmul(c.ps[4 + e % 2][:, t * P:(t + 1) * P], h[:, u % 2, t * P:(t + 1) * P],
                                  wd[u // UQ][:, u % UQ, :], start=(m == 0 and t == 0), stop=(m == FC - 1),
                                  skip_group_check=True)
                if m == FC - 1:
                    r.then_inc(y_ready[e % 2], 1)

            st.wait_loads(pe)
            pre.seed_pe(pe)
            pre.pe(pe, 0)
            logits()
            combine_t()
            combine_b2()
            with pe.Fori(0, B) as b:
                if not relu:
                    pe.wait_ge(pre.xT_ready, 1)
                    pe.sem_clear(pre.xT_ready)
                xb = c.xT[:, bass.ds(b * L, L)]
                for u in range(UNITS):
                    if u == AT_TRANSPOSE:
                        pre.pe(pe, b + 1)
                    if u == AT_LOGITS:
                        logits()
                    if u == AT_COMBINE_T:
                        combine_t()
                    if u == AT_COMBINE_B2:
                        combine_b2()
                    up(u, xb)
                    if u >= 1:
                        down(u - 1)
                down(UNITS - 1)
            for i in range(4):
                pe.wait_ge(a_free[i], 1)
                pe.sem_clear(a_free[i])
            pe.wait_ge(y_free[0], 1)
            pe.sem_clear(y_free[0])
            pe.wait_ge(y_free[1], 1)
            pe.sem_clear(y_free[1])
            pe.wait_ge(r_free, 1)
            pe.sem_clear(r_free)
            pe.wait_ge(pre.t_free, 1)
            pe.sem_clear(pre.t_free)
            if not relu:
                pe.wait_ge(pre.xT_ready, 1)
                pe.sem_clear(pre.xT_ready)

        @block.scalar
        def _(a):
            ch = Chain(a, core.lasting_sem("act_chain"))
            ch.reset()
            st.wait_loads(a)
            pre.seed_act(a)
            for i in ((0, 2) if silu else (0, 1, 2, 3)):
                a.sem_inc(a_free[i], 1)

            def exps():
                a.wait_ge(ex_ready, 1)
                a.sem_clear(ex_ready)
                a.activation(ex[:], ex[:], ACT.Exp).then_inc(ex_done, 1)

            def combine_t():
                a.wait_ge(combT_ps, 1)
                a.sem_clear(combT_ps)
                a.activation(combT[:], bank_r[0:E, :], ACT.Copy).then_inc(combT_ready, 1)

            pre.act(a, 0)
            exps()
            combine_t()
            a.wait_ge(consts_ready, 1)
            a.sem_clear(consts_ready)
            with a.Fori(0, B) as b:
                ch.reset()
                for u in range(UNITS):
                    if u == AT_TRANSPOSE:
                        pre.act(a, b + 1)
                    if u == AT_EXP:
                        exps()
                    if u == AT_COMBINE_T:
                        combine_t()
                    j = u % 2
                    if relu:
                        a.wait_ge(a_ready[u % 4], 1)
                        a.sem_clear(a_ready[u % 4])
                        a.activation(h[:, j, :], c.ps[u % 4][:], ACT.Relu, bias=ba[:, u:u + 1]).then_inc(h_ready[j], 1)
                        a.drain().then_inc(a_free[u % 4], 1)
                    elif silu:
                        a.wait_ge(a_ready[2 * j], 1)
                        a.sem_clear(a_ready[2 * j])
                        a.wait_ge(t_free[j], 1)
                        a.sem_clear(t_free[j])
                        a.activation(ta[:, j, :], c.ps[2 * j][:], ACT.Silu, bias=ba[:, u:u + 1]).then_inc(t_ready[j], 1)
                        a.drain().then_inc(a_free[2 * j], 1)
                    else:
                        a.wait_ge(a_ready[2 * j], 1)
                        a.sem_clear(a_ready[2 * j])
                        a.wait_ge(t_free[j], 1)
                        a.sem_clear(t_free[j])
                        ch.link(a.activation(ta[:, j, :], c.ps[2 * j][:], ACT.Relu, bias=ba[:, u:u + 1], scale=-1.0))
                        a.sem_inc(a_free[2 * j], 1)
                        a.activation(tc[:, j, :], ta[:, j, :], ACT.Sigmoid, scale=-1.702, bias=c1[:])
                        a.wait_ge(a_ready[2 * j + 1], 1)
                        a.sem_clear(a_ready[2 * j + 1])
                        a.activation(tb[:, j, :], c.ps[2 * j + 1][:], ACT.Relu, bias=bb[:, u:u + 1],
                                     scale=-1.0).then_inc(t_ready[j], 1)
                        a.drain().then_inc(a_free[2 * j + 1], 1)
            pre.drain_act(a)
            if not relu:
                a.wait_ge(t_free[0], 1)
                a.sem_clear(t_free[0])
                a.wait_ge(t_free[1], 1)
                a.sem_clear(t_free[1])

        @block.vector
        def _(v):
            ch = Chain(v, core.lasting_sem("dve_chain"))
            ch.reset()

            def route():
                v.wait_ge(logits_ready, 1)
                v.sem_clear(logits_ready)
                ch.link(v.tensor_tensor(lg[:, :, 0:E], bank_r[:, 0:TB * E].rearrange("p (t e) -> p t e", t=TB),
                                        gate_b[:].unsqueeze(1).broadcast_to((P, TB, E)), ALU.add))
                for t in range(TB):
                    r = v.max(top[:, t, :], lg[:, t, 0:E])
                ch.link(r)
                ch.link(v.tensor_copy(mark[:, :, 0:topk], top[:, :, 0:topk]))
                v.tensor_tensor(ex[:], lg[:, :, 0:E], top[:, :, 0:1].broadcast_to((P, TB, E)),
                                ALU.subtract).then_inc(ex_ready, 1)
                for t in range(TB):
                    r = v.match_replace(taken[:, t, :], mark[:, t, :], lg[:, t, :], TAKEN)
                ch.link(r)
                ch.link(v.tensor_scalar(taken[:, :, 0:E], taken[:, :, 0:E], TAKEN, None, ALU.is_equal))

            def weigh():
                v.wait_ge(ex_done, 1)
                v.sem_clear(ex_done)
                ch.link(v.tensor_tensor(ex[:], ex[:], taken[:, :, 0:E], ALU.mult))
                ch.link(v.tensor_reduce(den[:], ex[:], AX.X, ALU.add))
                ch.link(v.reciprocal(den[:], den[:]))
                ch.link(v.tensor_tensor(comb_next[:], ex[:], den[:].broadcast_to((P, TB, E)), ALU.mult))
                v.sem_inc(comb_ready, 1)

            def start_sum():
                v.wait_ge(cb_ready, 1)
                v.sem_clear(cb_ready)
                src = bank_r[:].rearrange("p (t d) -> p t d", t=TB)
                if residual:
                    ch.link(v.tensor_tensor(acc_next[:], src, pre.y1[:], ALU.add))
                else:
                    ch.link(v.tensor_copy(acc_next[:], src))
                v.sem_inc(r_free, 1)

            def make_normed(e, b):
                if e < E:
                    v.tensor_scalar(nrm[:, e % 2, :], c.xT[:, bass.ds(b * L, L)], eg[:, e:e + 1], eb[:, e:e + 1],
                                    ALU.mult, ALU.add).then_inc(n_ready[e % 2], 1)

            def collect(e, b):
                v.wait_ge(y_ready[e % 2], 1)
                v.sem_clear(y_ready[e % 2])
                for t in range(TB):
                    r = v.scalar_tensor_tensor(acc[:, t, :], c.ps[4 + e % 2][:, t * P:(t + 1) * P],
                                               comb[:, t, e:e + 1], acc[:, t, :], ALU.mult, ALU.add)
                ch.link(r)
                v.sem_inc(y_free[e % 2], 1)
                if relu:
                    make_normed(e + 2, b)

            st.wait_loads(v)
            v.memset(lg[:], SENTINEL)
            ch.link(v.memset(mark[:], SENTINEL))
            if glu7:
                v.memset(c1[:], 7.0 * 1.702)
                v.tensor_scalar(ba[:], ba[:], -1.0, 7.0, ALU.mult, ALU.add)
                ch.link(v.tensor_scalar(bb[:], bb[:], -1.0, 7.0, ALU.mult, ALU.add))
            v.sem_inc(consts_ready, 1)
            if silu:
                v.sem_inc(a_free[1], 1)
                v.sem_inc(a_free[3], 1)
            for i in range(2):
                v.sem_inc(y_free[i], 1)
                if not relu:
                    v.sem_inc(t_free[i], 1)
            v.sem_inc(r_free, 1)
            pre.dve(v, ch, 0)
            route()
            weigh()
            start_sum()
            with v.Fori(0, B) as b:
                ch.reset()
                v.tensor_copy(comb[:], comb_next[:])
                if relu:
                    v.wait_ge(pre.xT_ready, 1)
                    v.sem_clear(pre.xT_ready)
                    make_normed(0, b)
                    make_normed(1, b)
                ch.link(v.tensor_copy(acc[:], acc_next[:]))
                for u in range(UNITS):
                    if u == AT_LN:
                        pre.dve(v, ch, b + 1)
                    if u == AT_TOPK:
                        route()
                    if u == AT_WEIGH:
                        weigh()
                    if u == AT_SUM:
                        start_sum()
                    j = u % 2
                    if silu:
                        v.wait_ge(a_ready[2 * j + 1], 1)
                        v.sem_clear(a_ready[2 * j + 1])
                        v.wait_ge(t_ready[j], 1)
                        v.sem_clear(t_ready[j])
                        v.scalar_tensor_tensor(h[:, j, :], c.ps[2 * j + 1][:], bb[:, u:u + 1], ta[:, j, :],
                                               ALU.add, ALU.mult).then_inc(h_ready[j], 1)
                        v.drain().then_inc(a_free[2 * j + 1], 1)
                        v.sem_inc(t_free[j], 1)
                    if glu7:
                        v.wait_ge(t_ready[j], 1)
                        v.sem_clear(t_ready[j])
                        v.scalar_tensor_tensor(td[:, j, :], ta[:, j, :], 7.0, tc[:, j, :], ALU.subtract, ALU.mult)
                        ch.link(v.tensor_scalar(tb[:, j, :], tb[:, j, :], 8.0, 6.0, ALU.subtract, ALU.min))
                        v.tensor_tensor(h[:, j, :], td[:, j, :], tb[:, j, :], ALU.mult).then_inc(h_ready[j], 1)
                        v.drain().then_inc(t_free[j], 1)
                    if u >= FC + 1 and (u - FC - 1) % FC == 0:
                        collect((u - FC - 1) // FC, b)
                for e in range((UNITS - 1 - FC - 1) // FC + 1, E):
                    collect(e, b)
                post.dve_stats(v, ch, lambda t: acc[:, t, :])
                post.dve_add(v, ch, b, lambda t: acc[:, t, :])
            pre.drain_dve(v)
            if relu:
                v.wait_ge(pre.xT_ready, 1)
                v.sem_clear(pre.xT_ready)
    st.ctx.close()


def stage_moe1(core):
    stage_moe(core, "m1", 32, 4, "rms", 1e-5, True, "glu7")


def stage_moe2(core):
    stage_moe(core, "m2", 8, 2, "rms", float(np.finfo(np.float32).eps), False, "silu")


def stage_moe3(core):
    stage_moe(core, "m3", 8, 2, "ln", 1e-6, True, "relu")



H, HD = 16, 8
WIN = 32
G, HG = 4, 4
VW = HD + 1
CLIP, QK_EPS = 10000.0, 1e-5
SPAN = WIN + P
UN0 = G * TB
PRE0 = 10


def stage_attn0(core):
    st = Stage(core, "a0")
    c, nc, s = core, core.nc, core.sem
    wqk, wv = st.load("wqk", [P, 2 * D]), st.load("wv", [P, D])
    bqk, bv = st.load("bqk", [P, 2 * D]), st.load("bv", [P, D])
    nw = st.load("nw", [P, 2, HD])
    window = st.load("window", [P, SPAN])
    hm = st.load("headmask", [P, H])
    wo, bo = st.load("wo", [P, D]), st.load("bo", [P, D])
    pre, post = Pre(st, static=True), Post(st)
    NH = 2 * H
    raw = st.sb("raw", [P, TB * NH, HD])
    sq = st.sb("sq", [P, TB * NH, HD])
    rstd = st.sb("rstd", [P, TB * NH, 1])
    nwf = st.sb("nwf", [P, NH, HD])
    qk = st.sb("qk", [P, TB, 2, D])
    qT, kT = st.sb("qT", [P, L]), st.sb("kT", [P, L])
    qz = st.sb("qz", [P, H, L])
    va, vh = st.sb("v", [P, TB, H, VW]), st.sb("vh", [WIN, TB, H, VW])
    pr = st.sb("probs", [P, 4, HG, SPAN])
    nm = st.sb("negmax", [P, UN0, HG])
    pT, hT = st.sb("probsT", [P, L]), st.sb("haloT", [WIN, L])
    rec = st.sb("rec", [P, TB, HG, 1])
    o = st.sb("o", [P, TB, H, HD])
    oT, y = st.sb("oT", [P, L]), st.sb("y", [P, TB, D])
    qk_ps, v_ps = s("q_ps"), s("v_ps")
    ms_ready, rs_ready = s("head_ms_ready"), s("head_rstd_ready")
    qk_ready = s("qk_ready")
    tr_ready = [s(f"proj{i}_ready") for i in range(2)]
    qT_dve, qT_pool = s("qT_to_dve"), s("qT_to_pool")
    kT_ready = s("kT_ready")
    qz_ready = [s("qz_dve_ready"), s("qz_pool_ready")]
    v_ready = s("v_ready")
    s_ready = [s(f"scores{i}_ready") for i in range(2)]
    s_free = [s(f"scores{i}_free") for i in range(2)]
    m_ready = [s(f"max{i}_ready") for i in range(4)]
    p_ready = [s(f"probs{i}_ready") for i in range(4)]
    pt_ps, pt_ready = s("probsT0_ps"), s("probsT0_ready")
    ht_ps, ht_ready = s("probsT1_ps"), s("probsT1_ready")
    o_ready = [s(f"out{i}_ready") for i in range(2)]
    o_free = [s(f"out{i}_free") for i in range(2)]
    on_ready, oT_ps, oT_ready, y_ready = s("on_ready"), s("oT_ps"), s("oT_ready"), s("y_ready")
    y_free = s("y_free")

    def width(qb):
        return P if qb == 0 else SPAN

    def score_slot(i, w):
        return c.psum[:, 2 * i:2 * i + 2, :].rearrange("p a (c n) -> p (a c) n", c=2)[:, :, 0:w]

    with nc.Block() as block:
        @block.sync
        def _(sp):
            st.issue_loads(sp)

        @block.gpsimd
        def _(g):
            ch = Chain(g, core.lasting_sem("pool_chain"))
            ch.reset()
            pre.pool(g, ch, 0)
            with g.Fori(0, B) as b:
                ch.reset()
                g.wait_ge(qT_pool, 1)
                g.sem_clear(qT_pool)
                for h in range(H // 2, H):
                    r = g.tensor_scalar(qz[:, h, :], qT[:], hm[:, h:h + 1], None, ALU.mult)
                    if h % HG == HG - 1:
                        r.then_inc(qz_ready[1], 1)
                pre.pool(g, ch, b + 1)
                post.pool(g, ch)

        @block.tensor
        def _(pe):
            def scores(u):
                g, qb = u // TB, u % TB
                w = width(qb)
                k0 = (qb + 1) * P - w
                pe.wait_ge(s_free[u % 2], 1)
                pe.sem_clear(s_free[u % 2])
                if qb == 0:
                    ready, n = qz_ready[g // 2], g % 2 + 1
                    if n == 1:
                        pe.wait_ge(ready, n)
                    else:
                        pe.wait_ge(ready, n)
                        pe.sem_clear(ready)
                for j in range(HG):
                    r = pe.matmul(score_slot(u % 2, w)[:, j, :], qz[:, g * HG + j, qb * P:(qb + 1) * P],
                                  kT[:, k0:k0 + w], start=True, stop=True)
                r.then_inc(s_ready[u % 2], 1)

            def transposes(u):
                qb = u % TB
                w = width(qb)
                pe.wait_ge(p_ready[u % 4], 1)
                pe.sem_clear(p_ready[u % 4])
                if qb:
                    for j in range(HG):
                        r = pe.transpose(c.ps[7][0:WIN, j * P:(j + 1) * P], pr[:, u % 4, j, 0:WIN], c.ident[:])
                    r.then_inc(ht_ps, 1)
                for j in range(HG):
                    r = pe.transpose(c.ps[4][:, j * P:(j + 1) * P], pr[:, u % 4, j, w - P:w], c.ident[:])
                r.then_inc(pt_ps, 1)

            def values(u):
                g, qb = u // TB, u % TB
                if qb == 0:
                    pe.wait_ge(o_free[g % 2], 1)
                    pe.sem_clear(o_free[g % 2])
                pe.wait_ge(pt_ready, 1)
                pe.sem_clear(pt_ready)
                if qb:
                    pe.wait_ge(ht_ready, 1)
                    pe.sem_clear(ht_ready)
                for j in range(HG):
                    h = g * HG + j
                    at, bank = (qb * HG + j) * VW, c.ps[6 - g % 2]
                    r = pe.matmul(bank[:, at:at + VW], pT[:, j * P:(j + 1) * P], va[:, qb, h, :],
                                  start=True, stop=(qb == 0))
                    if qb:
                        r = pe.matmul(bank[:, at:at + VW], hT[:, j * P:(j + 1) * P], vh[:, qb, h, :],
                                      start=False, stop=True)
                if qb == TB - 1:
                    r.then_inc(o_ready[g % 2], 1)

            st.wait_loads(pe)
            pre.seed_pe(pe)
            pre.pe(pe, 0)
            with pe.Fori(0, B) as b:
                pe.wait_ge(pre.xT_ready, 1)
                pe.sem_clear(pre.xT_ready)
                pe.wait_ge(pre.xTs_ready, 1)
                pe.sem_clear(pre.xTs_ready)
                pe.wait_ge(s_free[0], 1)
                pe.sem_clear(s_free[0])
                pe.wait_ge(s_free[1], 1)
                pe.sem_clear(s_free[1])
                for t in range(TB):
                    r = pe.matmul(c.ps[t // 2][:, (t % 2) * 2 * D:(t % 2 + 1) * 2 * D],
                                  pre.xTs[:, t * P:(t + 1) * P], wqk[:], start=True, stop=True)
                r.then_inc(qk_ps, 1)
                for t in range(TB):
                    pe.matmul(c.ps[2][:, t * P:(t + 1) * P], pre.xTs[:, t * P:(t + 1) * P], wv[:],
                              start=True, stop=True)
                for t in range(1, TB):
                    r = pe.matmul(c.ps[3][0:WIN, t * P:(t + 1) * P], pre.xTs[:, t * P - WIN:t * P], wv[:],
                                  start=True, stop=True)
                r.then_inc(v_ps, 1)
                pe.drain().then_inc(pre.xTs_free, 1)
                pe.wait_ge(qk_ready, 1)
                pe.sem_clear(qk_ready)
                for i in range(2):
                    for t in range(TB):
                        r = pe.transpose(c.ps[4 + i][:, t * P:(t + 1) * P], qk[:, t, i, :], c.ident[:])
                    r.then_inc(tr_ready[i], 1)
                pe.wait_ge(v_ready, 1)
                pe.sem_clear(v_ready)
                pe.wait_ge(kT_ready, 1)
                pe.sem_clear(kT_ready)
                for u in range(UN0 + 3):
                    if u < UN0:
                        scores(u)
                    if u >= 3:
                        values(u - 3)
                    if u == PRE0:
                        pre.pe(pe, b + 1)
                    if u == PRE0 + 1:
                        pe.wait_ge(pre.t_free, 1)
                    if 2 <= u < UN0 + 2:
                        transposes(u - 2)
                pe.wait_ge(on_ready, 1)
                pe.sem_clear(on_ready)
                for t in range(TB):
                    r = pe.transpose(c.ps[4][:, t * P:(t + 1) * P], o[:, t, :, :].rearrange("p h d -> p (h d)"),
                                     c.ident[:])
                r.then_inc(oT_ps, 1)
                pe.wait_ge(oT_ready, 1)
                pe.sem_clear(oT_ready)
                pe.wait_ge(y_free, 1)
                pe.sem_clear(y_free)
                pe.wait_ge(pre.t_free, 1)
                pe.sem_clear(pre.t_free)
                for t in range(TB):
                    r = pe.matmul(c.ps[7][:, t * P:(t + 1) * P], oT[:, t * P:(t + 1) * P], wo[:],
                                  start=True, stop=True)
                r.then_inc(y_ready, 1)
            for i in range(2):
                pe.wait_ge(o_free[i], 1)
                pe.sem_clear(o_free[i])
                pe.wait_ge(s_free[i], 1)
                pe.sem_clear(s_free[i])
            pe.wait_ge(y_free, 1)
            pe.sem_clear(y_free)
            pe.wait_ge(pre.t_free, 1)
            pe.sem_clear(pre.t_free)
            pe.wait_ge(pre.xT_ready, 1)
            pe.sem_clear(pre.xT_ready)
            pe.wait_ge(pre.xTs_ready, 1)
            pe.sem_clear(pre.xTs_ready)

        @block.scalar
        def _(a):
            st.wait_loads(a)
            pre.seed_act(a)
            pre.act(a, 0)
            with a.Fori(0, B) as b:
                a.wait_ge(ms_ready, 1)
                a.sem_clear(ms_ready)
                a.activation(rstd[:], rstd[:], ACT.Sqrt).then_inc(rs_ready, 1)
                a.wait_ge(tr_ready[0], 1)
                a.sem_clear(tr_ready[0])
                a.activation(qT[:], c.ps[4], ACT.Copy).then_inc(qT_dve, 1)
                a.drain().then_inc(qT_pool, 1)
                for u in range(UN0 + 2):
                    if u == PRE0:
                        pre.act(a, b + 1)
                    if u < UN0:
                        w = width(u % TB)
                        a.wait_ge(m_ready[u % 4], 1)
                        a.sem_clear(m_ready[u % 4])
                        for j in range(HG):
                            e = pr[:, u % 4, j, 0:w]
                            r = a.activation(e, e, ACT.Exp, bias=nm[:, u, j:j + 1])
                        r.then_inc(p_ready[u % 4], 1)
                    if u >= 2 and (u - 2) % TB:
                        a.wait_ge(ht_ps, 1)
                        a.sem_clear(ht_ps)
                        a.activation(hT[:], c.ps[7][0:WIN, :], ACT.Copy).then_inc(ht_ready, 1)
                a.wait_ge(oT_ps, 1)
                a.sem_clear(oT_ps)
                a.activation(oT[:], c.ps[4][:], ACT.Copy).then_inc(oT_ready, 1)

        @block.vector
        def _(v):
            ch = Chain(v, core.lasting_sem("dve_chain"))
            ch.reset()
            st.wait_loads(v)
            v.memset(vh[:], 1.0)
            ch.link(v.memset(va[:], 1.0))
            ch.link(v.tensor_scalar(nw[:, 0, :], nw[:, 0, :], float(HD) ** -0.5, None, ALU.mult))
            ch.link(v.tensor_copy(nwf[:].rearrange("p (a h) d -> p a h d", a=2),
                                  nw[:].unsqueeze(2).broadcast_to((P, 2, H, HD))))
            for i in range(2):
                v.sem_inc(o_free[i], 1)
                v.sem_inc(s_free[i], 1)
            v.sem_inc(y_free, 1)

            def normalise():
                v.wait_ge(qk_ps, 1)
                v.sem_clear(qk_ps)
                ch.link(v.tensor_tensor(raw[:].rearrange("p (t h) d -> p t (h d)", t=TB),
                                        c.psum[:, 0:2, :].rearrange("p a (t n) -> p (a t) n", t=2),
                                        bqk[:].unsqueeze(1).broadcast_to((P, TB, 2 * D)), ALU.add))
                v.sem_inc(s_free[0], 1)
                ch.link(v.tensor_scalar(raw[:], raw[:], CLIP, -CLIP, ALU.min, ALU.max))
                ch.link(v.tensor_tensor(sq[:], raw[:], raw[:], ALU.mult))
                ch.link(v.tensor_reduce(rstd[:, :, 0], sq[:], AX.X, ALU.add))
                ch.link(v.tensor_scalar(rstd[:], rstd[:], 1.0 / HD, QK_EPS, ALU.mult, ALU.max))
                v.tensor_scalar(rstd[:], rstd[:], QK_EPS, None, ALU.add).then_inc(ms_ready, 1)
                v.wait_ge(v_ps, 1)
                v.sem_clear(v_ps)
                bh = bv[:].rearrange("p (h d) -> p h d", h=H)
                v.tensor_tensor(va[:, :, :, 0:HD], c.ps[2].rearrange("p (t h d) -> p t h d", t=TB, h=H),
                                bh.unsqueeze(1).broadcast_to((P, TB, H, HD)), ALU.add)
                ch.link(v.tensor_tensor(vh[:, 1:TB, :, 0:HD],
                                        c.ps[3][0:WIN, P:].rearrange("p (t h d) -> p t h d", t=TB - 1, h=H),
                                        bh[0:WIN].unsqueeze(1).broadcast_to((WIN, TB - 1, H, HD)), ALU.add))
                v.sem_inc(s_free[1], 1)
                v.sem_inc(v_ready, 1)
                v.wait_ge(rs_ready, 1)
                v.sem_clear(rs_ready)
                ch.link(v.reciprocal(rstd[:], rstd[:]))
                ch.link(v.tensor_tensor(raw[:], raw[:], rstd[:].broadcast_to((P, TB * NH, HD)), ALU.mult))
                v.tensor_tensor(qk[:].rearrange("p t a n -> p t (a n)"), raw[:].rearrange("p (t h) d -> p t (h d)", t=TB),
                                nwf[:].rearrange("p h d -> p (h d)").unsqueeze(1).broadcast_to((P, TB, 2 * D)),
                                ALU.mult).then_inc(qk_ready, 1)

            def norm(g):
                i = g % 2
                v.wait_ge(o_ready[i], 1)
                v.sem_clear(o_ready[i])
                ov = c.ps[6 - i][:, 0:UN0 * VW].rearrange("p (t j w) -> p t j w", t=TB, w=VW)
                ch.link(v.reciprocal(rec[:], ov[:, :, :, HD:VW]))
                ch.link(v.tensor_tensor(o[:, :, g * HG:(g + 1) * HG, :], ov[:, :, :, 0:HD],
                                        rec[:].broadcast_to((P, TB, HG, HD)), ALU.mult))
                v.sem_inc(o_free[i], 1)

            pre.dve(v, ch, 0)
            with v.Fori(0, B) as b:
                ch.reset()
                normalise()
                v.wait_ge(tr_ready[1], 1)
                v.sem_clear(tr_ready[1])
                v.tensor_copy(kT[:], c.ps[5]).then_inc(kT_ready, 1)
                v.wait_ge(qT_dve, 1)
                v.sem_clear(qT_dve)
                for h in range(H // 2):
                    r = v.tensor_scalar(qz[:, h, :], qT[:], hm[:, h:h + 1], None, ALU.mult)
                    if h % HG == HG - 1:
                        r.then_inc(qz_ready[0], 1)
                for u in range(UN0 + 3):
                    if u == 4:
                        pre.dve(v, ch, b + 1)
                    if u < UN0:
                        w = width(u % TB)
                        e = pr[:, u % 4, :, 0:w]
                        v.wait_ge(s_ready[u % 2], 1)
                        v.sem_clear(s_ready[u % 2])
                        ch.link(v.tensor_tensor(e, score_slot(u % 2, w),
                                                window[:, SPAN - w:].unsqueeze(1).broadcast_to((P, HG, w)), ALU.add))
                        v.sem_inc(s_free[u % 2], 1)
                        v.tensor_reduce(nm[:, u, :], e, AX.X, ALU.max, negate=True).then_inc(m_ready[u % 4], 1)
                    if 2 <= u < UN0 + 2:
                        v.wait_ge(pt_ps, 1)
                        v.sem_clear(pt_ps)
                        v.tensor_copy(pT[:], c.ps[4][:]).then_inc(pt_ready, 1)
                    if u >= TB + 3 and (u - 3) % TB == 0 and u < UN0 + 3:
                        norm((u - 3) // TB - 1)
                norm(G - 1)
                v.sem_inc(on_ready, 1)
                v.wait_ge(y_ready, 1)
                v.sem_clear(y_ready)
                ch.link(v.tensor_tensor(y[:], c.ps[7].rearrange("p (a b) -> p a b", a=TB),
                                        bo[:].unsqueeze(1).broadcast_to((P, TB, D)), ALU.add))
                v.sem_inc(y_free, 1)
                v.sem_inc(pre.t_free, 1)
                post.dve_stats(v, ch, lambda t: y[:, t, :])
                post.dve_add(v, ch, b, lambda t: y[:, t, :])
            pre.drain_dve(v)
    st.ctx.close()



def stage_attn1(core):
    st = Stage(core, "a1")
    c, nc, s = core, core.nc, core.sem
    wq, wk, wv = (st.load(n, [P, D]) for n in ("wq", "wk", "wv"))
    bq, bk, bv = st.load("bq", [P, 1]), st.load("bk", [P, 1]), st.load("bv", [P, D])
    causal = st.load("causal", [P, P])
    scale = float(D) ** -0.5
    pre, post = Pre(st, static=True), Post(st)
    q, k = st.sb("q", [P, L]), st.sb("k", [P, L])
    vv = st.sb("v", [P, TB, D])
    pr = st.sb("probs", [P, TB, L])
    prT = st.sb("probsT", [P, 2, L])
    nm, den = st.sb("negmax", [P, TB]), st.sb("den", [P, TB])
    y = st.sb("y", [P, TB, D])
    q_ps, k_ps, v_ps = s("q_ps"), s("k_ps"), s("v_ps")
    qk_ready, v_ready = s("qk_ready"), s("v_ready")
    s_ready = [s(f"scores{i}_ready") for i in range(4)]
    m_ready = [s(f"max{i}_ready") for i in range(4)]
    p_ready = [s(f"probs{i}_ready") for i in range(4)]
    pt_ready = [s(f"probsT{i}_ps") for i in range(4)]
    pts_ready = [s(f"probsT{i}_ready") for i in range(4)]
    o_ready, y_free = s("out_ready"), s("out_free")
    with nc.Block() as block:
        @block.sync
        def _(sp):
            st.issue_loads(sp)

        @block.gpsimd
        def _(g):
            ch = Chain(g, core.lasting_sem("pool_chain"))
            ch.reset()
            pre.pool(g, ch, 0)
            with g.Fori(0, B) as b:
                ch.reset()
                pre.pool(g, ch, b + 1)
                post.pool(g, ch)

        @block.tensor
        def _(pe):
            def av(qb):
                pe.wait_ge(pts_ready[qb], 1)
                pe.sem_clear(pts_ready[qb])
                for kb in range(qb + 1):
                    r = pe.matmul(c.ps[6][:, qb * P:(qb + 1) * P], prT[:, qb % 2, kb * P:(kb + 1) * P],
                                  vv[:, kb, :], start=(kb == 0), stop=(kb == qb))
                return r

            st.wait_loads(pe)
            pre.seed_pe(pe)
            pre.pe(pe, 0)
            with pe.Fori(0, B) as b:
                pe.wait_ge(pre.xT_ready, 1)
                pe.sem_clear(pre.xT_ready)
                pe.wait_ge(pre.xTs_ready, 1)
                pe.sem_clear(pre.xTs_ready)
                xb = c.xT[:, bass.ds(b * L, L)]
                pe.matmul(c.ps[0][:], wq[:], xb, start=True, stop=True).then_inc(q_ps, 1)
                pe.matmul(c.ps[1][:], wk[:], xb, start=True, stop=True).then_inc(k_ps, 1)
                for t in range(TB):
                    r = pe.matmul(c.ps[2][:, t * P:(t + 1) * P], pre.xTs[:, t * P:(t + 1) * P], wv[:],
                                  start=True, stop=True)
                r.then_inc(v_ps, 1)
                pe.drain().then_inc(pre.xTs_free, 1)
                pe.wait_ge(qk_ready, 1)
                pe.sem_clear(qk_ready)
                pe.wait_ge(v_ready, 1)
                pe.sem_clear(v_ready)
                for qb in (3, 2, 1, 0):
                    n = (qb + 1) * P
                    pe.matmul(c.ps[qb][:, 0:n], q[:, qb * P:n], k[:, 0:n], start=True,
                              stop=True).then_inc(s_ready[qb], 1)
                pre.pe(pe, b + 1)
                pe.wait_ge(y_free, 1)
                pe.sem_clear(y_free)
                for qb in (3, 2, 1, 0):
                    pe.wait_ge(p_ready[qb], 1)
                    pe.sem_clear(p_ready[qb])
                    for kb in range(qb + 1):
                        r = pe.transpose(c.ps[4 + qb % 2][:, kb * P:(kb + 1) * P],
                                         pr[:, qb, kb * P:(kb + 1) * P], c.ident[:])
                    r.then_inc(pt_ready[qb], 1)
                    if qb < 3:
                        av(qb + 1)
                av(0).then_inc(o_ready, 1)
            pe.wait_ge(y_free, 1)
            pe.sem_clear(y_free)
            pe.wait_ge(pre.t_free, 1)
            pe.sem_clear(pre.t_free)
            pe.wait_ge(pre.xT_ready, 1)
            pe.sem_clear(pre.xT_ready)
            pe.wait_ge(pre.xTs_ready, 1)
            pe.sem_clear(pre.xTs_ready)

        @block.scalar
        def _(a):
            ch = Chain(a, core.lasting_sem("act_chain"))
            ch.reset()
            st.wait_loads(a)
            pre.seed_act(a)
            pre.act(a, 0)
            with a.Fori(0, B) as b:
                ch.reset()
                a.wait_ge(q_ps, 1)
                a.sem_clear(q_ps)
                a.activation(q[:], c.ps[0][:], ACT.Identity, bias=bq[:])
                a.wait_ge(k_ps, 1)
                a.sem_clear(k_ps)
                a.activation(k[:], c.ps[1][:], ACT.Identity, bias=bk[:]).then_inc(qk_ready, 1)
                pre.act(a, b + 1)
                for qb in (3, 2, 1, 0):
                    n = (qb + 1) * P
                    a.wait_ge(m_ready[qb], 1)
                    a.sem_clear(m_ready[qb])
                    a.activation(pr[:, qb, 0:n], c.ps[qb][:, 0:n], ACT.Exp, bias=nm[:, qb:qb + 1], scale=scale,
                                 accum_out=den[:, qb:qb + 1]).then_inc(p_ready[qb], 1)
                    if qb == 2:
                        a.wait_ge(pt_ready[3], 1)
                        a.sem_clear(pt_ready[3])
                        a.activation(prT[:, 1, :], c.ps[5][:], ACT.Copy).then_inc(pts_ready[3], 1)

        @block.vector
        def _(v):
            ch = Chain(v, core.lasting_sem("dve_chain"))
            ch.reset()
            st.wait_loads(v)
            v.sem_inc(y_free, 1)
            pre.dve(v, ch, 0)
            with v.Fori(0, B) as b:
                ch.reset()
                v.wait_ge(v_ps, 1)
                v.sem_clear(v_ps)
                v.tensor_tensor(vv[:], c.ps[2][:].rearrange("p (a b) -> p a b", a=TB),
                                bv[:].unsqueeze(1).broadcast_to((P, TB, D)), ALU.add).then_inc(v_ready, 1)
                pre.dve(v, ch, b + 1)
                for qb in (3, 2, 1, 0):
                    n = (qb + 1) * P
                    v.wait_ge(s_ready[qb], 1)
                    v.sem_clear(s_ready[qb])
                    dg = c.ps[qb][:, qb * P:n]
                    ch.link(v.tensor_tensor(dg, dg, causal[:], ALU.add))
                    ch.link(v.tensor_reduce(nm[:, qb:qb + 1], c.ps[qb][:, 0:n], AX.X, ALU.max, negate=True))
                    v.tensor_scalar(nm[:, qb:qb + 1], nm[:, qb:qb + 1], scale, None, ALU.mult).then_inc(m_ready[qb], 1)
                for qb in (2, 1, 0):
                    n = (qb + 1) * P
                    v.wait_ge(pt_ready[qb], 1)
                    v.sem_clear(pt_ready[qb])
                    v.tensor_copy(prT[:, qb % 2, 0:n], c.ps[4 + qb % 2][:, 0:n]).then_inc(pts_ready[qb], 1)
                v.wait_ge(o_ready, 1)
                v.sem_clear(o_ready)
                ch.link(v.reciprocal(den[:], den[:]))
                for t in range(TB):
                    r = v.tensor_scalar(y[:, t, :], c.ps[6][:, t * P:(t + 1) * P], den[:, t:t + 1], None, ALU.mult)
                ch.link(r)
                v.sem_inc(y_free, 1)
                post.dve_stats(v, ch, lambda t: y[:, t, :])
                post.dve_add(v, ch, b, lambda t: y[:, t, :])
            pre.drain_dve(v)
    st.ctx.close()



LAT = 32


def stage_attn3(core):
    st = Stage(core, "a3")
    c, nc, s = core, core.nc, core.sem
    wq, bqk = st.load("wq", [P, D]), st.load("bqk", [P, 2, D])
    wd, bd = st.load("wd", [P, LAT]), st.load("bd", [LAT, 1])
    wkv, bv = st.load("wkv", [LAT, 2 * D]), st.load("bv", [P, D])
    cos, sin = st.load("cos", [P, TB, HD]), st.load("sin", [P, TB, HD])
    wo, bo = st.load("wo", [P, D]), st.load("bo", [P, D])
    scale = float(HD) ** -0.5
    pre, post = Pre(st, static=True), Post(st)
    lat = st.sb("lat", [LAT, L])
    raw = st.sb("raw", [P, TB, 2, D])
    rot, rot2 = st.sb("rot", [P, TB, 2, D]), st.sb("rot2", [P, TB, 2, D])
    vv = st.sb("v", [P, TB, D])
    prod = st.sb("prod", [P, 2, H * H, HD])
    pv = st.sb("pv", [P, 2, H * HD, H])
    sc = st.sb("scores", [P, 2, H, H])
    nm = st.sb("max", [P, 2, H, 1])
    den = st.sb("den", [P, 2, H, 1])
    o = st.sb("o", [P, TB, H, HD])
    oT, y = st.sb("oT", [P, L]), st.sb("y", [P, TB, D])
    lat_ps, lat_ready = s("lat_ps"), s("lat_ready")
    q_ps, kv_ps = s("q_ps"), s("kv_ps")
    bank_free = s("proj_free")
    rot_ready = s("rot_ready")
    prod_ready = [s(f"prod{i}_ready") for i in range(2)]
    prod_free = [s(f"prod{i}_free") for i in range(2)]
    s_ready = [s(f"scores{i}_ready") for i in range(2)]
    p_ready = [s(f"probs{i}_ready") for i in range(2)]
    p_sum = [s(f"probs{i}_sum") for i in range(2)]
    pv_ready = [s(f"pv{i}_ready") for i in range(2)]
    pv_free = [s(f"pv{i}_free") for i in range(2)]
    on_ready, oT_ps, oT_ready, y_ready = s("on_ready"), s("oT_ps"), s("oT_ready"), s("y_ready")
    y_free = s("y_free")

    with nc.Block() as block:
        @block.sync
        def _(sp):
            st.issue_loads(sp)

        @block.gpsimd
        def _(g):
            ch = Chain(g, core.lasting_sem("pool_chain"))
            ch.reset()

            def scores(t):
                i = t % 2
                g.wait_ge(prod_free[i], 1)
                g.sem_clear(prod_free[i])
                for h in range(0, H, 4):
                    qh = rot[:, t, 0, h * HD:(h + 4) * HD].rearrange("p (h d) -> p h d", d=HD)
                    kk = rot[:, t, 1, :].rearrange("p (g d) -> p g d", d=HD)
                    r = g.tensor_tensor(prod[:, i, h * H:(h + 4) * H, :].rearrange("p (h g) d -> p h g d", h=4),
                                        qh.unsqueeze(2).broadcast_to((P, 4, H, HD)),
                                        kk.unsqueeze(1).broadcast_to((P, 4, H, HD)), ALU.mult)
                r.then_inc(prod_ready[i], 1)

            def values(t):
                i = t % 2
                g.wait_ge(p_ready[i], 1)
                g.sem_clear(p_ready[i])
                g.wait_ge(pv_free[i], 1)
                g.sem_clear(pv_free[i])
                for h in range(0, H, 4):
                    ph = sc[:, i, h:h + 4, :]
                    vt = vv[:, t, :].rearrange("p (g d) -> p d g", d=HD)
                    r = g.tensor_tensor(pv[:, i, h * HD:(h + 4) * HD, :].rearrange("p (h d) g -> p h d g", h=4),
                                        ph.unsqueeze(2).broadcast_to((P, 4, HD, H)),
                                        vt.unsqueeze(1).broadcast_to((P, 4, HD, H)), ALU.mult)
                r.then_inc(pv_ready[i], 1)

            pre.pool(g, ch, 0)
            with g.Fori(0, B) as b:
                ch.reset()
                g.wait_ge(rot_ready, 1)
                g.sem_clear(rot_ready)
                for t in range(TB + 1):
                    if t < TB:
                        scores(t)
                    if t >= 1:
                        values(t - 1)
                    if t == 1:
                        pre.pool(g, ch, b + 1)
                post.pool(g, ch)
            for i in range(2):
                g.wait_ge(prod_free[i], 1)
                g.sem_clear(prod_free[i])
                g.wait_ge(pv_free[i], 1)
                g.sem_clear(pv_free[i])

        @block.tensor
        def _(pe):
            st.wait_loads(pe)
            pre.seed_pe(pe)
            pre.pe(pe, 0)
            with pe.Fori(0, B) as b:
                pe.wait_ge(pre.xT_ready, 1)
                pe.sem_clear(pre.xT_ready)
                pe.wait_ge(pre.xTs_ready, 1)
                pe.sem_clear(pre.xTs_ready)
                pe.wait_ge(bank_free, 1)
                pe.sem_clear(bank_free)
                pe.matmul(c.ps[3][0:LAT, :], wd[:], pre.xTs[:], start=True, stop=True).then_inc(lat_ps, 1)
                for t in range(TB):
                    r = pe.matmul(c.ps[0][:, t * P:(t + 1) * P], pre.xTs[:, t * P:(t + 1) * P], wq[:],
                                  start=True, stop=True)
                r.then_inc(q_ps, 1)
                pe.drain().then_inc(pre.xTs_free, 1)
                pe.wait_ge(lat_ready, 1)
                pe.sem_clear(lat_ready)
                for t in range(TB):
                    r = pe.matmul(c.ps[1 + t // 2][:, (t % 2) * 2 * D:(t % 2 + 1) * 2 * D],
                                  lat[:, t * P:(t + 1) * P], wkv[:], start=True, stop=True)
                r.then_inc(kv_ps, 1)
                pre.pe(pe, b + 1)
                pe.wait_ge(on_ready, 1)
                pe.sem_clear(on_ready)
                for t in range(TB):
                    r = pe.transpose(c.ps[4][:, t * P:(t + 1) * P], o[:, t, :, :].rearrange("p h d -> p (h d)"),
                                     c.ident[:])
                r.then_inc(oT_ps, 1)
                pe.wait_ge(oT_ready, 1)
                pe.sem_clear(oT_ready)
                pe.wait_ge(y_free, 1)
                pe.sem_clear(y_free)
                for t in range(TB):
                    r = pe.matmul(c.ps[5][:, t * P:(t + 1) * P], oT[:, t * P:(t + 1) * P], wo[:],
                                  start=True, stop=True)
                r.then_inc(y_ready, 1)
            pe.wait_ge(bank_free, 1)
            pe.sem_clear(bank_free)
            pe.wait_ge(y_free, 1)
            pe.sem_clear(y_free)
            pe.wait_ge(pre.t_free, 1)
            pe.sem_clear(pre.t_free)
            pe.wait_ge(pre.xT_ready, 1)
            pe.sem_clear(pre.xT_ready)
            pe.wait_ge(pre.xTs_ready, 1)
            pe.sem_clear(pre.xTs_ready)

        @block.scalar
        def _(a):
            st.wait_loads(a)
            pre.seed_act(a)
            pre.act(a, 0)
            with a.Fori(0, B) as b:
                a.wait_ge(lat_ps, 1)
                a.sem_clear(lat_ps)
                a.activation(lat[:], c.ps[3][0:LAT, :], ACT.Identity, bias=bd[:]).then_inc(lat_ready, 1)
                for t in range(TB):
                    if t == 2:
                        pre.act(a, b + 1)
                    i = t % 2
                    a.wait_ge(s_ready[i], 1)
                    a.sem_clear(s_ready[i])
                    a.activation(sc[:, i, :, :], sc[:, i, :, :], ACT.Exp, scale=scale).then_inc(p_ready[i], 1)
                    a.drain().then_inc(p_sum[i], 1)
                a.wait_ge(oT_ps, 1)
                a.sem_clear(oT_ps)
                a.activation(oT[:], c.ps[4][:], ACT.Copy).then_inc(oT_ready, 1)

        @block.vector
        def _(v):
            ch = Chain(v, core.lasting_sem("dve_chain"))
            ch.reset()
            st.wait_loads(v)
            for i in range(2):
                v.sem_inc(prod_free[i], 1)
                v.sem_inc(pv_free[i], 1)
            v.sem_inc(bank_free, 1)
            v.sem_inc(y_free, 1)

            def rotate():
                v.wait_ge(q_ps, 1)
                v.sem_clear(q_ps)
                v.tensor_tensor(raw[:, :, 0, :], c.ps[0].rearrange("p (t n) -> p t n", t=TB),
                                bqk[:, 0, :].unsqueeze(1).broadcast_to((P, TB, D)), ALU.add)
                v.wait_ge(kv_ps, 1)
                v.sem_clear(kv_ps)
                kv = c.psum[:, 1:3, :].rearrange("p a (t n) -> p (a t) n", t=2)
                v.tensor_tensor(vv[:], kv[:, :, D:], bv[:].unsqueeze(1).broadcast_to((P, TB, D)), ALU.add)
                ch.link(v.tensor_tensor(raw[:, :, 1, :], kv[:, :, 0:D],
                                        bqk[:, 1, :].unsqueeze(1).broadcast_to((P, TB, D)), ALU.add))
                v.sem_inc(bank_free, 1)
                half = HD // 2
                for t in range(TB):
                    x = raw[:, t, :, :].rearrange("p a (h d) -> p (a h) d", d=HD)
                    x1 = rot[:, t, :, :].rearrange("p a (h d) -> p (a h) d", d=HD)
                    x2 = rot2[:, t, :, :].rearrange("p a (h d) -> p (a h) d", d=HD)
                    v.tensor_tensor(x1, x, cos[:, t, :].unsqueeze(1).broadcast_to((P, 2 * H, HD)), ALU.mult)
                    v.tensor_tensor(x2[:, :, 0:half], x[:, :, half:HD],
                                    sin[:, t, 0:half].unsqueeze(1).broadcast_to((P, 2 * H, half)), ALU.mult)
                    r = v.tensor_tensor(x2[:, :, half:HD], x[:, :, 0:half],
                                        sin[:, t, half:HD].unsqueeze(1).broadcast_to((P, 2 * H, half)), ALU.mult)
                ch.link(r)
                ch.link(v.tensor_tensor(rot[:], rot[:], rot2[:], ALU.add))
                v.sem_inc(rot_ready, 1)

            def scores(t):
                i = t % 2
                v.wait_ge(prod_ready[i], 1)
                v.sem_clear(prod_ready[i])
                ch.link(v.tensor_reduce(sc[:, i, :, :].rearrange("p h g -> p (h g)"), prod[:, i, :, :], AX.X, ALU.add))
                v.sem_inc(prod_free[i], 1)
                ch.link(v.tensor_reduce(nm[:, i, :, 0], sc[:, i, :, :], AX.X, ALU.max))
                v.tensor_tensor(sc[:, i, :, :], sc[:, i, :, :], nm[:, i, :, :].broadcast_to((P, H, H)),
                                ALU.subtract).then_inc(s_ready[i], 1)

            def values(t):
                i = t % 2
                v.wait_ge(p_sum[i], 1)
                v.sem_clear(p_sum[i])
                ch.link(v.tensor_reduce(den[:, i, :, 0], sc[:, i, :, :], AX.X, ALU.add))
                ch.link(v.reciprocal(den[:, i, :, :], den[:, i, :, :]))
                v.wait_ge(pv_ready[i], 1)
                v.sem_clear(pv_ready[i])
                ch.link(v.tensor_reduce(o[:, t, :, :].rearrange("p h d -> p (h d)"), pv[:, i, :, :], AX.X, ALU.add))
                v.sem_inc(pv_free[i], 1)
                ch.link(v.tensor_tensor(o[:, t, :, :], o[:, t, :, :], den[:, i, :, :].broadcast_to((P, H, HD)),
                                        ALU.mult))

            pre.dve(v, ch, 0)
            with v.Fori(0, B) as b:
                ch.reset()
                rotate()
                for t in range(TB + 1):
                    if t < TB:
                        scores(t)
                    if t == 1:
                        pre.dve(v, ch, b + 1)
                    if t >= 1:
                        values(t - 1)
                v.sem_inc(on_ready, 1)
                v.wait_ge(y_ready, 1)
                v.sem_clear(y_ready)
                ch.link(v.tensor_tensor(y[:], c.ps[5].rearrange("p (a b) -> p a b", a=TB),
                                        bo[:].unsqueeze(1).broadcast_to((P, TB, D)), ALU.add))
                v.sem_inc(y_free, 1)
                post.dve_stats(v, ch, lambda t: y[:, t, :])
                post.dve_add(v, ch, b, lambda t: y[:, t, :])
            pre.drain_dve(v)
    st.ctx.close()



DH, NPAIR = 64, 8
NU = 2 * TB
LEVELS = 7
KCONV = 4
TURNS = B * NPAIR // 2
DELTA_EPS = 1e-6
RANK = 64
WCOLS = 5 * P + 2


def stage_delta_in(core):
    st = Stage(core, "d")
    c, nc, s = core, core.nc, core.sem
    gamma, cw, cb = st.load("gamma", [P, 1]), st.load("cw", [P, KCONV]), st.load("cb", [P, 1])
    bw, bb = st.load("betaw", [P, 2 * NPAIR]), st.load("betab", [P, 2 * NPAIR])
    pre = Pre(st, inner="rms", eps=DELTA_EPS)
    pad = KCONV - 1
    hp = st.sb("hp", [P, pad + L])
    cv = st.sb("cv", [P, 2, L])
    hs = st.sb("hs", [P, L])
    bt = st.sb("bt", [P, TB, 2 * NPAIR])
    t_ready, t_free = s("pre_t_ready"), s("pre_t_free")
    hp_ready, cv_ready, hs_ready, hs_free = s("conv_in_ready"), s("conv_ready"), s("hs_ready"), s("hs_free")
    b_ps, b_ready, b_done, bank_free = s("beta_ps"), s("beta_ready"), s("beta_done"), s("beta_bank_free")
    with nc.Block() as block:
        @block.sync
        def _(sp):
            st.issue_loads(sp)

        @block.gpsimd
        def _(g):
            ch = Chain(g, core.lasting_sem("pool_chain"))
            with g.Fori(0, B) as b:
                ch.reset()
                pre.pool(g, ch, b)

        @block.tensor
        def _(pe):
            st.wait_loads(pe)
            pe.sem_inc(pre.y_free, 1)
            pe.sem_inc(hs_free, 1)
            with pe.Fori(0, B) as b:
                pe.wait_ge(pre.y_ready, 1)
                pe.sem_clear(pre.y_ready)
                pe.wait_ge(t_free, 1)
                pe.sem_clear(t_free)
                for t in range(TB):
                    r = pe.transpose(c.ps[7][:, t * P:(t + 1) * P], pre.y2[:, t, :], c.ident[:])
                r.then_inc(t_ready, 1)
                pe.drain().then_inc(pre.y_free, 1)
                pe.wait_ge(hs_ready, 1)
                pe.sem_clear(hs_ready)
                pe.wait_ge(bank_free, 1)
                pe.sem_clear(bank_free)
                for t in range(TB):
                    r = pe.matmul(c.ps[6][:, t * 2 * NPAIR:(t + 1) * 2 * NPAIR], hs[:, t * P:(t + 1) * P], bw[:],
                                  start=True, stop=True)
                r.then_inc(b_ps, 1)
                pe.drain().then_inc(hs_free, 1)
            pe.wait_ge(t_free, 1)
            pe.sem_clear(t_free)
            pe.wait_ge(bank_free, 1)
            pe.sem_clear(bank_free)

        @block.scalar
        def _(a):
            ch = Chain(a, core.lasting_sem("act_chain"))
            st.wait_loads(a)
            a.sem_inc(t_free, 1)
            with a.Fori(0, B) as b:
                ch.reset()
                a.wait_ge(t_ready, 1)
                a.sem_clear(t_ready)
                a.activation(hp[:, pad:], c.ps[7], ACT.Identity, scale=gamma[:]).then_inc(hp_ready, 1)
                a.drain().then_inc(t_free, 1)
                a.wait_ge(cv_ready, 1)
                a.sem_clear(cv_ready)
                a.wait_ge(hs_free, 1)
                a.sem_clear(hs_free)
                a.activation(c.xT[:, bass.ds(b * L, L)], cv[:, 1, :], ACT.Silu, bias=cb[:])
                a.activation(hs[:], cv[:, 1, :], ACT.Silu, bias=cb[:]).then_inc(hs_ready, 1)
                a.wait_ge(b_ready, 1)
                a.sem_clear(b_ready)
                ch.link(a.activation(c.beta[:, :, bass.ds(b * TB, TB), :],
                                     bt[:].rearrange("p t (a h) -> p a t h", h=2), ACT.Sigmoid))
                a.sem_inc(b_done, 1)
            a.wait_ge(hs_free, 1)
            a.sem_clear(hs_free)

        @block.vector
        def _(v):
            ch = Chain(v, core.lasting_sem("dve_chain"))
            ch.reset()
            st.wait_loads(v)
            ch.link(v.memset(hp[:], 0.0))
            v.sem_inc(bank_free, 1)
            with v.Fori(0, B) as b:
                ch.reset()
                pre.dve(v, ch, b)
                v.wait_ge(hp_ready, 1)
                v.sem_clear(hp_ready)
                ch.link(v.tensor_scalar(cv[:, 0, :], hp[:, 0:L], cw[:, 0:1], None, ALU.mult))
                for k in range(1, KCONV):
                    r = v.scalar_tensor_tensor(cv[:, k % 2, :], hp[:, k:k + L], cw[:, k:k + 1],
                                               cv[:, (k + 1) % 2, :], ALU.mult, ALU.add)
                    ch.link(r)
                v.sem_inc(cv_ready, 1)
                v.wait_ge(b_ps, 1)
                v.sem_clear(b_ps)
                ch.link(v.tensor_tensor(bt[:], c.ps[6][:, 0:TB * 2 * NPAIR].rearrange("p (t h) -> p t h", t=TB),
                                        bb[:].unsqueeze(1).broadcast_to((P, TB, 2 * NPAIR)), ALU.add))
                v.sem_inc(bank_free, 1)
                v.sem_inc(b_ready, 1)
                v.wait_ge(b_done, 1)
                v.sem_clear(b_done)
            v.wait_ge(pre.y_free, 1)
            v.sem_clear(pre.y_free)
            v.memset(c.xn[:], 0.0)
    st.ctx.close()


def stage_delta(core):
    st = Stage(core, "e")
    c, nc, s = core, core.nc, core.sem
    load = st.load
    A, Bp = 0, 1
    both = (A, Bp)
    two = lambda name, shape: [st.sb(f"{name}{X}", shape) for X in both]
    tokens = lambda name: [s(f"{name}{X}") for X in both]
    low = load("low", [P, LEVELS, DH])
    lowi = st.sb("lowi", [P, LEVELS, DH], I32)
    heads2 = load("heads2", [P, 2])
    ow = load("ow", [P, NPAIR, D])
    hs = st.sb("hs", [P, L])
    hnw = load("hnw", [P, NPAIR])
    W = two("w", [P, WCOLS])
    k, kq = two("k", [P, L]), two("kq", [P, 2, L])
    pr, su = two("pre", [P, L]), two("suf", [P, L])
    ks, kp = two("ks", [P, 2, L]), two("kp", [P, 2, TB, 2, DH])
    N = two("N", [P, NU * P])
    Z = two("Z", [P, LEVELS, NU * P])
    T, TT, AT = two("T", [P, NU * P]), two("TT", [P, NU * P]), two("AT", [P, NU * P])
    ket, bv, tot = two("ket", [P, TB, P]), two("bv", [P, TB, P]), two("tot", [P, TB])
    S, U = two("S", [P, P]), two("U", [P, P])
    ysb, ms = two("ysb", [P, TB, P]), two("ms", [P, NU])
    rr = two("rr", [P, 2, NU, 1])
    rq, rq2 = two("rq", [P, NU]), two("rq2", [P, NU])
    be = su
    sq = [kp[X][:].rearrange("p a t n j -> p a (t n j)") for X in both]
    ysq = ket
    yT = [flat(ysb[X]) for X in both]
    w_ready, w_free = tokens("w_ready"), tokens("w_free")
    hs_ready, hs_free = s("hs_ready"), s("hs_free")
    qk_ps, v_ps = tokens("qk_ps"), tokens("v_ps")
    a_ps, be_ps = tokens("alpha_ps"), tokens("beta_ps")
    v_read = tokens("v_read")
    sq_ready, ss_ps, rn_ready = tokens("sq_ready"), tokens("ss_ps"), tokens("root_ready")
    rk_ready, rk_ps = tokens("rk_ready"), tokens("rk_ps")
    al_ready = tokens("alpha_ready")
    kq_ready, kq_pe = tokens("kq_ready"), tokens("kq_to_pe")
    lv_ready = [[s(f"scaled{X}{i}_ready") for i in range(2)] for X in both]
    lv_free = [[s(f"scaled{X}{i}_free") for i in range(2)] for X in both]
    heads = lambda name: [s(f"{name}{q}") for q in range(4)]
    gr_ps, gr_free = heads("gram_ps"), heads("gram_free")
    n_ready = heads("N_ready")
    z_ps, z_ready = heads("Z_ps"), heads("Z_ready")
    tt_ps, tt_ready = heads("TT_ps"), heads("TT_ready")
    t_ps, t_ready = heads("T_ps"), heads("T_ready")
    chain_in, ke_ps, ket_ready = tokens("chain_in"), tokens("ke_ps"), tokens("ket_ready")
    p_ps, r_ready, u_ps, u_ready = tokens("P_ps"), tokens("R_ready"), tokens("U_ps"), tokens("U_ready")
    s_ps, s_ready, o_ps = tokens("S_ps"), tokens("S_ready"), tokens("O_ps")
    ysq_ready, ms_ready, rs_ready = tokens("ysq_ready"), tokens("head_ms_ready"), tokens("head_rstd_ready")
    ys_ready, yT_ps, yT_ready = tokens("ys_ready"), tokens("yT_ps"), tokens("yT_ready")
    out_ps, out_free = tokens("out_ps"), tokens("out_free")
    V_, SS_ = (6, 3), (6, 0)
    PU_, O_, S_, YT_, OUT_ = (0, 1), (2, 3), (4, 5), (7, 2), (7, 2)
    HALF = TB * P

    def odd(ap, m):
        return ap.rearrange("p (b c) -> p b c", c=2 * m)[:, :, m:2 * m]

    def even(ap, m):
        return ap.rearrange("p (b c) -> p b c", c=2 * m)[:, :, 0:m]

    def packed(ap, m):
        return ap.rearrange("p (b c) -> p b c", c=m)

    def unit(ap, u):
        return ap[:, u * P:(u + 1) * P]

    def rows_of(hd):
        return slice(hd * DH, (hd + 1) * DH)

    def head(ap, q):
        return ap[:, (q % 2) * HALF:(q % 2 + 1) * HALF]

    eye4 = c.ident[:].unsqueeze(1).broadcast_to((P, TB, P))
    eyes = c.ident[:].unsqueeze(1).broadcast_to((P, NU, P))
    units = lambda ap: ap.rearrange("p (u n) -> p u n", u=NU)

    with nc.Block() as block:
        @block.sync
        def _(sp):
            st.issue_loads(sp)
            with sp.Fori(0, TURNS + 1) as i:
                for X in both:
                    sp.wait_ge(w_free[X], 2)
                    sp.sem_clear(w_free[X])
                    sp.dma_start(W[X][:], c.A["e_w"][bass.ds((((i % TURNS) // B) * 2 + X) * P, P), :]).then_inc(w_ready[X], 16)
            for X in both:
                sp.wait_ge(w_free[X], 2)
                sp.sem_clear(w_free[X])

        @block.gpsimd
        def _(g):
            ch = Chain(g, core.lasting_sem("pool_chain"))
            for X in both:
                g.memset(N[X][:], 0.0)
                g.memset(ks[X][:], 0.0)

            def start(i):
                g.wait_ge(hs_free, 1)
                g.sem_clear(hs_free)
                g.tensor_copy(hs[:], c.xT[:, bass.ds((i % B) * L, L)]).then_inc(hs_ready, 1)

            def fresh(X):
                g.wait_ge(al_ready[X], 1)
                g.sem_clear(al_ready[X])
                g.tensor_copy(units(T[X][:]), eyes)

            start(0)
            for X in both:
                fresh(X)
            with g.Fori(0, TURNS) as i:
                ch.reset()
                for l in range(LEVELS):
                    m = 1 << l
                    for X in both:
                        if l == 0:
                            g.wait_ge(kq_ready[X], 1)
                            g.sem_clear(kq_ready[X])
                            g.tensor_copy(even(ks[X][:, 0, :], m), even(k[X][:], m))
                        else:
                            if l >= 2:
                                g.wait_ge(lv_free[X][l % 2], 1)
                                g.sem_clear(lv_free[X][l % 2])
                            g.tensor_tensor(even(ks[X][:, l % 2, :], m), even(k[X][:], m), even(su[X][:], m), ALU.mult)
                        four = lambda ap: ap.rearrange("p (t b c) -> p t b c", t=TB, c=2 * m)[:, :, :, m:2 * m]
                        for n in range(2):
                            r = g.tensor_tensor(kp[X][:, l % 2, :, n, :].rearrange("p t (b c) -> p t b c", c=m),
                                                four(kq[X][:, n, :]), four(pr[X][:]), ALU.mult)
                        ch.link(r)
                        g.sem_inc(lv_ready[X][l % 2], 1)
                        nb = L // (2 * m)
                        tail_odd = odd(pr[X][:], m)[:, :, m - 1:m].broadcast_to((P, nb, m))
                        tail_even = even(pr[X][:], m)[:, :, m - 1:m].broadcast_to((P, nb, m))
                        if l == 0:
                            ch.link(g.memset(su[X][:], 1.0))
                            ch.link(g.tensor_copy(even(su[X][:], m), tail_odd))
                        else:
                            ch.link(g.tensor_tensor(even(su[X][:], m), even(su[X][:], m), tail_odd, ALU.mult))
                        ch.link(g.tensor_tensor(odd(pr[X][:], m), odd(pr[X][:], m), tail_even, ALU.mult))
                for X in both:
                    g.wait_ge(lv_free[X][0], 1)
                    g.sem_clear(lv_free[X][0])
                    g.wait_ge(lv_free[X][1], 1)
                    g.sem_clear(lv_free[X][1])
                    for n in range(2):
                        g.tensor_tensor(kq[X][:, n, :], kq[X][:, n, :], pr[X][:], ALU.mult)
                    g.tensor_copy(tot[X][:], pr[X][:].rearrange("p (t n) -> p t n", t=TB)[:, :, P - 1])
                    g.tensor_tensor(k[X][:], k[X][:], su[X][:], ALU.mult).then_inc(chain_in[X], 1)
                start(i + 1)
                for X in both:
                    g.wait_ge(ms_ready[X], 1)
                    g.sem_clear(ms_ready[X])
                    ch.link(g.tensor_scalar(ms[X][:], ms[X][:], 1.0 / DH, DELTA_EPS, ALU.mult, ALU.add))
                    g.tensor_tensor(ms[X][:], ms[X][:], c.mhalf[:, 0:NU], ALU.pow).then_inc(rs_ready[X], 1)
                for X in both:
                    fresh(X)
            g.wait_ge(hs_free, 1)
            g.sem_clear(hs_free)

        @block.tensor
        def _(pe):
            st.wait_loads(pe)
            pe.sem_inc(hs_free, 1)
            for X in both:
                pe.sem_inc(w_free[X], 1)

            def diagonal(q):
                X, hd = q // 2, q % 2
                for t in range(TB):
                    cols = slice(t * P, (t + 1) * P)
                    r = pe.matmul(c.ps[4 + q][:, cols], k[X][rows_of(hd), cols], kq[X][rows_of(hd), 1, cols],
                                  start=True, stop=True)
                r.then_inc(gr_ps[q], 1)

            def gram(q, l):
                X, hd = q // 2, q % 2
                pe.wait_ge(gr_free[q], 1)
                pe.sem_clear(gr_free[q])
                if hd == 0:
                    pe.wait_ge(lv_ready[X][l % 2], 1)
                    pe.sem_clear(lv_ready[X][l % 2])
                for t in range(TB):
                    r = pe.matmul(c.ps[4 + q][:, t * P:(t + 1) * P], ks[X][rows_of(hd), l % 2, t * P:(t + 1) * P],
                                  kp[X][rows_of(hd), l % 2, t, :, :].rearrange("p n j -> p (n j)"),
                                  start=True, stop=True)
                r.then_inc(gr_ps[q], 1)
                if hd == 1:
                    pe.drain().then_inc(lv_free[X][l % 2], 1)

            def z_step(q, l):
                X = q // 2
                pe.wait_ge(n_ready[q], 1)
                pe.sem_clear(n_ready[q])
                pe.wait_ge(t_ready[q], 1)
                pe.sem_clear(t_ready[q])
                for t in range(TB):
                    u = (q % 2) * TB + t
                    r = pe.matmul(c.ps[q][:, t * P:(t + 1) * P], unit(N[X][:], u), unit(T[X], u), start=True, stop=True)
                r.then_inc(z_ps[q], 1)

            def first_step(q):
                X = q // 2
                pe.wait_ge(n_ready[q], 1)
                pe.sem_clear(n_ready[q])
                for t in range(TB):
                    r = pe.transpose(c.ps[q][:, t * P:(t + 1) * P], unit(Z[X][:, 0, :], (q % 2) * TB + t), c.ident[:])
                r.then_inc(tt_ps[q], 1)

            def tt_step(q, l):
                X = q // 2
                pe.wait_ge(z_ready[q], 1)
                pe.sem_clear(z_ready[q])
                for t in range(TB):
                    u = (q % 2) * TB + t
                    r = pe.matmul(c.ps[q][:, t * P:(t + 1) * P], unit(Z[X][:, l, :], u), unit(TT[X], u), start=True, stop=True)
                r.then_inc(tt_ps[q], 1)

            def t_step(q):
                X = q // 2
                pe.wait_ge(tt_ready[q], 1)
                pe.sem_clear(tt_ready[q])
                for t in range(TB):
                    r = pe.transpose(c.ps[q][:, t * P:(t + 1) * P], unit(TT[X][:], (q % 2) * TB + t), c.ident[:])
                r.then_inc(t_ps[q], 1)

            def project(X):
                pe.wait_ge(w_ready[X], 16)
                pe.sem_clear(w_ready[X])
                for n, bank in enumerate((0, 1, 4, 5)):
                    r = pe.matmul(c.ps[bank][:], W[X][:, n * P:(n + 1) * P], hs[:], start=True, stop=True)
                    if n:
                        r.then_inc((None, qk_ps, a_ps, be_ps)[n][X], 1)
                for t in range(TB):
                    r = pe.matmul(c.ps[V_[X]][:, t * P:(t + 1) * P], hs[:, t * P:(t + 1) * P],
                                  W[X][:, 4 * P:5 * P], start=True, stop=True)
                r.then_inc(v_ps[X], 1)
                pe.drain().then_inc(w_free[X], 1)

            pe.wait_ge(hs_ready, 1)
            pe.sem_clear(hs_ready)
            project(A)
            pe.wait_ge(sq_ready[A], 1)
            pe.sem_clear(sq_ready[A])
            project(Bp)
            pe.sem_inc(hs_free, 1)
            with pe.Fori(0, TURNS) as i:
                for X in both:
                    if X == A:
                        pe.wait_ge(v_read[A], 1)
                        pe.sem_clear(v_read[A])
                    else:
                        pe.wait_ge(sq_ready[Bp], 1)
                        pe.sem_clear(sq_ready[Bp])
                    for n in range(2):
                        for t in range(TB):
                            at = (n * TB + t) * 2
                            r = pe.matmul(c.ps[SS_[X]][:, at:at + 2], sq[X][:, n, t * P:(t + 1) * P], heads2[:],
                                          start=True, stop=True)
                    r.then_inc(ss_ps[X], 1)
                for X in both:
                    pe.wait_ge(rk_ready[X], 1)
                    pe.sem_clear(rk_ready[X])
                    for t in range(TB):
                        r = pe.transpose(c.ps[SS_[X]][:, t * P:(t + 1) * P], sq[X][:, 1, t * P:(t + 1) * P], c.ident[:])
                    r.then_inc(rk_ps[X], 1)
                pe.wait_ge(v_read[Bp], 1)
                pe.sem_clear(v_read[Bp])
                for X in both:
                    pe.wait_ge(out_free[X], 1)
                    pe.sem_clear(out_free[X])
                    pe.wait_ge(kq_pe[X], 1)
                    pe.sem_clear(kq_pe[X])
                    for hd in range(2):
                        diagonal(2 * X + hd)
                for q in range(4):
                    gram(q, 0)
                for q in range(4):
                    first_step(q)
                    gram(q, 1)
                for l in range(1, LEVELS):
                    last = l + 1 == LEVELS
                    for q in range(4):
                        z_step(q, l)
                    for q in range(4):
                        tt_step(q, l)
                        if not last:
                            if q:
                                t_step(q - 1)
                            gram(q, l + 1)
                    if not last:
                        t_step(3)
                for q in range(4):
                    pe.wait_ge(gr_free[q], 1)
                    pe.sem_clear(gr_free[q])
                for X in both:
                    pe.wait_ge(chain_in[X], 1)
                    pe.sem_clear(chain_in[X])
                    for t in range(TB):
                        r = pe.transpose(c.ps[S_[X]][:, t * P:(t + 1) * P], k[X][:, t * P:(t + 1) * P], c.ident[:])
                    r.then_inc(ke_ps[X], 1)
                for q in range(4):
                    pe.wait_ge(tt_ready[q], 1)
                    pe.sem_clear(tt_ready[q])
                for t in range(TB):
                    cols = slice(t * P, (t + 1) * P)
                    if t:
                        for X in both:
                            pe.wait_ge(s_ready[X], 1)
                            pe.sem_clear(s_ready[X])
                            pe.matmul(c.ps[PU_[X]][:, 0:P], kq[X][:, 0, cols], S[X][:], start=True,
                                      stop=True).then_inc(p_ps[X], 1)
                            pe.matmul(c.ps[O_[X]][:, cols], kq[X][:, 1, cols], S[X][:], start=True, stop=False,
                                      skip_group_check=True)
                    for X in both:
                        if t:
                            pe.wait_ge(r_ready[X], 1)
                            pe.sem_clear(r_ready[X])
                        for hd in range(2):
                            r = pe.matmul(c.ps[PU_[X]][:, P + hd * DH:P + (hd + 1) * DH], unit(TT[X], hd * TB + t),
                                          bv[X][:, t, rows_of(hd)], start=True, stop=True)
                        r.then_inc(u_ps[X], 1)
                    for X in both:
                        if t == 0:
                            pe.wait_ge(ket_ready[X], 1)
                            pe.sem_clear(ket_ready[X])
                        pe.wait_ge(u_ready[X], 1)
                        pe.sem_clear(u_ready[X])
                        if t + 1 < TB:
                            pe.matmul(c.ps[S_[X]][:, 0:P], ket[X][:, t, :], U[X][:], start=True, stop=True).then_inc(s_ps[X], 1)
                        for hd in range(2):
                            r = pe.matmul(c.ps[O_[X]][:, t * P + hd * DH:t * P + (hd + 1) * DH], unit(AT[X], hd * TB + t),
                                          U[X][:, rows_of(hd)], start=(t == 0), stop=(t == 0 or hd == 1), skip_group_check=True)
                        if t + 1 == TB:
                            r.then_inc(o_ps[X], 1)
                pe.wait_ge(hs_ready, 1)
                pe.sem_clear(hs_ready)
                project(A)
                for X in both:
                    pe.wait_ge(ys_ready[X], 1)
                    pe.sem_clear(ys_ready[X])
                for X in both:
                    for t in range(TB):
                        r = pe.transpose(c.ps[YT_[X]][:, t * P:(t + 1) * P], ysb[X][:, t, :], c.ident[:])
                    r.then_inc(yT_ps[X], 1)
                pe.wait_ge(sq_ready[A], 1)
                pe.sem_clear(sq_ready[A])
                project(Bp)
                pe.sem_inc(hs_free, 1)
                for X in both:
                    pe.wait_ge(yT_ready[X], 1)
                    pe.sem_clear(yT_ready[X])
                    for t in range(TB):
                        r = pe.matmul(c.ps[OUT_[X]][:, t * P:(t + 1) * P], yT[X][:, t * P:(t + 1) * P],
                                      ow[:, bass.ds((i // B) * 2 + X, 1), :].rearrange("p o d -> p (o d)"), start=True, stop=True)
                    r.then_inc(out_ps[X], 1)
            pe.wait_ge(sq_ready[Bp], 1)
            pe.sem_clear(sq_ready[Bp])
            for X in both:
                pe.wait_ge(out_free[X], 1)
                pe.sem_clear(out_free[X])
                pe.wait_ge(v_read[X], 1)
                pe.sem_clear(v_read[X])

        @block.scalar
        def _(a):
            st.wait_loads(a)
            for X in both:
                a.sem_inc(w_free[X], 1)

            def projected(X):
                a.wait_ge(qk_ps[X], 1)
                a.sem_clear(qk_ps[X])
                a.activation(sq[X], c.psum[:, 0:2, :], ACT.Square)
                a.activation(kq[X][:, 1, :], c.ps[0][:], ACT.Copy)
                a.activation(k[X][:], c.ps[1][:], ACT.Copy)
                a.wait_ge(a_ps[X], 1)
                a.sem_clear(a_ps[X])
                a.activation(pr[X][:], c.ps[4][:], ACT.Sigmoid, bias=W[X][:, 5 * P:5 * P + 1]).then_inc(al_ready[X], 1)
                a.wait_ge(be_ps[X], 1)
                a.sem_clear(be_ps[X])
                a.activation(be[X][:], c.ps[5][:], ACT.Sigmoid,
                             bias=W[X][:, 5 * P + 1:5 * P + 2]).then_inc(sq_ready[X], 1)
                a.drain().then_inc(w_free[X], 1)

            for X in both:
                projected(X)
            with a.Fori(0, TURNS) as i:
                for X in both:
                    a.wait_ge(ss_ps[X], 1)
                    a.sem_clear(ss_ps[X])
                    a.activation(rr[X][:].rearrange("p n u o -> p (n u o)"), c.ps[SS_[X]][:, 0:2 * NU],
                                 ACT.Sqrt).then_inc(rn_ready[X], 1)
                for l in range(1, LEVELS):
                    m = 1 << l
                    for q in range(4):
                        a.wait_ge(z_ps[q], 1)
                        a.sem_clear(z_ps[q])
                        a.activation(even(head(Z[q // 2][:, l, :], q), m), even(c.ps[q][:], m),
                                     ACT.Copy).then_inc(z_ready[q], 1)
                    if l + 1 < LEVELS:
                        for q in range(4):
                            a.wait_ge(t_ps[q], 1)
                            a.sem_clear(t_ps[q])
                            a.activation(even(head(T[q // 2][:], q), m), even(c.ps[q][:], m),
                                         ACT.Copy).then_inc(t_ready[q], 1)
                for X in both:
                    a.wait_ge(ke_ps[X], 1)
                    a.sem_clear(ke_ps[X])
                    a.activation(flat(ket[X]), c.ps[S_[X]][:], ACT.Copy).then_inc(ket_ready[X], 1)
                for t in range(TB):
                    for X in both:
                        a.wait_ge(u_ps[X], 1)
                        a.sem_clear(u_ps[X])
                        a.activation(U[X][:], c.ps[PU_[X]][:, P:2 * P], ACT.Copy).then_inc(u_ready[X], 1)
                for X in both:
                    a.wait_ge(o_ps[X], 1)
                    a.sem_clear(o_ps[X])
                    a.activation(flat(ysq[X]), c.ps[O_[X]][:], ACT.Square).then_inc(ysq_ready[X], 1)
                projected(A)
                for X in both:
                    a.wait_ge(yT_ps[X], 1)
                    a.sem_clear(yT_ps[X])
                    a.activation(yT[X], c.ps[YT_[X]][:], ACT.Identity,
                                 scale=hnw[:, bass.ds((i // B) * 2 + X, 1)]).then_inc(yT_ready[X], 1)
                projected(Bp)

        @block.vector
        def _(v):
            ch = Chain(v, core.lasting_sem("dve_chain"))
            ch.reset()
            for X in both:
                v.sem_inc(out_free[X], 1)
                v.memset(Z[X][:], 0.0)
                v.memset(S[X][:], 0.0)
            st.wait_loads(v)
            ch.link(v.tensor_copy(lowi[:], low[:]))

            def level_in(q, l):
                m = 1 << l
                nb = DH // m
                X = q // 2
                v.wait_ge(gr_ps[q], 1)
                v.sem_clear(gr_ps[q])
                gr = c.ps[4 + q].rearrange("p (t n b c) -> p t n b c", n=2, t=TB, c=m)
                wide = lambda ap: ap.rearrange("p (b c) -> p b c", c=m).unsqueeze(1).broadcast_to((P, TB, nb, m))
                cols = lambda ap: ap.rearrange("p (u b c) -> p u b c", u=TB, c=2 * m)[:, :, :, m:2 * m]
                n_m = N[X][:] if l else Z[X][:, 0, :]
                v.tensor_tensor(cols(head(n_m, q)), gr[:, :, 0], wide(low[:, l, :]), ALU.mult).then_inc(n_ready[q], 1)
                ch.link(v.copy_predicated(cols(head(AT[X][:], q)), wide(lowi[:, l, :]), gr[:, :, 1]))
                v.sem_inc(gr_free[q], 1)

            def tt_out(q, l):
                m = 1 << l
                v.wait_ge(tt_ps[q], 1)
                v.sem_clear(tt_ps[q])
                tt = odd(head(TT[q // 2][:], q), m)
                ch.link(v.tensor_tensor(tt, tt, odd(c.ps[q][:], m), ALU.subtract))
                v.sem_inc(tt_ready[q], 1)

            def values(X, i):
                v.wait_ge(v_ps[X], 1)
                v.sem_clear(v_ps[X])
                beta = flat(c.beta[:, :, :, :].rearrange("p a t h -> p a (t h)"))[
                    :, bass.ds((((i % TURNS) // B) * 2 + X) * 2 * NT + (i % B) * 2 * TB, 2 * TB)]
                v.tensor_tensor(bv[X][:].rearrange("p t (h d) -> p (t h) d", h=2),
                                c.ps[V_[X]].rearrange("p (u d) -> p u d", d=DH),
                                beta.unsqueeze(2).broadcast_to((P, NU, DH)), ALU.mult)
                ch.link(v.tensor_copy(units(TT[X][:]), eyes))
                v.sem_inc(v_read[X], 1)

            for X in both:
                values(X, 0)
            with v.Fori(0, TURNS) as i:
                ch.reset()
                for X in both:
                    v.wait_ge(rn_ready[X], 1)
                    v.sem_clear(rn_ready[X])
                    ch.link(v.tensor_scalar(rr[X][:], rr[X][:], DELTA_EPS, None, ALU.add))
                    ch.link(v.reciprocal(rr[X][:], rr[X][:]))
                    v.tensor_copy(sq[X][:, 1, :].rearrange("p (u d) -> p u d", d=DH),
                                  rr[X][:, 1, :, :].broadcast_to((P, NU, DH))).then_inc(rk_ready[X], 1)
                for X in both:
                    v.wait_ge(rk_ps[X], 1)
                    v.sem_clear(rk_ps[X])
                    ch.link(v.tensor_tensor(k[X][:], k[X][:], c.ps[SS_[X]][:], ALU.mult))
                    ch.link(v.tensor_tensor(kq[X][:, 0, :], k[X][:], be[X][:], ALU.mult))
                    v.sem_inc(kq_ready[X], 1)
                    v.sem_inc(kq_pe[X], 1)
                for X in both:
                    v.tensor_copy(rq[X][:], rr[X][:, 0, :, 0])
                    ch.link(v.tensor_tensor(rq2[X][:], rr[X][:, 0, :, 0], rr[X][:, 0, :, 0], ALU.mult))
                for q in range(4):
                    v.wait_ge(gr_ps[q], 1)
                    v.sem_clear(gr_ps[q])
                    ch.link(v.tensor_tensor(head(AT[q // 2][:], q).rearrange("p (t n) -> p t n", t=TB),
                                            c.ps[4 + q].rearrange("p (t n) -> p t n", t=TB), eye4, ALU.mult))
                    v.sem_inc(gr_free[q], 1)
                for q in range(4):
                    level_in(q, 0)
                for q in range(4):
                    v.wait_ge(tt_ps[q], 1)
                    v.sem_clear(tt_ps[q])
                    t2, tt2 = even(head(T[q // 2][:], q), 1), odd(head(TT[q // 2][:], q), 1)
                    v.tensor_tensor(tt2, tt2, odd(head(Z[q // 2][:, 0, :], q), 1), ALU.subtract)
                    ch.link(v.tensor_tensor(t2, t2, even(c.ps[q][:], 1), ALU.subtract))
                    v.sem_inc(t_ready[q], 1)
                    level_in(q, 1)
                for l in range(1, LEVELS):
                    for q in range(4):
                        tt_out(q, l)
                        if l + 1 < LEVELS:
                            level_in(q, l + 1)
                for t in range(TB):
                    if t:
                        for X in both:
                            v.wait_ge(p_ps[X], 1)
                            v.sem_clear(p_ps[X])
                            v.tensor_tensor(bv[X][:, t, :], bv[X][:, t, :], c.ps[PU_[X]][:, 0:P], ALU.subtract).then_inc(r_ready[X], 1)
                    if t + 1 < TB:
                        for X in both:
                            v.wait_ge(s_ps[X], 1)
                            v.sem_clear(s_ps[X])
                            for hd in range(2):
                                blk = (rows_of(hd), rows_of(hd))
                                ps = c.psum[rows_of(hd), S_[X], rows_of(hd)]
                                if t:
                                    r = v.scalar_tensor_tensor(S[X][blk], S[X][blk], tot[X][rows_of(hd), t:t + 1], ps,
                                                               ALU.mult, ALU.add)
                                else:
                                    r = v.tensor_copy(S[X][blk], ps)
                            ch.link(r)
                            v.sem_inc(s_ready[X], 1)
                for X in both:
                    v.wait_ge(ysq_ready[X], 1)
                    v.sem_clear(ysq_ready[X])
                    ch.link(v.tensor_reduce(ms[X][:], ysq[X][:].rearrange("p t (h d) -> p (t h) d", h=2), AX.X, ALU.add))
                    v.tensor_tensor(ms[X][:], ms[X][:], rq2[X][:], ALU.mult).then_inc(ms_ready[X], 1)
                for X in both:
                    v.wait_ge(rs_ready[X], 1)
                    v.sem_clear(rs_ready[X])
                    ch.link(v.tensor_tensor(ms[X][:], ms[X][:], rq[X][:], ALU.mult))
                    v.tensor_tensor(ysb[X][:].rearrange("p t (h d) -> p (t h) d", h=2),
                                    c.ps[O_[X]].rearrange("p (u d) -> p u d", d=DH),
                                    ms[X][:].unsqueeze(2).broadcast_to((P, NU, DH)), ALU.mult).then_inc(ys_ready[X], 1)
                for X in both:
                    values(X, i + 1)
                for X in both:
                    v.wait_ge(out_ps[X], 1)
                    v.sem_clear(out_ps[X])
                    acc = c.xn[:, bass.ds((i % B) * TB, TB), :]
                    ch.link(v.tensor_tensor(acc, acc, c.ps[OUT_[X]].rearrange("p (t d) -> p t d", t=TB), ALU.add))
                    v.sem_inc(out_free[X], 1)
    st.ctx.close()


FF = 512


def stage_delta_out(core):
    st = Stage(core, "g")
    c, nc, s = core, core.nc, core.sem
    u1, u1b = st.load("u1", [P, RANK]), st.load("u1b", [RANK, 1])
    u2, u2b = st.load("u2", [RANK, D]), st.load("u2b", [P, D])
    w1, w3, w2 = st.load("w1", [P, FF]), st.load("w3", [P, FF]), st.load("w2", [P, FF // P, D])
    gamma = st.load("gamma", [P, 1])
    pre, post = Pre(st, static=True), Post(st)
    norm = Norm(st, "inner", DELTA_EPS, rms=True)
    yk, y2 = st.sb("y", [P, TB, D]), st.sb("y2", [P, TB, D])
    g1, gs = st.sb("g1", [RANK, L]), st.sb("gate", [P, TB, D])
    y2T, sl, hid = st.sb("y2T", [P, L]), st.sb("silu", [P, 2, L]), st.sb("hid", [P, FF // P, L])
    g1_ps, g1_ready, g2_ps = s("g1_ps"), s("g1_ready"), s("g2_ps")
    gs_ready, gate_ready = s("gs_ready"), s("gate_ready")
    y2_ready, y2_ps, y2T_ready = s("y2_ready"), s("y2T_ps"), s("y2T_ready")
    a_ps = [s(f"bank{i}_ready") for i in range(2)]
    b_ps = [s(f"bank{i + 2}_ready") for i in range(2)]
    sl_ready = [s(f"silu{i}_ready") for i in range(2)]
    h_free = [s(f"bank{i}_free") for i in range(2)]
    hid_ready, y_ready, y_free = s("hid_ready"), s("y_ready"), s("y_free")
    with nc.Block() as block:
        @block.sync
        def _(sp):
            st.issue_loads(sp)

        @block.gpsimd
        def _(g):
            ch = Chain(g, core.lasting_sem("pool_chain"))
            ch.reset()
            pre.pool(g, ch, 0)
            with g.Fori(0, B) as b:
                ch.reset()
                norm.pool_rstd(g, ch)
                pre.pool(g, ch, b + 1)
                post.pool(g, ch)

        @block.tensor
        def _(pe):
            st.wait_loads(pe)
            pre.seed_pe(pe)
            pre.pe(pe, 0)
            with pe.Fori(0, B) as b:
                pe.wait_ge(pre.xT_ready, 1)
                pe.sem_clear(pre.xT_ready)
                pe.wait_ge(pre.xTs_ready, 1)
                pe.sem_clear(pre.xTs_ready)
                pe.matmul(c.ps[0][0:RANK, :], u1[:], pre.xTs[:], start=True, stop=True).then_inc(g1_ps, 1)
                pe.drain().then_inc(pre.xTs_free, 1)
                pe.wait_ge(g1_ready, 1)
                pe.sem_clear(g1_ready)
                for t in range(TB):
                    r = pe.matmul(c.ps[1][:, t * P:(t + 1) * P], g1[:, t * P:(t + 1) * P], u2[:], start=True, stop=True)
                r.then_inc(g2_ps, 1)
                pe.wait_ge(y2_ready, 1)
                pe.sem_clear(y2_ready)
                for t in range(TB):
                    r = pe.transpose(c.ps[2][:, t * P:(t + 1) * P], y2[:, t, :], c.ident[:])
                r.then_inc(y2_ps, 1)
                pe.wait_ge(y2T_ready, 1)
                pe.sem_clear(y2T_ready)
                for m in range(FF // P):
                    i = m % 2
                    pe.wait_ge(h_free[i], 1)
                    pe.sem_clear(h_free[i])
                    pe.matmul(c.ps[3 + i][:], w1[:, m * P:(m + 1) * P], y2T[:], start=True, stop=True).then_inc(a_ps[i], 1)
                    pe.matmul(c.ps[5 + i][:], w3[:, m * P:(m + 1) * P], y2T[:], start=True, stop=True).then_inc(b_ps[i], 1)
                pre.pe(pe, b + 1)
                pe.wait_ge(hid_ready, 1)
                pe.sem_clear(hid_ready)
                pe.wait_ge(y_free, 1)
                pe.sem_clear(y_free)
                for t in range(TB):
                    for m in range(FF // P):
                        r = pe.matmul(c.ps[2][:, t * P:(t + 1) * P], hid[:, m, t * P:(t + 1) * P], w2[:, m, :],
                                      start=(m == 0), stop=(m == FF // P - 1))
                r.then_inc(y_ready, 1)
            for i in range(2):
                pe.wait_ge(h_free[i], 1)
                pe.sem_clear(h_free[i])
            pe.wait_ge(y_free, 1)
            pe.sem_clear(y_free)
            pre.drain_pe(pe)
            pe.wait_ge(pre.xTs_ready, 1)
            pe.sem_clear(pre.xTs_ready)

        @block.scalar
        def _(a):
            st.wait_loads(a)
            pre.seed_act(a)
            pre.act(a, 0)
            with a.Fori(0, B) as b:
                a.wait_ge(g1_ps, 1)
                a.sem_clear(g1_ps)
                a.activation(g1[:], c.ps[0][0:RANK, :], ACT.Silu, bias=u1b[:]).then_inc(g1_ready, 1)
                a.wait_ge(gs_ready, 1)
                a.sem_clear(gs_ready)
                a.activation(gs[:], gs[:], ACT.Sigmoid).then_inc(gate_ready, 1)
                a.wait_ge(y2_ps, 1)
                a.sem_clear(y2_ps)
                a.activation(y2T[:], c.ps[2][:], ACT.Copy, scale=gamma[:]).then_inc(y2T_ready, 1)
                for m in range(FF // P):
                    i = m % 2
                    a.wait_ge(a_ps[i], 1)
                    a.sem_clear(a_ps[i])
                    a.activation(sl[:, i, :], c.ps[3 + i][:], ACT.Silu).then_inc(sl_ready[i], 1)
                pre.act(a, b + 1)

        @block.vector
        def _(v):
            ch = Chain(v, core.lasting_sem("dve_chain"))
            ch.reset()
            st.wait_loads(v)
            for i in range(2):
                v.sem_inc(h_free[i], 1)
            v.sem_inc(y_free, 1)
            pre.dve(v, ch, 0)
            with v.Fori(0, B) as b:
                ch.reset()
                v.wait_ge(g2_ps, 1)
                v.sem_clear(g2_ps)
                v.tensor_tensor(gs[:], c.ps[1].rearrange("p (t d) -> p t d", t=TB),
                                u2b[:].unsqueeze(1).broadcast_to((P, TB, D)), ALU.add).then_inc(gs_ready, 1)
                v.wait_ge(gate_ready, 1)
                v.sem_clear(gate_ready)
                ch.link(v.tensor_tensor(gs[:], gs[:], c.xn[:, bass.ds(b * TB, TB), :], ALU.mult))
                ch.link(v.tensor_tensor(yk[:], pre.y1[:], gs[:], ALU.add))
                norm.dve_stats(v, ch, lambda t: yk[:, t, :])
                ch.link(norm.dve_apply(v, lambda t: y2[:, t, :], lambda t: yk[:, t, :]))
                v.sem_inc(y2_ready, 1)
                pre.dve(v, ch, b + 1)
                for m in range(FF // P):
                    i = m % 2
                    v.wait_ge(b_ps[i], 1)
                    v.sem_clear(b_ps[i])
                    v.wait_ge(sl_ready[i], 1)
                    v.sem_clear(sl_ready[i])
                    ch.link(v.tensor_tensor(hid[:, m, :], c.ps[5 + i][:], sl[:, i, :], ALU.mult))
                    v.sem_inc(h_free[i], 1)
                v.sem_inc(hid_ready, 1)
                v.wait_ge(y_ready, 1)
                v.sem_clear(y_ready)
                ch.link(v.tensor_tensor(yk[:], yk[:], c.ps[2].rearrange("p (t d) -> p t d", t=TB), ALU.add))
                v.sem_inc(y_free, 1)
                post.dve_stats(v, ch, lambda t: yk[:, t, :])
                post.dve_add(v, ch, b, lambda t: yk[:, t, :])
            pre.drain_dve(v)
    st.ctx.close()


def stage_attn2(core):
    stage_delta_in(core)
    stage_delta(core)
    stage_delta_out(core)


RUN = {0: stage_attn0, 4: stage_attn2, 1: stage_ffn0, 2: stage_attn1, 6: stage_attn3, 3: stage_moe1, 5: stage_moe2, 7: stage_moe3}


def network(nc, A, out):
    with ExitStack() as ctx:
        core = Core(nc, ctx, A)
        x_loaded, stored = core.lasting_sem("x_loaded"), core.lasting_sem("stored")
        with nc.Block() as block:
            @block.sync
            def _(sp):
                sp.dma_start(core.x[:, 0:NT, :], A["x"].rearrange("(t p) d -> p t d", p=P)).then_inc(x_loaded, 16)
                sp.dma_start(core.ident[:], A["ident"]).then_inc(x_loaded, 16)
                sp.wait_ge(x_loaded, 32)

            @block.gpsimd
            def _(g):
                g.memset(core.x[:, NT:NT + TB, :], 0.0)
                g.memset(core.xn[:], 0.0)
                g.memset(core.mhalf[:], -0.5)
        for n in STAGES:
            RUN[n](core)
        with nc.Block() as block:
            @block.sync
            def _(sp):
                sp.dma_start(out.rearrange("(t p) d -> p t d", p=P), core.x[:, 0:NT, :]).then_inc(stored, 16)
                sp.wait_ge(stored, 16)



def kmajor(w):
    k, n = w.shape
    return w.reshape(k // P, P, n).transpose(1, 0, 2)


def columns(v):
    return v.reshape(-1, P).T


def rows(v):
    return np.broadcast_to(v.reshape(1, -1), (P, v.size))


def layout(I):
    A = {"x": I["L0_attn_x"].reshape(B * L, D), "ident": np.eye(P, dtype=np.float32)}
    f = lambda n: I["L0_attn_" + n]
    seen = np.arange(P)[:, None] - (np.arange(SPAN)[None, :] - WIN)
    A.update(a0_wqk=np.concatenate([f("wq_w").T, f("wk_w").T], 1), a0_wv=f("wv_w").T,
             a0_bqk=rows(np.concatenate([f("wq_b"), f("wk_b")])), a0_bv=rows(f("wv_b")),
             a0_nw=rows(np.stack([f("qn_w"), f("kn_w")])).reshape(P, 2, HD), a0_wo=f("wo_w").T, a0_bo=rows(f("wo_b")),
             a0_headmask=np.repeat(np.eye(H, dtype=np.float32), HD, axis=0),
             a0_window=np.where((seen >= 0) & (seen < WIN), 0.0, NEG).astype(np.float32))

    f = lambda n: I["L0_ffn_" + n]
    A.update(f0_w1=f("w1_w").T, f0_w2=f("w2_w").T, f0_s1=columns(f("w1_s")), f0_s2=columns(f("w2_s")),
             f0_g1=columns(f("h1_s")), f0_g2=columns(f("h2_s")), f0_h1=kmajor(f("h1_w").T),
             f0_h2=kmajor(f("h2_w").T), f0_w3=kmajor(f("w3_w").T), f0_s3=rows(f("w3_s")))

    def quarters(name, w):
        for q in range(QUARTERS):
            A[f"{name}{q}"] = w[q * UQ:(q + 1) * UQ].transpose(1, 0, 2)

    ups = lambda w: w.reshape(w.shape[0], P, -1, P).transpose(0, 2, 1, 3).reshape(UNITS, P, P)
    downs = lambda w: w.reshape(UNITS, P, P)
    w, bias = I["L1_attn_W_qkv"], I["L1_attn_b_qkv"]
    i = np.arange(P)
    A.update(a1_wq=w[0:D].T, a1_wk=w[D:2 * D].T, a1_wv=w[2 * D:].T, a1_bq=columns(bias[0:D]),
             a1_bk=columns(bias[D:2 * D]), a1_bv=rows(bias[2 * D:]),
             a1_causal=np.where(i[None, :] <= i[:, None], 0.0, NEG).astype(np.float32))

    f = lambda n: I["L2_attn_" + n]
    A.update(d_gamma=columns(f("norm_in_w")), d_cw=f("conv_w").reshape(D, KCONV), d_cb=columns(f("conv_b")),
             d_betaw=f("beta_w"), d_betab=rows(f("beta_b")))
    pair = lambda w: w.reshape(w.shape[0], NPAIR, P).transpose(1, 0, 2)
    each = lambda w: np.repeat(w.reshape(-1, 2 * NPAIR), DH, axis=1)
    perchan = lambda v: v.reshape(NPAIR, P, 1)
    A["e_w"] = np.concatenate([pair(f("q_w")), pair(f("k_w")), pair(f("alpha_w")), pair(each(f("beta_w"))),
                               pair(f("v_w")), perchan(f("alpha_b")), perchan(each(f("beta_b")))], 2).reshape(NPAIR * P, WCOLS)
    slot = np.arange(DH)
    masks = []
    for m in (1 << l for l in range(LEVELS)):
        col = slot // m * 2 * m + m + slot % m
        masks.append(np.arange(P)[:, None] // m == col[None, :] // m - 1)
    A.update(e_hnw=columns(f("head_norm_w").reshape(-1)), e_low=np.stack(masks, 1).astype(np.float32), e_ow=f("out_w").reshape(NPAIR, P, D).transpose(1, 0, 2),
             e_heads2=np.kron(np.eye(2), np.ones((DH, 1))).astype(np.float32))
    A.update(g_u1=f("u1_w"), g_u1b=f("u1_b").reshape(RANK, 1), g_u2=f("u2_w"), g_u2b=rows(f("u2_b")),
             g_w1=f("ff_w1"), g_w3=f("ff_w3"), g_w2=kmajor(f("ff_w2")), g_gamma=columns(f("ff_norm_w")))

    f = lambda n: I["L3_attn_" + n]
    up, bup = f("Wup").reshape(LAT, H, 2, HD), f("bup").reshape(H, 2, HD)
    A.update(a3_wq=f("Wq"), a3_bqk=rows(np.stack([f("bq"), bup[:, 0].reshape(D)])).reshape(P, 2, D),
             a3_wd=f("Wdown"), a3_bd=f("bdown").reshape(LAT, 1),
             a3_wkv=up.transpose(0, 2, 1, 3).reshape(LAT, 2 * D), a3_bv=rows(bup[:, 1].reshape(D)),
             a3_wo=f("Wout"), a3_bo=rows(f("bout")))
    inv = (1.0 / 10000.0 ** (np.arange(0, HD, 2, dtype=np.float32) / HD)).astype(np.float32)
    ang = (np.arange(L, dtype=np.float32)[:, None] * inv[None, :]).astype(np.float32)
    tiles = lambda a: a.astype(np.float32).reshape(TB, P, HD).transpose(1, 0, 2)
    A.update(a3_cos=tiles(np.concatenate([np.cos(ang), np.cos(ang)], 1)),
             a3_sin=tiles(np.concatenate([-np.sin(ang), np.sin(ang)], 1)))

    f = lambda n: I["L1_ffn_" + n]
    A.update(m1_gate=f("gate_w").T, m1_gate_b=rows(f("gate_b")), m1_b2=f("b2"), m1_gamma=columns(f("norm_scale")),
             m1_ba=f("b1")[:, 0::2].reshape(UNITS, P).T, m1_bb=f("b1")[:, 1::2].reshape(UNITS, P).T)
    quarters("m1_wa", ups(f("w1")[:, 0::2, :].transpose(0, 2, 1)))
    quarters("m1_wb", ups(f("w1")[:, 1::2, :].transpose(0, 2, 1)))
    quarters("m1_wd", downs(f("w2").transpose(0, 2, 1)))
    f = lambda n: I["L2_ffn_" + n]
    A.update(m2_gate=f("Wg"), m2_gate_b=rows(f("bg")), m2_b2=f("b2"), m2_gamma=columns(f("ln_w")),
             m2_ba=f("b1a").reshape(UNITS, P).T, m2_bb=f("b1b").reshape(UNITS, P).T)
    quarters("m2_wa", ups(f("W1a")))
    quarters("m2_wb", ups(f("W1b")))
    quarters("m2_wd", downs(f("W2")))
    f = lambda n: I["L3_ffn_" + n]
    A.update(m3_gate=f("Wg"), m3_gate_b=np.zeros((P, 8), np.float32), m3_b2=f("b2"), m3_eg=f("gamma").T,
             m3_eb=f("beta").T, m3_ba=f("b1").reshape(UNITS, P).T)
    quarters("m3_wa", ups(f("W1")))
    quarters("m3_wd", downs(f("W2")))
    return A


def kernel(**inputs):
    import concourse.bacc as bacc
    from concourse.bass_utils import run_bass_kernel_spmd

    nc = bacc.Bacc("TRN2", target_bir_lowering=False, num_devices=1)
    arrays = {f"in_{k}": np.ascontiguousarray(a) for k, a in layout({k: np.asarray(a) for k, a in inputs.items()}).items()}
    A = {k[3:]: nc.dram_tensor(k, a.shape, F32, kind="ExternalInput").ap() for k, a in arrays.items()}
    out = nc.dram_tensor("out_0", (B * L, D), F32, kind="ExternalOutput").ap()
    network(nc, A, out)
    r = run_bass_kernel_spmd(nc, [arrays], core_ids=[0])
    return r.results[0]["out_0"].reshape(B, L, D)
```
